# Optimizing a Trainium2 kernel written in Bass

```python
import numpy as np
import jax
import jax.numpy as jnp

def _softmax(x, axis=-1):
    return jax.nn.softmax(x, axis=axis)

def _gelu(x):
    return jax.nn.gelu(x, approximate=True)

def _silu(x):
    return jax.nn.silu(x)

def _sigmoid(x):
    return jax.nn.sigmoid(x)

def _layernorm(x, axis=-1, eps=1e-05):
    m = jnp.mean(x, axis=axis, keepdims=True)
    v = jnp.var(x, axis=axis, keepdims=True)
    return (x - m) / jnp.sqrt(v + eps)

def _scatter_add(tgt, idx, src, axis=0):
    return tgt.at[idx].add(src)

def _segment_sum(src, seg, n):
    return jax.ops.segment_sum(src, seg, n)
kernel_name = 'mk_seq_postln_d1_jaxref_r8_bfee4a'

def setup_inputs(seed: int=0):
    np.random.seed(seed)
    _w = jnp.asarray

    def _L0_attn_setup():
        import jax, jax.numpy as jnp
        import numpy as np
        B, L, D, H = (2, 256, 128, 16)
        C = D // H
        SCALE = 1.0 / np.sqrt(D).astype(np.float32)
        key = jax.random.key(seed)
        ks = jax.random.split(key, 5)
        return {'x': jax.random.normal(ks[0], (B, L, D), dtype=jnp.float32), 'w_qkv': jax.random.normal(ks[1], (3 * D, D), dtype=jnp.float32) * (1.0 / np.sqrt(D)), 'b_qkv': jax.random.normal(ks[2], (3 * D,), dtype=jnp.float32) * 0.02, 'w_o': jax.random.normal(ks[3], (D, D), dtype=jnp.float32) * (1.0 / np.sqrt(D)), 'b_o': jax.random.normal(ks[4], (D,), dtype=jnp.float32) * 0.02}
    _L0_attn_in = _L0_attn_setup()

    def _L0_ffn_setup():
        import jax, jax.numpy as jnp
        import numpy as np
        NUM_EXPERTS = 8
        N_EMBD = 128
        D_FF = 4 * N_EMBD
        B, S = (4, 256)
        key = jax.random.key(seed)
        ks = jax.random.split(key, 6)
        x = jax.random.normal(ks[0], (B, S, N_EMBD), dtype=jnp.float32)
        gate_w = jax.random.normal(ks[1], (N_EMBD, NUM_EXPERTS), dtype=jnp.float32) * 0.02
        w1 = jax.random.normal(ks[2], (NUM_EXPERTS, N_EMBD, D_FF), dtype=jnp.float32) * 0.02
        b1 = jnp.zeros((NUM_EXPERTS, D_FF), dtype=jnp.float32)
        w2 = jax.random.normal(ks[3], (NUM_EXPERTS, D_FF, N_EMBD), dtype=jnp.float32) * 0.02
        b2 = jnp.zeros((NUM_EXPERTS, N_EMBD), dtype=jnp.float32)
        return {'x': x, 'gate_w': gate_w, 'w1': w1, 'b1': b1, 'w2': w2, 'b2': b2}
    _L0_ffn_in = _L0_ffn_setup()
    _d = {'L0_attn_x': _L0_attn_in['x'], 'L0_attn_w_qkv': _L0_attn_in['w_qkv'], 'L0_attn_b_qkv': _L0_attn_in['b_qkv'], 'L0_attn_w_o': _L0_attn_in['w_o'], 'L0_attn_b_o': _L0_attn_in['b_o'], 'L0_ffn_gate_w': _L0_ffn_in['gate_w'], 'L0_ffn_w1': _L0_ffn_in['w1'], 'L0_ffn_b1': _L0_ffn_in['b1'], 'L0_ffn_w2': _L0_ffn_in['w2'], 'L0_ffn_b2': _L0_ffn_in['b2']}
    _x0 = _d['L0_attn_x']
    _d['L0_attn_x'] = jax.random.normal(jax.random.fold_in(jax.random.key(seed), 1), (8, 512, 128), dtype=_x0.dtype)
    del _x0
    return _d

def reference(L0_attn_x, L0_attn_w_qkv, L0_attn_b_qkv, L0_attn_w_o, L0_attn_b_o, L0_ffn_gate_w, L0_ffn_w1, L0_ffn_b1, L0_ffn_w2, L0_ffn_b2):

    def _L0_attn_ref(x, w_qkv, b_qkv, w_o, b_o):
        import jax, jax.numpy as jnp
        import numpy as np
        B, L, D, H = (2, 256, 128, 16)
        C = D // H
        SCALE = 1.0 / np.sqrt(D).astype(np.float32)
        b, l, d = x.shape
        h, c = (H, d // H)
        qkv = jnp.einsum('bld,ed->ble', x, w_qkv) + b_qkv
        q, k, v = jnp.split(qkv, 3, axis=-1)
        q = q.reshape(b, l, h, c)
        k = k.reshape(b, l, h, c)
        v = v.reshape(b, l, h, c)
        attn = jax.nn.softmax(jnp.einsum('blhc,bmhc->bhlm', q, k) * SCALE, axis=-1)
        heads = jnp.einsum('bhlm,bmhc->blhc', attn, v).reshape(b, l, d)
        return jnp.einsum('bld,ed->ble', heads, w_o) + b_o + x

    def _L0_ffn_ref(x, gate_w, w1, b1, w2, b2):
        import jax, jax.numpy as jnp
        import numpy as np
        NUM_EXPERTS = 8
        N_EMBD = 128
        D_FF = 4 * N_EMBD
        B, S = (4, 256)
        Bb, Ss, D = x.shape
        x_flat = x.reshape(-1, D)
        router_logits = x_flat @ gate_w
        router_probs = jax.nn.softmax(router_logits, axis=-1)
        expert_idx = jnp.argmax(router_probs, axis=-1)
        expert_w = jnp.take_along_axis(router_probs, expert_idx[:, None], axis=1)[:, 0]
        out = jnp.zeros_like(x_flat)
        for e in range(NUM_EXPERTS):
            h = jax.nn.gelu(x_flat @ w1[e] + b1[e], approximate=False)
            y = h @ w2[e] + b2[e]
            sel = expert_idx == e
            out = out + jnp.where(sel, expert_w, 0.0)[:, None] * y
        return out.reshape(Bb, Ss, D)
    x = L0_attn_x
    x = _layernorm(x + _L0_attn_ref(x, L0_attn_w_qkv, L0_attn_b_qkv, L0_attn_w_o, L0_attn_b_o), axis=-1)
    x = _layernorm(x + _L0_ffn_ref(x, L0_ffn_gate_w, L0_ffn_w1, L0_ffn_b1, L0_ffn_w2, L0_ffn_b2), axis=-1)
    return x

_drawn_inputs = setup_inputs


def setup_inputs(seed=0):
    import zlib

    import numpy as np

    out = dict(_drawn_inputs(seed))
    spreads = {'L0_ffn_b1': (0.0, 0.8), 'L0_ffn_b2': (0.0, 0.477)}
    factors = {'L0_attn_b_qkv': 4.89,
     'L0_attn_b_o': 5.421,
     'L0_ffn_gate_w': 3.068,
     'L0_ffn_w1': 6.179,
     'L0_ffn_w2': 5.617}
    for name, (base, spread) in spreads.items():
        noise = np.random.default_rng([zlib.crc32(name.encode()), seed]).standard_normal(out[name].shape)
        drawn = base * np.exp(spread * noise) if base else spread * noise
        out[name] = jnp.asarray(drawn.astype(out[name].dtype))
    for name, factor in factors.items():
        out[name] = (out[name] * factor).astype(out[name].dtype)
    return out
```

```python
from contextlib import ExitStack

import concourse.bass as bass
from concourse import mybir

F32 = mybir.dt.float32
BF16 = mybir.dt.bfloat16
U32 = mybir.dt.uint32
I32 = mybir.dt.int32
ALU = mybir.AluOpType
ACT = mybir.ActivationFunctionType
AXIS_X = mybir.AxisListType.X

P = 128
EPS = 1e-5
ONES_BF16 = 0x3F803F80


def build(nc, x, x_t, w_qkv_t, b_qkv, w_o_t, b_o, gate_w, w1, b1, w2, b2, out):
    BATCHES, L, D = x.shape
    HEADS = 16
    CH = D // HEADS
    SCALE = 1.0 / float(D) ** 0.5
    TILES = L // P
    GH = 4
    GROUPS = HEADS // GH
    EXPERTS, _, FF = w1.shape
    FCH = FF // P
    TOKENS = BATCHES * L
    PARTS = 3
    BLOCKS9 = PARTS * PARTS
    ROWS_S = 96
    SHIFT_ROW = 96
    VW = 32
    GR = GH * TILES
    REGION = TOKENS + P
    NBLK = TOKENS // P + EXPERTS
    ROW = D + 2
    SCRATCH_ROWS = EXPERTS * REGION + P * EXPERTS

    ctx = ExitStack()
    with ctx:
        def sb(name, shape, dt=F32):
            return ctx.enter_context(nc.sbuf_tensor(name, shape, dt))

        def psum(name, shape, dt=F32):
            return ctx.enter_context(nc.psum_tensor(name, shape, dt))

        def sem(name):
            return ctx.enter_context(nc.semaphore(name))

        parts_dram = nc.dram_tensor("split_parts", [2, 2, PARTS, CH, HEADS * L], BF16, kind="Internal").ap()
        scratch = nc.dram_tensor("routed_rows", [SCRATCH_ROWS, ROW], F32, kind="Internal").ap()

        wqkv = sb("wqkv", [P, 3 * D])
        bqk = sb("bqk", [P, 2])
        bv = sb("bv", [P, D])
        wo = sb("wo", [P, D])
        bo = sb("bo", [P, D])
        gate = sb("gate", [P, EXPERTS])
        ident = sb("ident", [P, P])
        ident_bf = sb("ident_bf", [P, P], BF16)
        before = sb("before", [P, P])
        ones = sb("ones", [P, P])
        expert_no = sb("expert_no", [P, TILES, EXPERTS])
        token_no = sb("token_no", [P, TOKENS // P], U32)
        minus_half = sb("minus_half", [P, TILES])
        minus_one = sb("minus_one", [P, TILES])
        xt_in = sb("xt_in", [P, 2, L])
        x_in = sb("x_in", [P, 2, TILES, D])
        x2b = sb("x2b", [P, 2, TILES, D])
        qk_rest = sb("qk_rest", [P, 2, L])
        qk_parts = sb("qk_parts", [P, PARTS, 2, L], BF16)
        q_stack = sb("q_stack", [P, 2, HEADS, L], BF16)
        k_stack = sb("k_stack", [P, 2, HEADS, L], BF16)
        v_stack = sb("v_stack", [P, 2, TILES, HEADS, VW])
        probs = sb("probs", [P, 2, GH, TILES, L])
        maxima = sb("maxima", [P, 2, GR])
        shift_rest = sb("shift_rest", [P, GR])
        shift = sb("shift", [P, PARTS, GR], BF16)
        shift_t = sb("shift_t", [PARTS * GR, 2, P], BF16)
        pv_copy = sb("pv_copy", [P, 2, L])
        recip = sb("recip", [P, TILES, GH])
        heads = sb("heads", [P, TILES, D])
        heads_t = sb("heads_t", [P, L])
        resid = sb("resid", [P, TILES, D])
        stats = sb("stats", [P, TILES, 6])
        mean_var = sb("mean_var", [P, TILES, 2])
        var_eps = sb("var_eps", [P, TILES])
        rstd = sb("rstd", [P, TILES])
        rows = sb("rows", [P, 2, TILES, ROW])
        x1_t = sb("x1_t", [P, L])
        logits = sb("logits", [P, TILES, EXPERTS])
        counts = sb("counts", [P, 2, TILES, EXPERTS])
        key = sb("key", [P, TILES, EXPERTS])
        top = sb("top", [P, TILES])
        is_top = sb("is_top", [P, TILES, EXPERTS])
        below = sb("below", [P, TILES, EXPERTS])
        prob = sb("prob", [P, TILES, EXPERTS])
        first = sb("first", [P, TILES])
        one_hot = sb("one_hot", [P, TILES, EXPERTS])
        prob_sum = sb("prob_sum", [P, TILES, EXPERTS // 2])
        base = sb("base", [P, 2, TILES + 1, EXPERTS])
        place = sb("place", [P, TILES, EXPERTS])
        slot = sb("slot", [P, 2, TILES], U32)

        b2_row = sb("b2_row", [1, EXPERTS, D])
        b1_t = sb("b1_t", [P, EXPERTS, FCH])
        pad_rows = sb("pad_rows", [P, ROW])
        block_no = sb("block_no", [1, NBLK, EXPERTS])
        full_at = sb("full_at", [1, EXPERTS, TOKENS // P])
        up_to = sb("up_to", [1, EXPERTS, EXPERTS])
        held = sb("held", [1, EXPERTS])
        begun = sb("begun", [1, EXPERTS, TOKENS // P])
        blocks = sb("blocks", [1, EXPERTS])
        upto_blocks = sb("upto_blocks", [1, EXPERTS, EXPERTS])
        last_block = sb("last_block", [1, EXPERTS])
        passed = sb("passed", [1, NBLK, EXPERTS])
        hole = sb("hole", [1, EXPERTS])
        holes = sb("holes", [1, NBLK, EXPERTS])
        sums = sb("sums", [1, 2, NBLK])
        expert_of = sb("expert_of", [1, NBLK], I32)
        row_of = sb("row_of", [1, NBLK], I32)
        region_end = sb("region_end", [1, EXPERTS], I32)
        sq_mean_var = sb("sq_mean_var", [P, 2, 2])
        sq_stats = sb("sq_stats", [P, 2, 6])
        sq_rstd = sb("sq_rstd", [P, 2])
        sq_var = sb("sq_var", [P, 2])

        s_bank = [psum(f"s_bank{i}", [P, L]) for i in range(3)]
        st_bank = [psum(f"st_bank{i}", [P, L]) for i in range(3)]
        pv_bank = psum("pv_bank", [P, L])
        misc = psum("misc", [P, 512])

        consts_loaded = sem("consts_loaded")
        consts_built = sem("consts_built")
        register_waited = sem("register_waited")
        stacks_cleared = sem("stacks_cleared")
        stacks1_cleared = sem("stacks1_cleared")
        base_ready = sem("base_ready")
        ones_col = sem("ones_col")
        x_loaded = sem("x_loaded")
        xt_loaded = sem("xt_loaded")
        qk_hi = sem("qk_hi")
        rest_ready = sem("rest_ready")
        mid_ready = sem("mid_ready")
        lo_ready = sem("lo_ready")
        x2b_ready = sem("x2b_ready")
        s_filled = sem("s_filled")
        s_reduced = sem("s_reduced")
        shift_step = sem("shift_step")
        shift_loaded = sem("shift_loaded")
        st_filled = sem("st_filled")
        exp_done = sem("exp_done")
        pv_done = sem("pv_done")
        pv_copied = sem("pv_copied")
        recip_ready = sem("recip_ready")
        stats_ready = sem("stats_ready")
        aggr_ready = sem("aggr_ready")
        vareps_ready = sem("vareps_ready")
        rstd_ready = sem("rstd_ready")
        x1_ready = sem("x1_ready")
        top_ready = sem("top_ready")
        below_ready = sem("below_ready")
        istop_ready = sem("istop_ready")
        key_ready = sem("key_ready")
        first_ready = sem("first_ready")
        onehot_ready = sem("onehot_ready")
        prob_ready = sem("prob_ready")
        psum_ready = sem("psum_ready")
        weight_ready = sem("weight_ready")
        based = sem("based")
        place_step = sem("place_step")
        slot_ready = sem("slot_ready")
        id_ready = sem("id_ready")
        misc_filled = sem("misc_filled")
        misc_emptied = sem("misc_emptied")

        scattered = [sem(f"scattered{i}") for i in range(2)]
        parts_stored = [sem(f"parts_stored{i}") for i in range(PARTS)]

        stack_loaded = [sem(f"stack_loaded{i}") for i in range(2)]
        LOADS = [(1, 1, PARTS * k, 0, PARTS) for k in range(PARTS)]
        for k in range(PARTS):
            LOADS.append((0, 0, PARTS * k, k, PARTS - k))
            if k:
                LOADS.append((0, 0, PARTS * k + PARTS - k, 0, k))

        w1_all = q_stack[:, 0, :, :].rearrange("p h l -> p (h l)").bitcast(F32).rearrange(
            "p (e f) -> p e f", e=EXPERTS)
        w2_all = k_stack[:, 0, :, :].rearrange("p h l -> p (h l)").bitcast(F32).rearrange(
            "p (e c d) -> p e c d", e=EXPERTS, c=FCH)
        pool_of = probs[:, :, :, :, :].rearrange("p a g t l -> p (a g t l)")
        NX = 8
        widths = {"block_rows": NX * ROW, "block_t": 2 * P, "w1_now": 2 * FF, "hidden_t": 2 * FF,
                  "b1_now": 2 * FCH, "z_now": 2 * D, "out_rows": 2 * D}
        starts, begin = {}, 0
        for name, width in widths.items():
            starts[name] = begin
            begin += width

        def over_probs(name, count):
            return pool_of[:, starts[name]:starts[name] + widths[name]].rearrange("p (a x) -> p a x", a=count)

        block_rows, block_t = over_probs("block_rows", NX), over_probs("block_t", 2)
        w1_now, b1_now, hidden_t = over_probs("w1_now", 2), over_probs("b1_now", 2), over_probs("hidden_t", 2)
        z_now, out_rows = over_probs("z_now", 2), over_probs("out_rows", 2)
        turn_bank, hidden_bank, y_bank = st_bank[0:2], s_bank[0:2], [s_bank[2], st_bank[2]]
        out_flat = out.rearrange("b l d -> (b l) d")

        experts_loaded = sem("experts_loaded")
        tables_built = sem("tables_built")
        plan_step = sem("plan_step")
        padded = sem("padded")
        rows_loaded = [sem(f"rows_loaded{i}") for i in range(NX)]
        turned = sem("turned")
        turn_copied = sem("turn_copied")
        w1_copied = sem("w1_copied")
        b1_copied = sem("b1_copied")
        hidden_filled = sem("hidden_filled")
        gelu_done = sem("gelu_done")
        y_filled = sem("y_filled")
        z_ready = sem("z_ready")
        z_stats = sem("z_stats")
        z_aggr = sem("z_aggr")
        z_var = sem("z_var")
        z_rstd = sem("z_rstd")
        out_ready = sem("out_ready")
        out_stored = [sem(f"out_stored{i}") for i in range(2)]

        LAG = 3

        def run_steps(eng, first, step):
            for k in range(first):
                step(0, k)
            turns = (NBLK - 1 - first) // NX
            with eng.Fori(0, turns) as i:
                for r in range(NX):
                    step(i, first + r)
            for k in range(first + turns * NX, NBLK + LAG):
                step(0, k)

        def block_at(i, m, lag):
            number = i * NX + m - lag
            if isinstance(number, int) and not 0 <= number < NBLK:
                return None
            return number, (m - lag) % NX, i + (m - lag) // NX

        ORDER = [("q", 0, 0), ("k", 0, 1), ("sh", 0, 2), ("U", 0, 3),
                 ("U", 1, 0), ("sh", 1, 1), ("headsT", 1, 2), ("proj", 1, 3),
                 ("U", 2, 0), ("sh", 2, 1), ("v", 2, 2), ("x1T", 2, 3),
                 ("logits", 3, 0), ("sh", 3, 1), ("U", 3, 2), ("counts", 3, 3)]
        OLD = ("headsT", "proj", "x1T", "logits", "counts")

        CONSTS = 7
        TABLES = 5
        PLAN_STEPS = 13
        LOOPED = 3
        HALVINGS = 3
        PLACE_STEPS = 2 + HALVINGS

        def present(kind, n, b):
            if isinstance(b, int):
                if b == 0:
                    return kind not in OLD and not (kind == "U" and n < 2)
                if b == BATCHES - 1:
                    return kind not in ("q", "k", "v") and not (kind == "sh" and n == GROUPS - 1)
                if b == BATCHES:
                    return kind in OLD or (kind == "U" and n < 2)
            return True

        START = ["q", "k", "v", "sh"]
        uses0 = sum(present(k, n, 0) for k, n, _ in ORDER)
        uses7 = sum(present(k, n, BATCHES - 1) for k, n, _ in ORDER)

        def misc_before(kind, n, b):
            at = sum(present(k, m, b) for k, m, s in ORDER[:[(k, m) for k, m, _ in ORDER].index((kind, n))])
            if isinstance(b, int) and b == 0:
                return len(START) + at
            if isinstance(b, int) and b == BATCHES:
                return len(START) + uses0 + len(ORDER) * (BATCHES - 2) + uses7 + at
            return len(START) + uses0 + len(ORDER) * (b - 1) + at

        def emptied(kind, n, b):
            return misc_before(kind, n, b) + 1

        def slot_of(n, s, b):
            for kind, m, t in ORDER:
                if (m, t) == (n, s) and present(kind, m, b):
                    return kind
            return None

        def run_batches(eng, body, tail):
            for b in range(LOOPED):
                body(b, b % 2, max(b - 1, 0) // 2)
            with eng.Fori((LOOPED - 1) // 2, (BATCHES - 2) // 2) as i:
                body(i * 2 + 1, 1, i)
                body(i * 2 + 2, 0, i)
            body(BATCHES - 1, 1, (BATCHES - 2) // 2)
            tail()

        def is_last(b):
            return isinstance(b, int) and b == BATCHES - 1

        def is_first(b):
            return isinstance(b, int) and b == 0

        def ahead(b, par, n, k):
            m = n + k
            if is_last(b) and m >= GROUPS:
                return None
            return (b + 1, 1 - par, m - GROUPS) if m >= GROUPS else (b, par, m)

        def behind(b, par, n, k):
            m = n - k
            if is_first(b) and m < 0:
                return None
            return (b - 1, 1 - par, m + GROUPS) if m < 0 else (b, par, m)

        def bank_of(banks, j, i):
            at = j * TILES + i
            return banks[1 if at == GR - 1 else at % 3], {0: 4, 1: 2, 2: 4, GR - 1: 2}.get(at, 3)

        q32, k32 = q_stack[:, :, :, :].bitcast(U32), k_stack[:, :, :, :].bitcast(U32)
        misc_h = misc[:, 0:TILES * P].rearrange("p (t g w) -> p t g w", t=TILES, g=GH)
        misc_bf = misc[:, 0:P].bitcast(BF16)
        misc_v = misc[:, 0:TILES * D].rearrange("p (t h c) -> p t h c", t=TILES, c=CH)
        misc_td = misc[:, 0:TILES * D].rearrange("p (t d) -> p t d", t=TILES)
        misc_counts = misc[:, 0:2 * 64].rearrange("p (a x) -> p a x", a=2)[:, :, 0:TILES * EXPERTS].rearrange(
            "p a (t e) -> p a t e", t=TILES)
        misc_lg = misc[:, 0:TILES * EXPERTS].rearrange("p (t e) -> p t e", t=TILES)

        def stand_apart(eng):
            eng.sem_inc(register_waited, 1)

        block = ctx.enter_context(nc.Block())

        @block.sync
        def _(sp):
            def load_x(b, par):
                sp.dma_start(xt_in[:, par, :], x_t[b]).then_inc(xt_loaded, 16)
                sp.dma_start(x_in[:, par], x[b].rearrange("(t p) d -> p t d", p=P)).then_inc(x_loaded, 16)

            def fill_stacks(b, par, read):
                for part, ready in enumerate((qk_hi, mid_ready, lo_ready)):
                    sp.wait_ge(ready, b * 2 + 2)
                    sp.dma_start(parts_dram[par, :, part].rearrange("s c (h l) -> (c h) s l", l=L),
                                 qk_parts[:, part]).then_inc(parts_stored[part], 16)
                for part in range(PARTS):
                    sp.wait_ge(parts_stored[part], (b + 1) * 16)
                sp.wait_ge(st_filled, read)
                stand_apart(sp)
                for half in range(2):
                    heads_of = slice(half * HEADS // 2, (half + 1) * HEADS // 2)
                    for stack, side, at, part, count in LOADS:
                        sp.dma_start(
                            (q_stack, k_stack)[stack][CH * at:CH * (at + count), par, heads_of].rearrange(
                                "c h l -> c (h l)"),
                            parts_dram[par, side, part:part + count].rearrange("a c h -> (a c) h")[
                                :, half * HEADS // 2 * L:(half + 1) * HEADS // 2 * L],
                            max_dma_last_dim=2048).then_inc(stack_loaded[half], 16)

            sp.dma_start(wqkv[:, :], w_qkv_t).then_inc(consts_loaded, 16)
            load_x(0, 0)
            sp.dma_start(bqk[:, :], b_qkv[0:2 * D].rearrange("(a p) -> p a", p=P),
                         allow_slow_non_contiguous=True).then_inc(consts_loaded, 16)
            sp.dma_start(bv[:, :], b_qkv[2 * D:3 * D].rearrange("(a d) -> a d", a=1).broadcast_to([P, D])
                         ).then_inc(consts_loaded, 16)
            sp.dma_start(wo[:, :], w_o_t).then_inc(consts_loaded, 16)
            sp.dma_start(bo[:, :], b_o.rearrange("(a d) -> a d", a=1).broadcast_to([P, D])
                         ).then_inc(consts_loaded, 16)
            sp.dma_start(gate[:, :], gate_w).then_inc(consts_loaded, 16)
            sp.wait_ge(stacks_cleared, 2)
            fill_stacks(0, 0, 0)
            sp.dma_start(b2_row[:, :, :], b2.rearrange("(a e) d -> a e d", a=1)).then_inc(experts_loaded, 16)
            sp.dma_start(b1_t[:, :, :], b1.rearrange("e (c p) -> p e c", p=P), allow_slow_non_contiguous=True
                         ).then_inc(experts_loaded, 16)

            def batch(b, par, pairs):
                if not is_last(b):
                    if not is_first(b):
                        sp.wait_ge(st_filled, b * (GROUPS * GR) - GR)
                        stand_apart(sp)
                        sp.wait_ge(x2b_ready, b * 2)
                    load_x(b + 1, 1 - par)
                    if is_first(b):
                        sp.wait_ge(stacks1_cleared, 2)
                    else:
                        for half in range(2):
                            sp.wait_ge(stack_loaded[half], b * (len(LOADS) * 16))
                    fill_stacks(b + 1, 1 - par, b * (GROUPS * GR))

            def tail():
                sp.wait_ge(st_filled, (BATCHES - 1) * GROUPS * GR)
                sp.dma_start(w1_all, w1.rearrange("e d f -> d e f")).then_inc(experts_loaded, 16)
                sp.dma_start(w2_all, w2.rearrange("e (c f) d -> f e c d", f=P)).then_inc(experts_loaded, 16)
                sp.wait_ge(tables_built, TABLES)
                sp.dma_start(scratch[EXPERTS * REGION:SCRATCH_ROWS].rearrange("(a p) r -> p a r", p=P),
                             pad_rows[:, :].rearrange("p (a r) -> p a r", a=1).broadcast_to([P, EXPERTS, ROW])
                             ).then_inc(padded, 16)
                sp.wait_ge(plan_step, 1)
                for e in range(EXPERTS):
                    end = sp.value_load(region_end[0:1, e:e + 1], min_val=0, max_val=EXPERTS * REGION)
                    sp.dma_start(scratch[bass.ds(end, P), :], pad_rows[:, :]).then_inc(padded, 16)
                for par in range(2):
                    sp.wait_ge(scattered[par], BATCHES // 2 * TILES * 16)
                sp.wait_ge(padded, (EXPERTS + 1) * 16)
                sp.wait_ge(plan_step, PLAN_STEPS)
                sp.wait_ge(pv_done, BATCHES * GROUPS)

                def step(q, r):
                    if block_at(q, r, 0) is None:
                        return
                    k, buf, turn = block_at(q, r, 0)
                    if not (isinstance(k, int) and k < NX):
                        sp.wait_ge(out_stored[buf % 2], ((turn - 1) * (NX // 2) + buf // 2 + 1) * 16)
                    row = sp.value_load(row_of[0:1, k:k + 1] if isinstance(k, int) else row_of[0:1, bass.ds(k, 1)],
                                        min_val=0, max_val=SCRATCH_ROWS - P)
                    sp.dma_start(block_rows[:, buf], scratch[bass.ds(row, P), :]).then_inc(rows_loaded[buf], 16)

                run_steps(sp, NX, step)

            run_batches(sp, batch, tail)

        @block.tensor
        def _(pe):
            def fill_misc(index):
                pe.wait_ge(misc_emptied, index)

            def project_qk(side, par):
                nc.tensor.matmul(misc[:, 0:L], wqkv[:, side * D:(side + 1) * D], xt_in[:, par, :],
                                 start=True, stop=True).then_inc(misc_filled, 1)

            def project_v(par):
                for t in range(TILES):
                    mm = nc.tensor.matmul(misc[:, t * D:(t + 1) * D], xt_in[:, par, t * P:(t + 1) * P],
                                          wqkv[:, 2 * D:3 * D], start=True, stop=True)
                mm.then_inc(misc_filled, 1)

            def turn_shift():
                nc.tensor.transpose(misc_bf[0:PARTS * GR, 0:P],
                                    shift[:, :, :].rearrange("p a g -> p (a g)"),
                                    ident_bf[:, :]).then_inc(misc_filled, 1)

            def scores(b, par, n, j, i):
                h = n * GH + j
                number = (b * GROUPS + n) * GR + j * TILES + i
                bank, last = bank_of(s_bank, j, i)
                if not (isinstance(number, int) and number < last):
                    pe.wait_ge(s_reduced, number - last + 1)
                nc.tensor.matmul(bank[:, :], q_stack[0:ROWS_S, par, h, i * P:(i + 1) * P],
                                 k_stack[0:ROWS_S, par, h, :], start=True, stop=True).then_inc(s_filled, 1)

            def scores_t(b, par, n, j, i):
                h = n * GH + j
                number = (b * GROUPS + n) * GR + j * TILES + i
                bank, last = bank_of(st_bank, j, i)
                if not (isinstance(number, int) and number < last):
                    pe.wait_ge(exp_done, number - last + 1)
                nc.tensor.matmul(bank[:, :], k_stack[:, par, h, i * P:(i + 1) * P],
                                 q_stack[:, par, h, :], start=True, stop=True).then_inc(st_filled, 1)

            def probs_v(b, par, n, i, buf):
                for j in range(GH):
                    mm = nc.tensor.matmul(pv_bank[VW * j:VW * (j + 1), :], v_stack[:, par, i, n * GH + j, :],
                                          probs[:, buf, j, i, :], start=(i == 0), stop=(i == TILES - 1))
                if i == TILES - 1:
                    mm.then_inc(pv_done, 1)

            def misc_work(kind, b, par, n):
                if kind is None:
                    return
                fill_misc(misc_before(kind, n, b))
                if kind == "U":
                    g = behind(b, par, n, 2) if not (isinstance(b, int) and b == BATCHES) else (b - 1, 1 - par, n + 2)
                    pe.wait_ge(pv_copied, g[0] * GROUPS + g[2] + 1)
                    for t in range(TILES):
                        mm = nc.tensor.transpose(misc[:, t * P:(t + 1) * P],
                                                 pv_copy[:, g[2] % 2, t * P:(t + 1) * P], ident[:, :])
                    mm.then_inc(misc_filled, 1)
                elif kind == "sh":
                    pe.wait_ge(shift_step, (b * GROUPS + n + 2) * 4)
                    stand_apart(pe)
                    turn_shift()
                elif kind in ("q", "k"):
                    if kind == "q":
                        pe.wait_ge(xt_loaded, (b + 2) * 16)
                    project_qk(int(kind == "k"), 1 - par)
                elif kind == "v":
                    project_v(1 - par)
                elif kind == "headsT":
                    for t in range(TILES):
                        mm = nc.tensor.transpose(misc[:, t * P:(t + 1) * P], heads[:, t, :], ident[:, :])
                    mm.then_inc(misc_filled, 1)
                elif kind == "proj":
                    for t in range(TILES):
                        mm = nc.tensor.matmul(misc[:, t * D:(t + 1) * D], heads_t[:, t * P:(t + 1) * P],
                                              wo[:, :], start=True, stop=True)
                    mm.then_inc(misc_filled, 1)
                elif kind == "x1T":
                    pe.wait_ge(x1_ready, b * TILES)
                    for t in range(TILES):
                        mm = nc.tensor.transpose(misc[:, t * P:(t + 1) * P], rows[:, 1 - par, t, 0:D], ident[:, :])
                    mm.then_inc(misc_filled, 1)
                elif kind == "logits":
                    for t in range(TILES):
                        mm = nc.tensor.matmul(misc[:, t * EXPERTS:(t + 1) * EXPERTS],
                                              x1_t[:, t * P:(t + 1) * P], gate[:, :], start=True, stop=True)
                    mm.then_inc(misc_filled, 1)
                elif kind == "counts":
                    pe.wait_ge(onehot_ready, b)
                    oh = one_hot[:, :, :].rearrange("p t e -> p (t e)")
                    nc.tensor.matmul(misc[:, 0:TILES * EXPERTS], before[:, :], oh, start=True, stop=True)
                    nc.tensor.matmul(misc[:, 64:64 + TILES * EXPERTS], ones[:, :], oh,
                                     start=True, stop=True).then_inc(misc_filled, 1)

            pe.wait_ge(xt_loaded, 16)
            pe.wait_ge(consts_loaded, 6 * 16)
            project_qk(0, 0)
            fill_misc(1)
            project_qk(1, 0)
            fill_misc(2)
            project_v(0)
            for half in range(2):
                pe.wait_ge(stack_loaded[half], len(LOADS) * 16)
            pe.wait_ge(consts_built, CONSTS)
            for n in range(2):
                for j in range(GH):
                    for i in range(TILES):
                        scores(0, 0, n, j, i)
                if n == 0:
                    fill_misc(3)
                    pe.wait_ge(shift_step, 4)
                    turn_shift()
            scores(0, 0, 2, 0, 0)

            def batch(b, par, pairs):
                for n in range(GROUPS):
                    maxing, multiplying = ahead(b, par, n, 2), behind(b, par, n, 1)
                    pe.wait_ge(shift_loaded, (b * GROUPS + n + 1) * (PARTS * 16))
                    for j in range(GH):
                        for i in range(TILES):
                            scores_t(b, par, n, j, i)
                            if maxing and i < TILES - 1:
                                scores(*maxing, j, i + 1)
                            if i == 1:
                                misc_work(slot_of(n, j, b), b, par, n)
                        following = maxing if j < GH - 1 else ahead(b, par, n, 3)
                        if following:
                            if j == GH - 1 and n % 2 == 1:
                                half = n // 2
                                pe.wait_ge(stack_loaded[half], (b + 2) * (len(LOADS) * 16))
                            scores(*following, (j + 1) % GH, 0)
                        if multiplying:
                            if j == 0:
                                pe.wait_ge(exp_done, (b * GROUPS + n) * GR)
                                if behind(b, par, n, 2):
                                    pe.wait_ge(pv_copied, b * GROUPS + n - 1)
                            probs_v(*multiplying, j, (n - 1) % 2)

            def tail():
                b = BATCHES
                pe.wait_ge(exp_done, b * GROUPS * GR)
                pe.wait_ge(pv_copied, b * GROUPS - 1)
                for i in range(TILES):
                    probs_v(b - 1, 1, GROUPS - 1, i, (GROUPS - 1) % 2)
                for kind, n, _ in ORDER:
                    if present(kind, n, b):
                        misc_work(kind, b, 0, n)

                def step(q, r):
                    if block_at(q, r, 2):
                        k, _, _ = block_at(q, r, 2)
                        par = r % 2
                        if isinstance(k, int) and k == 0:
                            pe.wait_ge(experts_loaded, 4 * 16)
                        e = pe.value_load(expert_of[0:1, k:k + 1] if isinstance(k, int)
                                          else expert_of[0:1, bass.ds(k, 1)], min_val=0, max_val=EXPERTS - 1)
                        pe.wait_ge(gelu_done, k + 1)
                        if not (isinstance(k, int) and k < 2):
                            pe.wait_ge(z_ready, k - 1)
                        nc.tensor.matmul(y_bank[par][:, 0:D], ones[0:1, :],
                                         b2_row[:, bass.ds(e, 1), :].rearrange("p a d -> p (a d)"),
                                         start=True, stop=False)
                        for c in range(FCH):
                            mm = nc.tensor.matmul(y_bank[par][:, 0:D], hidden_t[:, par, c * P:(c + 1) * P],
                                                  w2_all[:, bass.ds(e, 1), c, :].rearrange("p a d -> p (a d)"),
                                                  start=False, stop=(c == FCH - 1))
                        mm.then_inc(y_filled, 1)
                    for at in ([block_at(q, r, 0)] if isinstance(q, int) and q * NX + r == 0 else []) + [
                            block_at(q, r, -1)]:
                        if at is None:
                            continue
                        k, buf, turn = at
                        pe.wait_ge(rows_loaded[buf], (turn + 1) * 16)
                        if not (isinstance(k, int) and k < 2):
                            pe.wait_ge(turn_copied, k - 1)
                        nc.tensor.transpose(turn_bank[buf % 2][:, 0:P], block_rows[:, buf, 0:D], ident[:, :]
                                            ).then_inc(turned, 1)
                    if block_at(q, r, 0):
                        k, buf, _ = block_at(q, r, 0)
                        par = r % 2
                        pe.wait_ge(turn_copied, k + 1)
                        pe.wait_ge(w1_copied, k + 1)
                        if not (isinstance(k, int) and k < 2):
                            pe.wait_ge(gelu_done, k - 1)
                        for c in range(FCH):
                            mm = nc.tensor.matmul(hidden_bank[par][:, c * P:(c + 1) * P],
                                                  w1_now[:, par, c * P:(c + 1) * P], block_t[:, par, :],
                                                  start=True, stop=True)
                        mm.then_inc(hidden_filled, 1)

                pe.wait_ge(plan_step, PLAN_STEPS)
                pe.wait_ge(exp_done, BATCHES * GROUPS * GR)
                pe.wait_ge(s_reduced, BATCHES * GROUPS * GR)
                run_steps(pe, LAG + 2, step)

            run_batches(pe, batch, tail)

        @block.scalar
        def _(act):
            def lead(b, side):
                act.wait_ge(misc_emptied, side + 1 if is_first(b) else emptied("qk"[side], 0, b - 1))
                if not is_first(b):
                    for part in range(PARTS):
                        act.wait_ge(parts_stored[part], b * 16)
                nc.scalar.activation(qk_parts[:, 0, side, :], qk_rest[:, side, :], ACT.Copy).then_inc(qk_hi, 1)

            def middle(b, side):
                act.wait_ge(rest_ready, b * 2 + side + 1)
                nc.scalar.activation(qk_parts[:, 1, side, :], qk_rest[:, side, :], ACT.Copy).then_inc(mid_ready, 1)

            def copy_shift(g, index):
                b, par, n = g
                number = b * GROUPS + n
                act.wait_ge(misc_filled, index + 1)
                if not (is_first(b) and n < 2):
                    act.wait_ge(shift_loaded, (number - 1) * (PARTS * 16))
                nc.scalar.activation(shift_t[:, n % 2, :], misc_bf[0:PARTS * GR, 0:P], ACT.Copy
                                     ).then_inc(misc_emptied, 1)

            def load_shift(g, index):
                b, par, n = g
                act.wait_ge(misc_emptied, index + 1)
                for a in range(PARTS):
                    act.dma_start(
                        q_stack[SHIFT_ROW + a:SHIFT_ROW + a + 1, par, n * GH:(n + 1) * GH, :].rearrange(
                            "a h (t l) -> a (h t) l", t=TILES),
                        shift_t[a * GR:(a + 1) * GR, n % 2, :]).then_inc(shift_loaded, 16)

            def copy_pv(g):
                b, par, n = g
                act.wait_ge(pv_done, b * GROUPS + n + 1)
                nc.scalar.activation(pv_copy[:, n % 2, :], pv_bank[:, :], ACT.Copy).then_inc(pv_copied, 1)

            def exps(b, par, n, j, i):
                number = (b * GROUPS + n) * GR + j * TILES + i
                act.wait_ge(st_filled, number + 1)
                if j == 0 and i == 0 and behind(b, par, n, 2):
                    act.wait_ge(pv_done, b * GROUPS + n - 1)
                nc.scalar.activation(probs[:, n % 2, j, i, :], bank_of(st_bank, j, i)[0][:, :],
                                     ACT.Exp, scale=SCALE).then_inc(exp_done, 1)

            def misc_copy(kind, b, par, n):
                if kind not in ("sh", "headsT", "x1T", "logits", "counts"):
                    return
                index = misc_before(kind, n, b)
                if kind == "sh":
                    copy_shift(ahead(b, par, n, 1), index)
                else:
                    target, source = {
                        "headsT": (heads_t[:, :], misc[:, 0:L]),
                        "x1T": (x1_t[:, :], misc[:, 0:L]),
                        "logits": (logits[:, :, :], misc_lg),
                        "counts": (counts[:, :, :, :], misc_counts)}[kind]
                    act.wait_ge(misc_filled, index + 1)
                    if kind == "logits" and not (isinstance(b, int) and b == 1):
                        act.wait_ge(below_ready, b - 1)
                    if kind == "counts" and not (isinstance(b, int) and b == 1):
                        act.wait_ge(place_step, (b - 1) * PLACE_STEPS)
                    nc.scalar.activation(target, source, ACT.Copy).then_inc(misc_emptied, 1)

            def router_exp(b):
                act.wait_ge(below_ready, b)
                if not (isinstance(b, int) and b == 1):
                    act.wait_ge(psum_ready, (b - 1) * HALVINGS)
                nc.scalar.activation(prob[:, :, :], below[:, :, :], ACT.Exp).then_inc(prob_ready, 1)

            act.wait_ge(consts_loaded, 6 * 16)
            for side in range(2):
                lead(0, side)
            for side in range(2):
                middle(0, side)
            act.wait_ge(stacks_cleared, 2)
            copy_shift((0, 0, 0), 3)
            load_shift((0, 0, 0), 3)

            def batch(b, par, pairs):
                for n in range(GROUPS):
                    if behind(b, par, n, 2):
                        copy_pv(behind(b, par, n, 2))
                    for j in range(GH):
                        for i in range(TILES):
                            exps(b, par, n, j, i)
                            at = (n, j, i)
                            if not is_last(b):
                                if at in ((0, 1, 0), (0, 2, 0)):
                                    lead(b + 1, j - 1)
                                elif at in ((0, 2, 1), (0, 3, 0)):
                                    middle(b + 1, j - 2)
                            if at == (3, 2, 3) and not is_first(b):
                                router_exp(b)
                            if i == 0 and j > 0 and slot_of(n, j - 1, b) == "sh":
                                load_shift(ahead(b, par, n, 1), misc_before("sh", n, b))
                        misc_copy(slot_of(n, j, b), b, par, n)

            def tail():
                b = BATCHES
                copy_pv((b - 1, 1, GROUPS - 2))
                copy_pv((b - 1, 1, GROUPS - 1))
                for kind, n, _ in ORDER:
                    if present(kind, n, b):
                        misc_copy(kind, b, 0, n)
                        if kind == "logits":
                            router_exp(b)

                def copy_turned(k, par):
                    act.wait_ge(turned, k + 1)
                    if not (isinstance(k, int) and k < 2):
                        act.wait_ge(hidden_filled, k - 1)
                    nc.scalar.activation(block_t[:, par, :], turn_bank[par][:, 0:P], ACT.Copy
                                         ).then_inc(turn_copied, 1)

                def copy_w1(k, par):
                    e = act.value_load(expert_of[0:1, k:k + 1] if isinstance(k, int)
                                       else expert_of[0:1, bass.ds(k, 1)], min_val=0, max_val=EXPERTS - 1)
                    if not (isinstance(k, int) and k < 2):
                        act.wait_ge(gelu_done, k - 1)
                    nc.scalar.activation(b1_now[:, par, :], b1_t[:, bass.ds(e, 1), :].rearrange("p a c -> p (a c)"),
                                         ACT.Copy).then_inc(b1_copied, 1)
                    nc.scalar.activation(w1_now[:, par, :], w1_all[:, bass.ds(e, 1), :].rearrange("p a f -> p (a f)"),
                                         ACT.Copy).then_inc(w1_copied, 1)

                def step(q, r):
                    par = r % 2
                    if isinstance(q, int) and q * NX + r == 0:
                        copy_w1(0, 0)
                        copy_turned(0, 0)
                    if block_at(q, r, -1):
                        k, _, _ = block_at(q, r, -1)
                        copy_w1(k, 1 - par)
                        copy_turned(k, 1 - par)
                    if block_at(q, r, 0):
                        k, _, _ = block_at(q, r, 0)
                        act.wait_ge(b1_copied, k + 1)
                        act.wait_ge(hidden_filled, k + 1)
                        if not (isinstance(k, int) and k < 2):
                            act.wait_ge(y_filled, k - 1)
                        for c in range(FCH):
                            done = nc.scalar.activation(
                                hidden_t[:, par, c * P:(c + 1) * P], hidden_bank[par][:, c * P:(c + 1) * P],
                                ACT.Gelu, bias=b1_now[:, par, c:c + 1])
                        done.then_inc(gelu_done, 1)

                act.wait_ge(plan_step, PLAN_STEPS)
                act.wait_ge(experts_loaded, 4 * 16)
                run_steps(act, LAG + 2, step)

            run_batches(act, batch, tail)

        @block.vector
        def _(dve):
            def reduce(b, par, n, j, i):
                number = (b * GROUPS + n) * GR + j * TILES + i
                dve.wait_ge(s_filled, number + 1)
                if j == 0 and i == 0 and not (is_first(b) and n < 2):
                    dve.wait_ge(shift_step, (b * GROUPS + n - 1) * 4)
                nc.vector.reduce_max(maxima[:, n % 2, j * TILES + i:j * TILES + i + 1], bank_of(s_bank, j, i)[0][:, :],
                                     AXIS_X).then_inc(s_reduced, 1)

            def split_shift(g, step, turned=None):
                b, par, n = g
                number = b * GROUPS + n
                top_of = maxima[:, n % 2, :]
                if step == 0:
                    dve.wait_ge(s_reduced, (number + 1) * GR)
                    if turned is not None:
                        dve.wait_ge(misc_filled, turned)
                    nc.vector.tensor_scalar(shift[:, 0, :], top_of, -1.0, None, ALU.mult).then_inc(shift_step, 1)
                elif step == 1:
                    dve.wait_ge(shift_step, number * 4 + 1)
                    nc.vector.scalar_tensor_tensor(out=shift_rest[:, :], in0=top_of, scalar=-1.0,
                                                   in1=shift[:, 0, :], op0=ALU.mult, op1=ALU.subtract
                                                   ).then_inc(shift_step, 1)
                elif step == 2:
                    dve.wait_ge(shift_step, number * 4 + 2)
                    nc.vector.tensor_copy(shift[:, 1, :], shift_rest[:, :]).then_inc(shift_step, 1)
                else:
                    dve.wait_ge(shift_step, number * 4 + 3)
                    nc.vector.tensor_tensor(shift[:, 2, :], shift_rest[:, :], shift[:, 1, :],
                                            ALU.subtract).then_inc(shift_step, 1)

            def copy_qk(b, side, index):
                dve.wait_ge(misc_filled, index + 1)
                if not is_first(b):
                    dve.wait_ge(lo_ready, b * 2)
                nc.vector.tensor_scalar(qk_rest[:, side, :], misc[:, 0:L], bqk[:, side:side + 1], None,
                                        ALU.add).then_inc(misc_emptied, 1)

            def copy_v(b, par, index):
                dve.wait_ge(misc_filled, index + 1)
                if is_first(b):
                    dve.wait_ge(ones_col, 2)
                bias = bv[:, :].rearrange("p (a h c) -> p a h c", a=1, c=CH).broadcast_to([P, TILES, HEADS, CH])
                nc.vector.tensor_tensor(v_stack[:, par, :, :, 0:CH], misc_v, bias, ALU.add).then_inc(misc_emptied, 1)

            def invert(g, index):
                dve.wait_ge(misc_filled, index + 1)
                nc.vector.reciprocal(recip[:, :, :], misc_h[:, :, :, CH]).then_inc(recip_ready, 1)

            def normalise_heads(g):
                b, par, n = g
                dve.wait_ge(recip_ready, b * GROUPS + n + 1)
                over = recip[:, :, :].rearrange("p t (g a) -> p t g a", a=1).broadcast_to([P, TILES, GH, CH])
                nc.vector.tensor_tensor(
                    heads[:, :, n * GH * CH:(n + 1) * GH * CH].rearrange("p t (g c) -> p t g c", c=CH),
                    misc_h[:, :, :, 0:CH], over, ALU.mult).then_inc(misc_emptied, 1)

            def add_residual(b, par, index):
                dve.wait_ge(misc_filled, index + 1)
                dve.wait_ge(x2b_ready, b * 2)
                if not (isinstance(b, int) and b == 1):
                    dve.wait_ge(x1_ready, (b - 1) * TILES)
                nc.vector.tensor_tensor(resid[:, :, :], misc_td, x2b[:, 1 - par], ALU.add).then_inc(misc_emptied, 1)

            def statistics(b, t):
                if t == 0:
                    dve.wait_ge(misc_emptied, emptied("proj", 1, b))
                nc.vector.bn_stats(stats[:, t, :], resid[:, t, :]).then_inc(stats_ready, 1)

            def aggregate(b, t):
                if t == 0:
                    dve.wait_ge(stats_ready, b * TILES)
                    if not (isinstance(b, int) and b == 1):
                        dve.wait_ge(rstd_ready, b - 1)
                    stand_apart(dve)
                nc.vector.bn_aggr(mean_var[:, t, :], stats[:, t, :]).then_inc(aggr_ready, 1)

            def normalise(b, par, pairs, t):
                if t == 0:
                    dve.wait_ge(rstd_ready, b)
                    dve.wait_ge(scattered[1 - par], pairs * (TILES * 16))
                nc.vector.tensor_scalar(rows[:, 1 - par, t, 0:D], resid[:, t, :], mean_var[:, t, 0:1],
                                        rstd[:, t:t + 1], ALU.subtract, ALU.mult).then_inc(x1_ready, 1)

            def spread(ap):
                return ap.rearrange("p (t a) -> p t a", a=1).broadcast_to([P, TILES, EXPERTS])

            ROUTE_STEPS = 6

            def route(b, step):
                if step == 0:
                    dve.wait_ge(misc_emptied, emptied("logits", 3, b))
                    nc.vector.reduce_max(top[:, :], logits[:, :, :], AXIS_X).then_inc(top_ready, 1)
                elif step == 1:
                    dve.wait_ge(top_ready, b)
                    nc.vector.tensor_tensor(is_top[:, :, :], logits[:, :, :], spread(top[:, :]), ALU.is_equal
                                            ).then_inc(istop_ready, 1)
                elif step == 2:
                    dve.wait_ge(istop_ready, b)
                    nc.vector.scalar_tensor_tensor(out=key[:, :, :], in0=is_top[:, :, :], scalar=-float(EXPERTS),
                                                   in1=expert_no[:, :, :], op0=ALU.mult, op1=ALU.add
                                                   ).then_inc(key_ready, 1)
                elif step == 3:
                    dve.wait_ge(key_ready, b)
                    nc.vector.tensor_reduce(first[:, :], key[:, :, :], AXIS_X, ALU.min).then_inc(first_ready, 1)
                elif step == 4:
                    dve.wait_ge(first_ready, b)
                    if not (isinstance(b, int) and b == 1):
                        dve.wait_ge(place_step, (b - 1) * PLACE_STEPS)
                    nc.vector.tensor_tensor(one_hot[:, :, :], key[:, :, :], spread(first[:, :]), ALU.is_equal
                                            ).then_inc(onehot_ready, 1)
                elif step == 5:
                    if not (isinstance(b, int) and b == 1):
                        dve.wait_ge(prob_ready, b - 1)
                    nc.vector.tensor_tensor(below[:, :, :], logits[:, :, :], spread(top[:, :]), ALU.subtract
                                            ).then_inc(below_ready, 1)

            def misc_use(kind, b, par, n, step):
                if kind is None:
                    return
                index = misc_before(kind, n, b)
                if kind == "U":
                    g = behind(b, par, n, 2) if not (isinstance(b, int) and b == BATCHES) else (b - 1, 1 - par, n + 2)
                    (invert(g, index) if step == 0 else normalise_heads(g))
                elif step == 1:
                    return
                elif kind in ("q", "k"):
                    copy_qk(b + 1, int(kind == "k"), index)
                elif kind == "v":
                    copy_v(b + 1, 1 - par, index)
                elif kind == "proj":
                    add_residual(b, par, index)

            nc.vector.memset(q32[64:128, 0], 0).then_inc(stacks_cleared, 1)
            nc.vector.memset(k32[64:128, 0], ONES_BF16).then_inc(stacks_cleared, 1)
            copy_qk(0, 0, 0)
            copy_qk(0, 1, 1)
            copy_v(0, 0, 2)
            for j in range(GH):
                for i in range(TILES):
                    reduce(0, 0, 0, j, i)
            for step in range(4):
                split_shift((0, 0, 0), step)
            for j in range(GH):
                for i in range(TILES):
                    reduce(0, 0, 1, j, i)
            reduce(0, 0, 2, 0, 0)

            def batch(b, par, pairs):
                for n in range(GROUPS):
                    maxing = ahead(b, par, n, 2)
                    for j in range(GH):
                        following = maxing if j < GH - 1 else ahead(b, par, n, 3)
                        for i in range(TILES):
                            if i < TILES - 1 and maxing:
                                reduce(*maxing, j, i + 1)
                            if i == TILES - 1 and following:
                                reduce(*following, (j + 1) % GH, 0)
                            if j == 0 and ahead(b, par, n, 1):
                                turned = misc_before("q", 0, b) if n == 0 else emptied("sh", n - 1, b)
                                if is_first(b) and n == 0:
                                    turned = len(START)
                                split_shift(ahead(b, par, n, 1), i, turned)
                            if i >= 2:
                                misc_use(slot_of(n, j, b), b, par, n, i - 2)
                            if not is_first(b):
                                at = (n * GH + j) * TILES + i
                                steps = (2 * GH * TILES - 1, 2 * GH * TILES + TILES - 1, (2 * GH + 2) * TILES,
                                         (3 * GH + 1) * TILES)
                                if steps[0] <= at < steps[0] + TILES:
                                    statistics(b, at - steps[0])
                                elif steps[1] <= at < steps[1] + TILES:
                                    aggregate(b, at - steps[1])
                                elif steps[2] <= at < steps[2] + TILES:
                                    normalise(b, par, pairs, at - steps[2])
                                elif steps[3] <= at < steps[3] + ROUTE_STEPS:
                                    route(b, at - steps[3])

            def tail():
                b = BATCHES
                for kind, n, _ in ORDER:
                    if present(kind, n, b):
                        for step in range(2):
                            misc_use(kind, b, 0, n, step)
                        if kind == "proj":
                            for t in range(TILES):
                                statistics(b, t)
                            for t in range(TILES):
                                aggregate(b, t)
                            for t in range(TILES):
                                normalise(b, 0, (b - 1) // 2, t)
                        if kind == "logits":
                            for step in range(ROUTE_STEPS):
                                route(b, step)
                plan_blocks()
                run_steps(dve, LAG + 2, expert_step)

            def plan_blocks():
                done = 0

                def then(instruction):
                    nonlocal done
                    done += 1
                    instruction.then_inc(plan_step, 1)
                    dve.wait_ge(plan_step, done)

                def over_blocks(ap):
                    return ap.rearrange("p (a e) -> p a e", a=1).broadcast_to([1, NBLK, EXPERTS])

                dve.wait_ge(based, BATCHES * (TILES + 1))
                dve.wait_ge(tables_built, TABLES)
                ends = base[0:1, 1, TILES, :]
                then(nc.vector.tensor_copy(region_end[:, :], ends))
                then(nc.vector.scalar_tensor_tensor(out=held[:, :], in0=expert_no[0:1, 0, :], scalar=-float(REGION),
                                                    in1=ends, op0=ALU.mult, op1=ALU.add))
                then(nc.vector.tensor_tensor(
                    begun[:, :, :], held[:, :].rearrange("p (e a) -> p e a", a=1).broadcast_to(
                        [1, EXPERTS, TOKENS // P]), full_at[:, :, :], ALU.is_gt))
                then(nc.vector.tensor_reduce(blocks[:, :], begun[:, :, :], AXIS_X, ALU.add))
                then(nc.vector.tensor_tensor(
                    upto_blocks[:, :, :], up_to[:, :, :], blocks[:, :].rearrange("p (a e) -> p a e", a=1
                                                                                 ).broadcast_to([1, EXPERTS, EXPERTS]),
                    ALU.mult))
                then(nc.vector.tensor_reduce(last_block[:, :], upto_blocks[:, :, :], AXIS_X, ALU.add))
                then(nc.vector.tensor_tensor(passed[:, :, :], block_no[:, :, :], over_blocks(last_block[:, :]),
                                             ALU.is_ge))
                then(nc.vector.tensor_reduce(sums[:, 0, :], passed[:, :, :], AXIS_X, ALU.add))
                then(nc.vector.tensor_scalar(expert_of[:, :], sums[:, 0, :], float(EXPERTS - 1), None, ALU.min))
                then(nc.vector.tensor_scalar(hole[:, :], blocks[:, :], -float(P), float(REGION), ALU.mult, ALU.add))
                then(nc.vector.tensor_tensor(holes[:, :, :], passed[:, :, :], over_blocks(hole[:, :]), ALU.mult))
                then(nc.vector.tensor_reduce(sums[:, 1, :], holes[:, :, :], AXIS_X, ALU.add))
                then(nc.vector.scalar_tensor_tensor(out=row_of[:, :], in0=block_no[:, :, 0], scalar=float(P),
                                                    in1=sums[:, 1, :], op0=ALU.mult, op1=ALU.add))
                assert done == PLAN_STEPS

            def expert_step(q, r):
                par = r % 2
                two, three = block_at(q, r, 2), block_at(q, r, 3)
                if two:
                    k, buf, turn = two
                    dve.wait_ge(rows_loaded[buf], (turn + 1) * 16)
                    if not (isinstance(k, int) and k < 2):
                        dve.wait_ge(out_ready, k - 1)
                    dve.wait_ge(y_filled, k + 1)
                    nc.vector.scalar_tensor_tensor(out=z_now[:, par, :], in0=y_bank[par][:, 0:D],
                                                   scalar=block_rows[:, buf, D:D + 1],
                                                   in1=block_rows[:, buf, 0:D], op0=ALU.mult, op1=ALU.add
                                                   ).then_inc(z_ready, 1)
                if three:
                    k, buf, turn = three
                    if not (isinstance(k, int) and k < 2):
                        dve.wait_ge(out_stored[1 - par], (turn * (NX // 2) + buf // 2) * 16)
                    dve.wait_ge(z_rstd, k + 1)
                    nc.vector.tensor_scalar(out_rows[:, 1 - par, :], z_now[:, 1 - par, :],
                                            sq_mean_var[:, 1 - par, 0:1], sq_rstd[:, 1 - par:2 - par],
                                            ALU.subtract, ALU.mult).then_inc(out_ready, 1)
                if two:
                    k, buf, turn = two
                    dve.wait_ge(z_ready, k + 1)
                    nc.vector.bn_stats(sq_stats[:, par, :], z_now[:, par, :]).then_inc(z_stats, 1)
                    dve.wait_ge(z_stats, k + 1)
                    stand_apart(dve)
                    nc.vector.bn_aggr(sq_mean_var[:, par, :], sq_stats[:, par, :]).then_inc(z_aggr, 1)
                    dve.wait_ge(z_aggr, k + 1)
                    nc.vector.tensor_scalar(sq_var[:, par:par + 1], sq_mean_var[:, par, 1:2], EPS, None, ALU.add
                                            ).then_inc(z_var, 1)

            run_batches(dve, batch, tail)

        @block.gpsimd
        def _(pool):
            nc.gpsimd.memset(v_stack[:, 0], 0.0).then_inc(ones_col, 1)
            pool.wait_ge(ones_col, 1)
            nc.gpsimd.memset(v_stack[:, 0, :, :, CH:CH + 1], 1.0).then_inc(ones_col, 1)

            def split(b, side, step):
                if step == 0:
                    pool.wait_ge(qk_hi, b * 2 + side + 1)
                    nc.gpsimd.tensor_tensor(qk_rest[:, side, :], qk_rest[:, side, :], qk_parts[:, 0, side, :],
                                            ALU.subtract).then_inc(rest_ready, 1)
                else:
                    pool.wait_ge(mid_ready, b * 2 + side + 1)
                    nc.gpsimd.tensor_tensor(qk_parts[:, 2, side, :], qk_rest[:, side, :], qk_parts[:, 1, side, :],
                                            ALU.subtract).then_inc(lo_ready, 1)

            for step in range(2):
                for side in range(2):
                    split(0, side, step)
            pool.wait_ge(lo_ready, 2)
            nc.gpsimd.memset(q32[64:128, 1], 0).then_inc(stacks1_cleared, 1)
            nc.gpsimd.memset(k32[64:128, 1], ONES_BF16).then_inc(stacks1_cleared, 1)
            pool.wait_ge(stacks1_cleared, 2)
            nc.gpsimd.memset(v_stack[:, 1], 0.0).then_inc(ones_col, 1)
            pool.wait_ge(ones_col, 3)
            nc.gpsimd.memset(v_stack[:, 1, :, :, CH:CH + 1], 1.0).then_inc(ones_col, 1)
            nc.gpsimd.memset(ones[:, :], 1.0).then_inc(base_ready, 1)
            pool.wait_ge(base_ready, 1)
            nc.gpsimd.affine_select(out=ident[:, :], in_=ones[:, :], compare_op=ALU.is_equal, fill=0.0, base=0,
                                    pattern=[[-1, P]], channel_multiplier=1).then_inc(consts_built, 1)
            nc.gpsimd.affine_select(out=ident_bf[:, :], in_=ones[:, :], compare_op=ALU.is_equal, fill=0.0, base=0,
                                    pattern=[[-1, P]], channel_multiplier=1).then_inc(consts_built, 1)
            nc.gpsimd.affine_select(out=before[:, :], in_=ones[:, :], compare_op=ALU.is_gt, fill=0.0, base=0,
                                    pattern=[[1, P]], channel_multiplier=-1).then_inc(consts_built, 1)
            nc.gpsimd.iota(expert_no[:, :, :], pattern=[[0, TILES], [1, EXPERTS]], base=0, channel_multiplier=0,
                           allow_small_or_imprecise_dtypes=True).then_inc(consts_built, 1)
            nc.gpsimd.iota(token_no[:, :], pattern=[[P, TOKENS // P]], base=0, channel_multiplier=1
                           ).then_inc(consts_built, 1)
            nc.gpsimd.memset(minus_half[:, :], -0.5).then_inc(consts_built, 1)
            nc.gpsimd.memset(minus_one[:, :], -1.0).then_inc(consts_built, 1)
            nc.gpsimd.memset(base[:, 1, TILES, :], 0.0).then_inc(base_ready, 1)
            pool.wait_ge(base_ready, 2)
            nc.gpsimd.iota(base[:, 1, TILES, :], pattern=[[REGION, EXPERTS]], base=0, channel_multiplier=0,
                           allow_small_or_imprecise_dtypes=True).then_inc(base_ready, 1)
            nc.gpsimd.iota(block_no[:, :, :], pattern=[[1, NBLK], [0, EXPERTS]], base=0, channel_multiplier=0,
                           allow_small_or_imprecise_dtypes=True).then_inc(tables_built, 1)
            nc.gpsimd.iota(full_at[:, :, :], pattern=[[0, EXPERTS], [P, TOKENS // P]], base=0, channel_multiplier=0,
                           allow_small_or_imprecise_dtypes=True).then_inc(tables_built, 1)
            nc.gpsimd.affine_select(out=up_to[:, :, :], in_=ones[0:1, 0:EXPERTS * EXPERTS].rearrange(
                "p (e f) -> p e f", e=EXPERTS), compare_op=ALU.is_ge, fill=0.0, base=0,
                pattern=[[1, EXPERTS], [-1, EXPERTS]], channel_multiplier=0).then_inc(tables_built, 1)
            nc.gpsimd.memset(pad_rows[:, 0:D + 1], 0.0).then_inc(tables_built, 1)
            nc.gpsimd.iota(pad_rows[:, D + 1:D + 2].bitcast(U32), pattern=[[0, 1]], base=TOKENS, channel_multiplier=1
                           ).then_inc(tables_built, 1)
            pool.wait_ge(consts_loaded, 6 * 16)
            pool.wait_ge(consts_built, CONSTS)

            def weigh(b, par):
                pool.wait_ge(prob_ready, b)
                width = EXPERTS
                while width > 1:
                    width //= 2
                    source = prob if width == EXPERTS // 2 else prob_sum
                    nc.gpsimd.tensor_tensor(prob_sum[:, :, 0:width], source[:, :, 0:width],
                                            source[:, :, width:2 * width], ALU.add).then_inc(psum_ready, 1)
                    pool.wait_ge(psum_ready, (b - 1) * HALVINGS + {4: 1, 2: 2, 1: 3}[width])
                nc.gpsimd.tensor_tensor(rows[:, 1 - par, :, D], prob_sum[:, :, 0], minus_one[:, :], ALU.pow
                                        ).then_inc(weight_ready, 1)

            def place_rows(b, par):
                now, was = 1 - par, par
                pool.wait_ge(misc_emptied, emptied("counts", 3, b))
                stand_apart(pool)
                nc.gpsimd.tensor_copy(base[:, now, 0, :], base[:, was, TILES, :]).then_inc(based, 1)
                for t in range(TILES):
                    pool.wait_ge(based, (b - 1) * (TILES + 1) + t + 1)
                    nc.gpsimd.tensor_tensor(base[:, now, t + 1, :], counts[:, 1, t, :], base[:, now, t, :],
                                            ALU.add).then_inc(based, 1)
                pool.wait_ge(based, b * (TILES + 1))
                nc.gpsimd.tensor_tensor(place[:, :, :], counts[:, 0], base[:, now, 0:TILES, :], ALU.add
                                        ).then_inc(place_step, 1)
                pool.wait_ge(place_step, (b - 1) * PLACE_STEPS + 1)
                nc.gpsimd.tensor_tensor(place[:, :, :], place[:, :, :], one_hot[:, :, :], ALU.mult
                                        ).then_inc(place_step, 1)
                for step, width in enumerate((4, 2, 1)):
                    pool.wait_ge(place_step, (b - 1) * PLACE_STEPS + 2 + step)
                    nc.gpsimd.tensor_tensor(place[:, :, 0:width], place[:, :, 0:width],
                                            place[:, :, width:2 * width], ALU.add).then_inc(place_step, 1)
                pool.wait_ge(place_step, (b - 1) * PLACE_STEPS + 5)
                stand_apart(pool)
                nc.gpsimd.tensor_copy(slot[:, 1 - par, :], place[:, :, 0]).then_inc(slot_ready, 1)

            def scatter(b, par):
                pool.wait_ge(slot_ready, b)
                pool.wait_ge(weight_ready, b)
                pool.wait_ge(x1_ready, b * TILES)
                pool.wait_ge(id_ready, b)
                stand_apart(pool)
                for t in range(TILES):
                    nc.gpsimd.indirect_dma_start(
                        scratch, bass.IndirectOffsetOnAxis(ap=slot[:, 1 - par, t:t + 1], axis=0),
                        rows[:, 1 - par, t, :], None).then_inc(scattered[1 - par], 16)

            def row_work(b, par, pairs):
                pool.wait_ge(aggr_ready, b * TILES)
                if not (isinstance(b, int) and b == 1):
                    pool.wait_ge(x1_ready, (b - 1) * TILES)
                stand_apart(pool)
                nc.gpsimd.tensor_scalar_add(var_eps[:, :], mean_var[:, :, 1], EPS).then_inc(vareps_ready, 1)
                pool.wait_ge(vareps_ready, b)
                nc.gpsimd.tensor_tensor(rstd[:, :], var_eps[:, :], minus_half[:, :], ALU.pow).then_inc(rstd_ready, 1)
                pool.wait_ge(scattered[1 - par], pairs * (TILES * 16))
                stand_apart(pool)
                numbers = (token_no[:, (b - 1) * TILES:b * TILES] if isinstance(b, int)
                           else token_no[:, bass.ds((b - 1) * TILES, TILES)])
                nc.gpsimd.tensor_copy(rows[:, 1 - par, :, :].bitcast(U32)[:, :, D + 1], numbers).then_inc(id_ready, 1)

            def batch(b, par, pairs):
                pool.wait_ge(x_loaded, (b + 1) * 16)
                if not is_first(b):
                    pool.wait_ge(misc_emptied, len(START) if is_first(b) else misc_before("q", 0, b))
                bias = bo[:, :].rearrange("p (a d) -> p a d", a=1).broadcast_to([P, TILES, D])
                nc.gpsimd.tensor_tensor(x2b[:, par], x_in[:, par], bias, ALU.add).then_inc(x2b_ready, 1)
                pool.wait_ge(x2b_ready, b * 2 + 1)
                nc.gpsimd.tensor_tensor(x2b[:, par], x2b[:, par], x_in[:, par], ALU.add).then_inc(x2b_ready, 1)
                if not is_last(b):
                    for step in range(2):
                        for side in range(2):
                            split(b + 1, side, step)
                if not is_first(b):
                    row_work(b, par, pairs)
                    weigh(b, par)
                    place_rows(b, par)
                    scatter(b, par)

            def tail():
                row_work(BATCHES, 0, (BATCHES - 1) // 2)
                weigh(BATCHES, 0)
                place_rows(BATCHES, 0)
                scatter(BATCHES, 0)

                def step(q, r):
                    par = r % 2
                    if block_at(q, r, 1):
                        k, buf, _ = block_at(q, r, 1)
                        pool.wait_ge(out_ready, k + 1)
                        stand_apart(pool)
                        nc.gpsimd.indirect_dma_start(
                            out_flat, bass.IndirectOffsetOnAxis(
                                ap=block_rows[:, buf, D + 1:D + 2].bitcast(U32), axis=0),
                            out_rows[:, 1 - par, :], None, bounds_check=TOKENS - 1, oob_is_err=False
                            ).then_inc(out_stored[1 - par], 16)
                    if block_at(q, r, 0):
                        k, _, _ = block_at(q, r, 0)
                        pool.wait_ge(z_var, k + 1)

                        if not (isinstance(k, int) and k < 2):
                            pool.wait_ge(out_ready, k - 1)
                        stand_apart(pool)
                        nc.gpsimd.tensor_tensor(sq_rstd[:, par:par + 1], sq_var[:, par:par + 1], minus_half[:, 0:1],
                                                ALU.pow).then_inc(z_rstd, 1)

                run_steps(pool, LAG + 2, step)
                for par in range(2):
                    pool.wait_ge(out_stored[par], NBLK // 2 * 16)

            run_batches(pool, batch, tail)


def kernel(**inputs):
    import numpy as _np
    import concourse.bacc as _bacc
    from concourse import mybir as _mybir
    from concourse.bass_utils import run_bass_kernel_spmd as _run

    given = {name[3:].split("_", 1)[1]: _np.asarray(a) for name, a in inputs.items()}
    x, w_qkv, b_qkv = given["x"], given["w_qkv"], given["b_qkv"]
    D = x.shape[-1]
    HEADS = 16
    order = _np.arange(D).reshape(HEADS, D // HEADS).T.reshape(-1)
    order = _np.concatenate([order, D + order, _np.arange(2 * D, 3 * D)])
    arrays = {"x": x, "x_t": x.transpose(0, 2, 1), "w_qkv_t": w_qkv[order].T, "b_qkv": b_qkv[order],
              "w_o_t": given["w_o"].T, "b_o": given["b_o"], "gate_w": given["gate_w"],
              "w1": given["w1"], "b1": given["b1"], "w2": given["w2"], "b2": given["b2"]}

    nc = _bacc.Bacc("TRN2", target_bir_lowering=False, num_devices=1)
    args = []
    for name in list(arrays):
        a = _np.ascontiguousarray(arrays.pop(name))
        arrays[f"in_{name}_dram"] = a
        args.append(nc.dram_tensor(f"in_{name}_dram", a.shape, _mybir.dt.from_np(a.dtype), kind="ExternalInput").ap())
    args.append(nc.dram_tensor("out_dram", x.shape, _mybir.dt.float32, kind="ExternalOutput").ap())
    build(nc, *args)
    r = _run(nc, [arrays], core_ids=[0])
    return r.results[0]["out_dram"]
```

```python
from contextlib import ExitStack

import concourse.bass as bass
from concourse import mybir

F32 = mybir.dt.float32
BF16 = mybir.dt.bfloat16
U32 = mybir.dt.uint32
I32 = mybir.dt.int32
ALU = mybir.AluOpType
ACT = mybir.ActivationFunctionType
AXIS_X = mybir.AxisListType.X

P = 128
EPS = 1e-5
MINUS_ONES_BF16 = 0xBF80BF80


def build(nc, x, x_t, w_qkv_t, b_qkv, w_o_t, b_o, gate_w, w1, b1, w2, b2, out):
    BATCHES, L, D = x.shape
    HEADS = 16
    CH = D // HEADS
    SCALE = 1.0 / float(D) ** 0.5
    TILES = L // P
    GH = 4
    GROUPS = HEADS // GH
    EXPERTS, _, FF = w1.shape
    FCH = FF // P
    TOKENS = BATCHES * L
    PARTS = 3
    BLOCKS9 = PARTS * PARTS
    ROWS_S = 96
    SHIFT_ROW = 96
    VW = 32
    GR = GH * TILES
    REGION = TOKENS + P
    NBLK = (TOKENS + EXPERTS * (P - 1)) // P
    ROW = D + 2
    SCRATCH_ROWS = EXPERTS * REGION + P * EXPERTS

    ctx = ExitStack()
    with ctx:
        def sb(name, shape, dt=F32):
            return ctx.enter_context(nc.sbuf_tensor(name, shape, dt))

        def psum(name, shape, dt=F32):
            return ctx.enter_context(nc.psum_tensor(name, shape, dt))

        def sem(name):
            return ctx.enter_context(nc.semaphore(name))

        Q_PARTS = 2 * PARTS - 1
        parts_dram = nc.dram_tensor("split_parts", [2, Q_PARTS + PARTS, CH, HEADS * L], BF16, kind="Internal").ap()
        scratch = nc.dram_tensor("routed_rows", [SCRATCH_ROWS, ROW], F32, kind="Internal").ap()

        warm = sb("warm", [P, 1])
        wqkv = sb("wqkv", [P, 3 * D])
        bqk = sb("bqk", [P, 2])
        bv = sb("bv", [P, D])
        wo = sb("wo", [P, D])
        bo = sb("bo", [P, D])
        gate = sb("gate", [P, EXPERTS])
        ident = sb("ident", [P, P])
        ident_bf = sb("ident_bf", [P, P], BF16)
        before = sb("before", [P, P], BF16)
        ones_bf = sb("ones_bf", [P, P], BF16)
        ones = sb("ones", [P, P])
        expert_no = sb("expert_no", [P, TILES, EXPERTS])
        token_no = sb("token_no", [P, TOKENS // P], U32)
        minus_half = sb("minus_half", [P, TILES])
        xt_in = sb("xt_in", [P, 2, L])
        x_in = sb("x_in", [P, 2, TILES, D])
        x2b = sb("x2b", [P, 2, TILES, D])
        qk_rest = sb("qk_rest", [P, 2, L])
        qk_parts = sb("qk_parts", [P, PARTS, 2, L], BF16)
        q_stack = sb("q_stack", [P, 2, HEADS, L], BF16)
        k_stack = sb("k_stack", [P, 2, HEADS, L], BF16)
        v_stack = sb("v_stack", [P, 2, TILES, HEADS, VW])
        probs = sb("probs", [P, 2, GH, TILES, L])
        maxima = sb("maxima", [P, 2, GR])
        shift_rest = sb("shift_rest", [P, GR])
        shift = sb("shift", [P, PARTS, GR], BF16)
        shift_t = sb("shift_t", [PARTS * GR, 2, P], BF16)
        pv_copy = sb("pv_copy", [P, 2, L])
        recip = sb("recip", [P, TILES, GH])
        heads = sb("heads", [P, TILES, D])
        heads_t = sb("heads_t", [P, L])
        resid = sb("resid", [P, TILES, D])
        stats = sb("stats", [P, TILES, 6])
        mean_var = sb("mean_var", [P, TILES, 2])
        var_eps = sb("var_eps", [P, TILES])
        rstd = sb("rstd", [P, TILES])
        rows = sb("rows", [P, 2, TILES, ROW])
        x1_t = sb("x1_t", [P, L])
        logits = sb("logits", [P, TILES, EXPERTS])
        key = sb("key", [P, TILES, EXPERTS])
        top = sb("top", [P, TILES])
        is_top = sb("is_top", [P, TILES, EXPERTS])
        below = sb("below", [P, TILES, EXPERTS])
        prob = sb("prob", [P, TILES, EXPERTS])
        first = sb("first", [P, TILES])
        one_hot = sb("one_hot", [P, TILES, EXPERTS], BF16)
        prob_sum = sb("prob_sum", [P, TILES])
        base = sb("base", [P, 2, EXPERTS])
        place = sb("place", [P, TILES, EXPERTS])
        own_place = sb("own_place", [P, TILES])
        slot = sb("slot", [P, 2, TILES], U32)

        b2_row = sb("b2_row", [1, EXPERTS, D])
        b1_t = sb("b1_t", [P, EXPERTS, FCH])
        pad_rows = sb("pad_rows", [P, ROW])
        block_no = sb("block_no", [1, NBLK, EXPERTS])
        full_at = sb("full_at", [1, EXPERTS, TOKENS // P])
        up_to = sb("up_to", [1, EXPERTS, EXPERTS])
        held = sb("held", [1, EXPERTS])
        begun = sb("begun", [1, EXPERTS, TOKENS // P])
        blocks = sb("blocks", [1, EXPERTS])
        upto_blocks = sb("upto_blocks", [1, EXPERTS, EXPERTS])
        last_block = sb("last_block", [1, EXPERTS])
        passed = sb("passed", [1, NBLK, EXPERTS])
        hole = sb("hole", [1, EXPERTS])
        holes = sb("holes", [1, NBLK, EXPERTS])
        sums = sb("sums", [1, 2, NBLK])
        expert_of = sb("expert_of", [1, NBLK], I32)
        row_of = sb("row_of", [1, NBLK], I32)
        region_end = sb("region_end", [1, EXPERTS], I32)
        sq_mean_var = sb("sq_mean_var", [P, 2, 2])
        sq_stats = sb("sq_stats", [P, 2, 6])
        sq_rstd = sb("sq_rstd", [P, 2])
        sq_var = sb("sq_var", [P, 2])

        s_bank = [psum(f"s_bank{i}", [P, L]) for i in range(3)]
        st_bank = [psum(f"st_bank{i}", [P, L]) for i in range(3)]
        pv_bank = psum("pv_bank", [P, L])
        misc = psum("misc", [P, 512])

        qkv_loaded = sem("qkv_loaded")
        consts_loaded = sem("consts_loaded")
        consts_built = sem("consts_built")
        tables_warm = sem("tables_warm")
        register_waited = sem("register_waited")
        stacks_cleared = sem("stacks_cleared")
        stacks1_cleared = sem("stacks1_cleared")
        base_ready = sem("base_ready")
        ones_col = sem("ones_col")
        x_loaded = sem("x_loaded")
        xt_loaded = sem("xt_loaded")
        qk_hi = sem("qk_hi")
        k0_projected = sem("k0_projected")
        k0_rest = sem("k0_rest")
        mid_ready = sem("mid_ready")
        lo_ready = sem("lo_ready")
        x2b_ready = sem("x2b_ready")
        s_filled = sem("s_filled")
        s_reduced = sem("s_reduced")
        shift_step = sem("shift_step")
        shift_loaded = sem("shift_loaded")
        st_filled = sem("st_filled")
        exp_done = sem("exp_done")
        pv_done = sem("pv_done")
        pv_copied = sem("pv_copied")
        recip_ready = sem("recip_ready")
        stats_ready = sem("stats_ready")
        aggr_ready = sem("aggr_ready")
        vareps_ready = sem("vareps_ready")
        rstd_ready = sem("rstd_ready")
        x1_ready = sem("x1_ready")
        top_ready = sem("top_ready")
        below_ready = sem("below_ready")
        istop_ready = sem("istop_ready")
        key_ready = sem("key_ready")
        first_ready = sem("first_ready")
        onehot_ready = sem("onehot_ready")
        prob_ready = sem("prob_ready")
        sum_ready = sem("sum_ready")
        weight_ready = sem("weight_ready")
        based = sem("based")
        placed = sem("placed")
        place_own = sem("place_own")
        place_summed = sem("place_summed")
        slot_ready = sem("slot_ready")
        id_ready = sem("id_ready")
        misc_filled = sem("misc_filled")
        misc_emptied = sem("misc_emptied")

        scattered = [sem(f"scattered{i}") for i in range(2)]
        parts_stored = [sem(f"parts_stored{i}") for i in range(PARTS)]

        stack_loaded = [sem(f"stack_loaded{i}") for i in range(2)]
        STACK_LOADS = 2
        STORES = [2 if part < PARTS - 1 else 1 for part in range(PARTS)]

        w1_all = q_stack[:, 0, :, :].rearrange("p h l -> p (h l)").bitcast(F32).rearrange(
            "p (e f) -> p e f", e=EXPERTS)
        w2_all = k_stack[:, 0, :, :].rearrange("p h l -> p (h l)").bitcast(F32).rearrange(
            "p (e c d) -> p e c d", e=EXPERTS, c=FCH)
        pool_of = probs[:, :, :, :, :].rearrange("p a g t l -> p (a g t l)")
        NX = 8
        widths = {"block_rows": NX * ROW, "block_t": 2 * P, "w1_now": 2 * FF, "hidden_t": 2 * FF,
                  "b1_now": 2 * FCH, "z_now": 2 * D, "out_rows": 2 * D}
        starts, begin = {}, 0
        for name, width in widths.items():
            starts[name] = begin
            begin += width

        def over_probs(name, count):
            return pool_of[:, starts[name]:starts[name] + widths[name]].rearrange("p (a x) -> p a x", a=count)

        block_rows, block_t = over_probs("block_rows", NX), over_probs("block_t", 2)
        w1_now, b1_now, hidden_t = over_probs("w1_now", 2), over_probs("b1_now", 2), over_probs("hidden_t", 2)
        z_now, out_rows = over_probs("z_now", 2), over_probs("out_rows", 2)
        turn_bank, hidden_bank, y_bank = st_bank[0:2], s_bank[0:2], [s_bank[2], st_bank[2]]
        out_flat = out.rearrange("b l d -> (b l) d")

        experts_loaded = sem("experts_loaded")
        tables_built = sem("tables_built")
        plan_step = sem("plan_step")
        padded = sem("padded")
        rows_loaded = [sem(f"rows_loaded{i}") for i in range(NX)]
        turned = sem("turned")
        turn_copied = sem("turn_copied")
        w1_copied = sem("w1_copied")
        b1_copied = sem("b1_copied")
        hidden_filled = sem("hidden_filled")
        gelu_done = sem("gelu_done")
        y_filled = sem("y_filled")
        z_ready = sem("z_ready")
        z_stats = sem("z_stats")
        z_aggr = sem("z_aggr")
        z_var = sem("z_var")
        z_rstd = sem("z_rstd")
        out_ready = sem("out_ready")
        out_stored = [sem(f"out_stored{i}") for i in range(2)]

        LAG = 3

        def run_steps(eng, first, step):
            for k in range(first):
                step(0, k)
            turns = (NBLK - 1 - first) // NX
            with eng.Fori(0, turns) as i:
                for r in range(NX):
                    step(i, first + r)
            for k in range(first + turns * NX, NBLK + LAG):
                step(0, k)

        def block_at(i, m, lag):
            number = i * NX + m - lag
            if isinstance(number, int) and not 0 <= number < NBLK:
                return None
            return number, (m - lag) % NX, i + (m - lag) // NX

        ORDER = [("q", 0, 0), ("sh", 0, 1), ("k", 0, 2), ("U", 0, 3),
                 ("U", 1, 0), ("sh", 1, 1), ("headsT", 1, 2), ("proj", 1, 3),
                 ("U", 2, 0), ("sh", 2, 1), ("v", 2, 2), ("x1T", 2, 3),
                 ("logits", 3, 0), ("sh", 3, 1), ("U", 3, 2), ("counts", 3, 3)]
        OLD = ("headsT", "proj", "x1T", "logits", "counts")

        CONSTS = 7
        TABLES = 5
        PLAN_STEPS = 13
        LOOPED = 3
        def present(kind, n, b):
            if isinstance(b, int):
                if b == 0:
                    return kind not in OLD and not (kind == "U" and n < 2)
                if b == BATCHES - 1:
                    return kind not in ("q", "k", "v") and not (kind == "sh" and n == GROUPS - 1)
                if b == BATCHES:
                    return kind in OLD or (kind == "U" and n < 2)
            return True

        START = ["q", "v", "sh"]
        uses0 = sum(present(k, n, 0) for k, n, _ in ORDER)
        uses7 = sum(present(k, n, BATCHES - 1) for k, n, _ in ORDER)

        def misc_before(kind, n, b):
            at = sum(present(k, m, b) for k, m, s in ORDER[:[(k, m) for k, m, _ in ORDER].index((kind, n))])
            if isinstance(b, int) and b == 0:
                return len(START) + at
            if isinstance(b, int) and b == BATCHES:
                return len(START) + uses0 + len(ORDER) * (BATCHES - 2) + uses7 + at
            return len(START) + uses0 + len(ORDER) * (b - 1) + at

        def emptied(kind, n, b):
            return misc_before(kind, n, b) + 1

        def slot_of(n, s, b):
            for kind, m, t in ORDER:
                if (m, t) == (n, s) and present(kind, m, b):
                    return kind
            return None

        def run_batches(eng, body, tail):
            for b in range(LOOPED):
                body(b, b % 2, max(b - 1, 0) // 2)
            with eng.Fori((LOOPED - 1) // 2, (BATCHES - 2) // 2) as i:
                body(i * 2 + 1, 1, i)
                body(i * 2 + 2, 0, i)
            body(BATCHES - 1, 1, (BATCHES - 2) // 2)
            tail()

        def is_last(b):
            return isinstance(b, int) and b == BATCHES - 1

        def is_first(b):
            return isinstance(b, int) and b == 0

        def ahead(b, par, n, k):
            m = n + k
            if is_last(b) and m >= GROUPS:
                return None
            return (b + 1, 1 - par, m - GROUPS) if m >= GROUPS else (b, par, m)

        def behind(b, par, n, k):
            m = n - k
            if is_first(b) and m < 0:
                return None
            return (b - 1, 1 - par, m + GROUPS) if m < 0 else (b, par, m)

        def bank_of(banks, j, i):
            at = j * TILES + i
            return banks[1 if at == GR - 1 else at % 3], {0: 4, 1: 2, 2: 4, GR - 1: 2}.get(at, 3)

        q32, k32 = q_stack[:, :, :, :].bitcast(U32), k_stack[:, :, :, :].bitcast(U32)
        misc_h = misc[:, 0:TILES * P].rearrange("p (t g w) -> p t g w", t=TILES, g=GH)
        misc_bf = misc[:, 0:P].bitcast(BF16)
        misc_v = misc[:, 0:TILES * D].rearrange("p (t h c) -> p t h c", t=TILES, c=CH)
        misc_td = misc[:, 0:TILES * D].rearrange("p (t d) -> p t d", t=TILES)
        misc_counts = misc[:, 0:(TILES + 1) * EXPERTS].rearrange("p (t e) -> p t e", e=EXPERTS)
        misc_lg = misc[:, 0:TILES * EXPERTS].rearrange("p (t e) -> p t e", t=TILES)

        def stand_apart(eng):
            eng.sem_inc(register_waited, 1)

        block = ctx.enter_context(nc.Block())

        @block.sync
        def _(sp):
            def load_x(b, par):
                sp.dma_start(xt_in[:, par, :], x_t[b]).then_inc(xt_loaded, 16)
                sp.dma_start(x_in[:, par], x[b].rearrange("(t p) d -> p t d", p=P)).then_inc(x_loaded, 16)

            def store_part(b, par, part):
                sp.wait_ge((qk_hi, mid_ready, lo_ready)[part], b * 2 + 2)
                sp.dma_start(parts_dram[par, part:part + Q_PARTS + 1:Q_PARTS].rearrange("s c (h l) -> (c h) s l", l=L),
                             qk_parts[:, part]).then_inc(parts_stored[part], 16)
                if part < PARTS - 1:
                    sp.dma_start(parts_dram[par, PARTS + part].rearrange("c (h l) -> (c h) l", l=L),
                                 qk_parts[:, part, 0]).then_inc(parts_stored[part], 16)

            def fill_stacks(b, par, read):
                for part in range(PARTS):
                    sp.wait_ge(parts_stored[part], (b + 1) * (STORES[part] * 16))
                    stand_apart(sp)
                sp.wait_ge(st_filled, read)
                stand_apart(sp)
                for half in range(2):
                    heads_of = slice(half * HEADS // 2, (half + 1) * HEADS // 2)
                    columns = slice(half * HEADS // 2 * L, (half + 1) * HEADS // 2 * L)
                    k_parts = parts_dram[par, Q_PARTS:Q_PARTS + PARTS, :, columns].rearrange(
                        "(z a) c l -> z (a c) l", z=1).broadcast_to([PARTS, PARTS * CH, HEADS // 2 * L])
                    q_parts = bass.AP(tensor=parts_dram.tensor, offset=parts_dram[par, 0, :, columns].offset,
                                      ap=[[CH * HEADS * L, PARTS], [HEADS * L, PARTS * CH], [1, HEADS // 2 * L]])
                    for stack, source in ((k_stack, k_parts), (q_stack, q_parts)):
                        sp.dma_start(stack[0:CH * BLOCKS9, par, heads_of].rearrange("c h l -> c (h l)"),
                                     source).then_inc(stack_loaded[half], 16)

            def load_shift(g, index):
                b, par, n = g
                sp.wait_ge(misc_emptied, index + 1)
                for a in range(PARTS):
                    sp.dma_start(
                        q_stack[SHIFT_ROW + a:SHIFT_ROW + a + 1, par, n * GH:(n + 1) * GH, :].rearrange(
                            "a h (t l) -> a (h t) l", t=TILES),
                        shift_t[a * GR:(a + 1) * GR, n % 2, :]).then_inc(shift_loaded, 16)

            sp.dma_start(wqkv[:, :], w_qkv_t).then_inc(qkv_loaded, 16)
            sp.dma_start(xt_in[:, 0, :], x_t[0]).then_inc(xt_loaded, 16)
            sp.dma_start(bqk[:, :], b_qkv[0:2 * D].rearrange("(a p) -> p a", p=P),
                         allow_slow_non_contiguous=True).then_inc(qkv_loaded, 16)
            sp.dma_start(bv[:, :], b_qkv[2 * D:3 * D].rearrange("(a d) -> a d", a=1).broadcast_to([P, D])
                         ).then_inc(consts_loaded, 16)
            sp.dma_start(x_in[:, 0], x[0].rearrange("(t p) d -> p t d", p=P)).then_inc(x_loaded, 16)
            sp.dma_start(wo[:, :], w_o_t).then_inc(consts_loaded, 16)
            sp.dma_start(bo[:, :], b_o.rearrange("(a d) -> a d", a=1).broadcast_to([P, D])
                         ).then_inc(consts_loaded, 16)
            sp.dma_start(gate[:, :], gate_w).then_inc(consts_loaded, 16)
            sp.wait_ge(stacks_cleared, 2)
            for part in range(PARTS):
                store_part(0, 0, part)
            fill_stacks(0, 0, 0)
            load_x(1, 1)
            load_shift((0, 0, 0), 2)

            def batch(b, par, pairs):
                def turned_shift(n):
                    if ahead(b, par, n, 1):
                        load_shift(ahead(b, par, n, 1), misc_before("sh", n, b))

                if not is_last(b):
                    if not is_first(b):
                        sp.wait_ge(st_filled, b * (GROUPS * GR) - GR)
                        stand_apart(sp)
                        sp.wait_ge(x2b_ready, b * 2)
                        load_x(b + 1, 1 - par)
                    if is_first(b):
                        sp.wait_ge(stacks1_cleared, 2)
                    else:
                        for half in range(2):
                            sp.wait_ge(stack_loaded[half], b * (STACK_LOADS * 16))
                turned_shift(0)
                if not is_last(b):
                    for part in range(PARTS):
                        store_part(b + 1, 1 - par, part)
                    fill_stacks(b + 1, 1 - par, b * (GROUPS * GR))
                for n in range(1, GROUPS):
                    turned_shift(n)

            def tail():
                sp.dma_start(b2_row[:, :, :], b2.rearrange("(a e) d -> a e d", a=1)).then_inc(experts_loaded, 16)
                sp.dma_start(b1_t[:, :, :], b1.rearrange("e (c p) -> p e c", p=P), allow_slow_non_contiguous=True
                             ).then_inc(experts_loaded, 16)
                sp.wait_ge(st_filled, (BATCHES - 1) * GROUPS * GR)
                sp.dma_start(w1_all, w1.rearrange("e d f -> d e f")).then_inc(experts_loaded, 16)
                sp.dma_start(w2_all, w2.rearrange("e (c f) d -> f e c d", f=P)).then_inc(experts_loaded, 16)
                sp.wait_ge(tables_built, TABLES)
                sp.dma_start(scratch[EXPERTS * REGION:SCRATCH_ROWS].rearrange("(a p) r -> p a r", p=P),
                             pad_rows[:, :].rearrange("p (a r) -> p a r", a=1).broadcast_to([P, EXPERTS, ROW])
                             ).then_inc(padded, 16)
                sp.wait_ge(plan_step, 1)
                for e in range(EXPERTS // 2):
                    end = sp.value_load(region_end[0:1, e:e + 1], min_val=0, max_val=EXPERTS * REGION)
                    sp.dma_start(scratch[bass.ds(end, P), :], pad_rows[:, :]).then_inc(padded, 16)
                for par in range(2):
                    sp.wait_ge(scattered[par], BATCHES // 2 * TILES * 16)
                sp.wait_ge(padded, (EXPERTS + 1) * 16)
                sp.wait_ge(plan_step, PLAN_STEPS)
                sp.wait_ge(pv_done, BATCHES * GROUPS)

                def step(q, r):
                    if block_at(q, r, 0) is None:
                        return
                    k, buf, turn = block_at(q, r, 0)
                    if not (isinstance(k, int) and k < NX):
                        sp.wait_ge(out_stored[buf % 2], ((turn - 1) * (NX // 2) + buf // 2 + 1) * 16)
                    row = sp.value_load(row_of[0:1, k:k + 1] if isinstance(k, int) else row_of[0:1, bass.ds(k, 1)],
                                        min_val=0, max_val=SCRATCH_ROWS - P)
                    sp.dma_start(block_rows[:, buf], scratch[bass.ds(row, P), :]).then_inc(rows_loaded[buf], 16)

                run_steps(sp, NX, step)

            run_batches(sp, batch, tail)

        @block.tensor
        def _(pe):
            def fill_misc(index):
                pe.wait_ge(misc_emptied, index)

            def project_qk(side, par):
                nc.tensor.matmul(misc[:, 0:L], wqkv[:, side * D:(side + 1) * D], xt_in[:, par, :],
                                 start=True, stop=True).then_inc(misc_filled, 1)

            def count():
                last = TILES * EXPERTS
                oh = one_hot[:, :, :].rearrange("p t e -> p (t e)")
                nc.tensor.matmul(misc[:, last:last + EXPERTS], ones_bf[:, :], oh[:, last - EXPERTS:last],
                                 start=True, stop=False)
                nc.tensor.matmul(misc[:, 0:last], before[:, :], oh, start=False, stop=False)
                for later in range(1, TILES + 1):
                    width = min(TILES - 1, TILES + 1 - later) * EXPERTS
                    mm = nc.tensor.matmul(misc[:, later * EXPERTS:later * EXPERTS + width], ones_bf[:, :],
                                          oh[:, 0:width], start=False, stop=(later == TILES))
                mm.then_inc(misc_filled, 1)

            def project_v(par):
                for t in range(TILES):
                    mm = nc.tensor.matmul(misc[:, t * D:(t + 1) * D], xt_in[:, par, t * P:(t + 1) * P],
                                          wqkv[:, 2 * D:3 * D], start=True, stop=True)
                mm.then_inc(misc_filled, 1)

            def turn_shift():
                nc.tensor.transpose(misc_bf[0:PARTS * GR, 0:P],
                                    shift[:, :, :].rearrange("p a g -> p (a g)"),
                                    ident_bf[:, :]).then_inc(misc_filled, 1)

            def scores(b, par, n, j, i):
                h = n * GH + j
                number = (b * GROUPS + n) * GR + j * TILES + i
                bank, last = bank_of(s_bank, j, i)
                if not (isinstance(number, int) and number < last):
                    pe.wait_ge(s_reduced, number - last + 1)
                nc.tensor.matmul(bank[:, :], q_stack[0:ROWS_S, par, h, i * P:(i + 1) * P],
                                 k_stack[0:ROWS_S, par, h, :], start=True, stop=True).then_inc(s_filled, 1)

            def scores_t(b, par, n, j, i):
                h = n * GH + j
                number = (b * GROUPS + n) * GR + j * TILES + i
                bank, last = bank_of(st_bank, j, i)
                if not (isinstance(number, int) and number < last):
                    pe.wait_ge(exp_done, number - last + 1)
                nc.tensor.matmul(bank[:, :], k_stack[:, par, h, i * P:(i + 1) * P],
                                 q_stack[:, par, h, :], start=True, stop=True).then_inc(st_filled, 1)

            def probs_v(b, par, n, i, buf):
                for j in range(GH):
                    mm = nc.tensor.matmul(pv_bank[VW * j:VW * (j + 1), :], v_stack[:, par, i, n * GH + j, :],
                                          probs[:, buf, j, i, :], start=(i == 0), stop=(i == TILES - 1))
                if i == TILES - 1:
                    mm.then_inc(pv_done, 1)

            def misc_work(kind, b, par, n):
                if kind is None:
                    return
                fill_misc(misc_before(kind, n, b))
                if kind == "U":
                    g = behind(b, par, n, 2) if not (isinstance(b, int) and b == BATCHES) else (b - 1, 1 - par, n + 2)
                    pe.wait_ge(pv_copied, g[0] * GROUPS + g[2] + 1)
                    for t in range(TILES):
                        mm = nc.tensor.transpose(misc[:, t * P:(t + 1) * P],
                                                 pv_copy[:, g[2] % 2, t * P:(t + 1) * P], ident[:, :])
                    mm.then_inc(misc_filled, 1)
                elif kind == "sh":
                    pe.wait_ge(shift_step, (b * GROUPS + n + 2) * 4)
                    stand_apart(pe)
                    turn_shift()
                elif kind in ("q", "k"):
                    if kind == "q":
                        pe.wait_ge(xt_loaded, (b + 2) * 16)
                    project_qk(int(kind == "k"), 1 - par)
                elif kind == "v":
                    project_v(1 - par)
                elif kind == "headsT":
                    for t in range(TILES):
                        mm = nc.tensor.transpose(misc[:, t * P:(t + 1) * P], heads[:, t, :], ident[:, :])
                    mm.then_inc(misc_filled, 1)
                elif kind == "proj":
                    for t in range(TILES):
                        mm = nc.tensor.matmul(misc[:, t * D:(t + 1) * D], heads_t[:, t * P:(t + 1) * P],
                                              wo[:, :], start=True, stop=True)
                    mm.then_inc(misc_filled, 1)
                elif kind == "x1T":
                    pe.wait_ge(x1_ready, b * TILES)
                    for t in range(TILES):
                        mm = nc.tensor.transpose(misc[:, t * P:(t + 1) * P], rows[:, 1 - par, t, 0:D], ident[:, :])
                    mm.then_inc(misc_filled, 1)
                elif kind == "logits":
                    for t in range(TILES):
                        mm = nc.tensor.matmul(misc[:, t * EXPERTS:(t + 1) * EXPERTS],
                                              x1_t[:, t * P:(t + 1) * P], gate[:, :], start=True, stop=True)
                    mm.then_inc(misc_filled, 1)
                elif kind == "counts":
                    pe.wait_ge(onehot_ready, b)
                    count()

            pe.wait_ge(xt_loaded, 16)
            pe.wait_ge(qkv_loaded, 2 * 16)
            project_qk(0, 0)
            nc.tensor.matmul(s_bank[0][:, :], wqkv[:, D:2 * D], xt_in[:, 0, :],
                             start=True, stop=True).then_inc(k0_projected, 1)
            fill_misc(1)
            project_v(0)
            pe.wait_ge(k0_rest, 1)
            for n in range(2):
                pe.wait_ge(stack_loaded[0], STACK_LOADS * 16)
                for j in range(GH):
                    for i in range(TILES):
                        scores(0, 0, n, j, i)
                if n == 0:
                    fill_misc(2)
                    pe.wait_ge(consts_built, CONSTS)
                    pe.wait_ge(shift_step, 4)
                    turn_shift()
            pe.wait_ge(stack_loaded[1], STACK_LOADS * 16)
            scores(0, 0, 2, 0, 0)
            pe.wait_ge(consts_loaded, 4 * 16)

            def batch(b, par, pairs):
                for n in range(GROUPS):
                    maxing, multiplying = ahead(b, par, n, 2), behind(b, par, n, 1)
                    pe.wait_ge(shift_loaded, (b * GROUPS + n + 1) * (PARTS * 16))
                    for j in range(GH):
                        for i in range(TILES):
                            scores_t(b, par, n, j, i)
                            if maxing and i < TILES - 1:
                                scores(*maxing, j, i + 1)
                            if i == 1:
                                misc_work(slot_of(n, j, b), b, par, n)
                        following = maxing if j < GH - 1 else ahead(b, par, n, 3)
                        if following:
                            if j == GH - 1 and n % 2 == 1:
                                half = n // 2
                                pe.wait_ge(stack_loaded[half], (b + 2) * (STACK_LOADS * 16))
                            scores(*following, (j + 1) % GH, 0)
                        if multiplying:
                            if j == 0:
                                pe.wait_ge(exp_done, (b * GROUPS + n) * GR)
                                if behind(b, par, n, 2):
                                    pe.wait_ge(pv_copied, b * GROUPS + n - 1)
                            probs_v(*multiplying, j, (n - 1) % 2)

            def tail():
                b = BATCHES
                misc_work("U", b, 0, 0)
                pe.wait_ge(exp_done, b * GROUPS * GR)
                pe.wait_ge(pv_copied, b * GROUPS - 1)
                for i in range(TILES):
                    probs_v(b - 1, 1, GROUPS - 1, i, (GROUPS - 1) % 2)
                for kind, n, _ in ORDER:
                    if present(kind, n, b) and (kind, n) != ("U", 0):
                        misc_work(kind, b, 0, n)

                def step(q, r):
                    if block_at(q, r, 2):
                        k, _, _ = block_at(q, r, 2)
                        par = r % 2
                        if isinstance(k, int) and k == 0:
                            pe.wait_ge(experts_loaded, 4 * 16)
                        e = pe.value_load(expert_of[0:1, k:k + 1] if isinstance(k, int)
                                          else expert_of[0:1, bass.ds(k, 1)], min_val=0, max_val=EXPERTS - 1)
                        pe.wait_ge(gelu_done, k + 1)
                        if not (isinstance(k, int) and k < 2):
                            pe.wait_ge(z_ready, k - 1)
                        nc.tensor.matmul(y_bank[par][:, 0:D], ones[0:1, :],
                                         b2_row[:, bass.ds(e, 1), :].rearrange("p a d -> p (a d)"),
                                         start=True, stop=False)
                        for c in range(FCH):
                            mm = nc.tensor.matmul(y_bank[par][:, 0:D], hidden_t[:, par, c * P:(c + 1) * P],
                                                  w2_all[:, bass.ds(e, 1), c, :].rearrange("p a d -> p (a d)"),
                                                  start=False, stop=(c == FCH - 1))
                        mm.then_inc(y_filled, 1)
                    for at in ([block_at(q, r, 0)] if isinstance(q, int) and q * NX + r == 0 else []) + [
                            block_at(q, r, -1)]:
                        if at is None:
                            continue
                        k, buf, turn = at
                        pe.wait_ge(rows_loaded[buf], (turn + 1) * 16)
                        if not (isinstance(k, int) and k < 2):
                            pe.wait_ge(turn_copied, k - 1)
                        nc.tensor.transpose(turn_bank[buf % 2][:, 0:P], block_rows[:, buf, 0:D], ident[:, :]
                                            ).then_inc(turned, 1)
                    if block_at(q, r, 0):
                        k, buf, _ = block_at(q, r, 0)
                        par = r % 2
                        pe.wait_ge(turn_copied, k + 1)
                        pe.wait_ge(w1_copied, k + 1)
                        if not (isinstance(k, int) and k < 2):
                            pe.wait_ge(gelu_done, k - 1)
                        for c in range(FCH):
                            mm = nc.tensor.matmul(hidden_bank[par][:, c * P:(c + 1) * P],
                                                  w1_now[:, par, c * P:(c + 1) * P], block_t[:, par, :],
                                                  start=True, stop=True)
                        mm.then_inc(hidden_filled, 1)

                pe.wait_ge(plan_step, PLAN_STEPS)
                pe.wait_ge(exp_done, BATCHES * GROUPS * GR)
                pe.wait_ge(s_reduced, BATCHES * GROUPS * GR)
                run_steps(pe, LAG + 2, step)

            run_batches(pe, batch, tail)

        @block.scalar
        def _(act):
            def lead(b, side):
                if is_first(b):
                    act.wait_ge(*((misc_filled, 1), (k0_projected, 1))[side])
                else:
                    act.wait_ge(misc_filled, emptied("qk"[side], 0, b - 1))
                    for part in range(PARTS):
                        act.wait_ge(parts_stored[part], b * (STORES[part] * 16))
                source = s_bank[0] if is_first(b) and side else misc
                nc.scalar.activation(qk_parts[:, 0, side, :], source[:, 0:L], ACT.Identity,
                                     bias=bqk[:, side:side + 1]).then_inc(qk_hi, 1)

            def middle(b, side):
                if is_first(b):
                    act.wait_ge(*((misc_emptied, 1), (k0_rest, 1))[side])
                else:
                    act.wait_ge(misc_emptied, emptied("qk"[side], 0, b - 1))
                nc.scalar.activation(qk_parts[:, 1, side, :], qk_rest[:, side, :], ACT.Copy).then_inc(mid_ready, 1)

            def copy_shift(g, index):
                b, par, n = g
                number = b * GROUPS + n
                act.wait_ge(misc_filled, index + 1)
                if not (is_first(b) and n < 2):
                    act.wait_ge(shift_loaded, (number - 1) * (PARTS * 16))
                nc.scalar.activation(shift_t[:, n % 2, :], misc_bf[0:PARTS * GR, 0:P], ACT.Copy
                                     ).then_inc(misc_emptied, 1)

            def copy_pv(g):
                b, par, n = g
                act.wait_ge(pv_done, b * GROUPS + n + 1)
                nc.scalar.activation(pv_copy[:, n % 2, :], pv_bank[:, :], ACT.Copy).then_inc(pv_copied, 1)

            def exps(b, par, n, j, i):
                number = (b * GROUPS + n) * GR + j * TILES + i
                act.wait_ge(st_filled, number + 1)
                if j == 0 and i == 0 and behind(b, par, n, 2):
                    act.wait_ge(pv_done, b * GROUPS + n - 1)
                nc.scalar.activation(probs[:, n % 2, j, i, :], bank_of(st_bank, j, i)[0][:, :],
                                     ACT.Exp, scale=SCALE).then_inc(exp_done, 1)

            def misc_copy(kind, b, par, n):
                if kind not in ("sh", "headsT", "x1T", "logits"):
                    return
                index = misc_before(kind, n, b)
                if kind == "sh":
                    copy_shift(ahead(b, par, n, 1), index)
                else:
                    target, source = {
                        "headsT": (heads_t[:, :], misc[:, 0:L]),
                        "x1T": (x1_t[:, :], misc[:, 0:L]),
                        "logits": (logits[:, :, :], misc_lg)}[kind]
                    act.wait_ge(misc_filled, index + 1)
                    if kind == "logits" and not (isinstance(b, int) and b == 1):
                        act.wait_ge(below_ready, b - 1)
                    nc.scalar.activation(target, source, ACT.Copy).then_inc(misc_emptied, 1)

            def router_exp(b):
                act.wait_ge(below_ready, b)
                if not (isinstance(b, int) and b == 1):
                    act.wait_ge(sum_ready, b - 1)
                nc.scalar.activation(prob[:, :, :], below[:, :, :], ACT.Exp).then_inc(prob_ready, 1)

            act.wait_ge(tables_warm, 1)
            nc.scalar.activation(warm[:, :], warm[:, :], ACT.Exp).then_inc(tables_warm, 1)
            act.wait_ge(qkv_loaded, 2 * 16)
            for side in range(2):
                lead(0, side)
            for side in range(2):
                middle(0, side)
            copy_shift((0, 0, 0), 2)

            def batch(b, par, pairs):
                for n in range(GROUPS):
                    if behind(b, par, n, 2):
                        copy_pv(behind(b, par, n, 2))
                    for j in range(GH):
                        for i in range(TILES):
                            exps(b, par, n, j, i)
                            at = (n, j, i)
                            if not is_last(b):
                                if at in ((0, 0, 2), (0, 2, 2)):
                                    lead(b + 1, j // 2)
                                elif at in ((0, 1, 2), (0, 3, 2)):
                                    middle(b + 1, j // 2)
                            if at == (3, 2, 2) and not is_first(b):
                                router_exp(b)
                        misc_copy(slot_of(n, j, b), b, par, n)

            def tail():
                b = BATCHES
                copy_pv((b - 1, 1, GROUPS - 2))
                copy_pv((b - 1, 1, GROUPS - 1))
                for kind, n, _ in ORDER:
                    if present(kind, n, b):
                        misc_copy(kind, b, 0, n)
                        if kind == "logits":
                            router_exp(b)

                def copy_turned(k, par):
                    act.wait_ge(turned, k + 1)
                    if not (isinstance(k, int) and k < 2):
                        act.wait_ge(hidden_filled, k - 1)
                    nc.scalar.activation(block_t[:, par, :], turn_bank[par][:, 0:P], ACT.Copy
                                         ).then_inc(turn_copied, 1)

                def copy_w1(k, par):
                    e = act.value_load(expert_of[0:1, k:k + 1] if isinstance(k, int)
                                       else expert_of[0:1, bass.ds(k, 1)], min_val=0, max_val=EXPERTS - 1)
                    if not (isinstance(k, int) and k < 2):
                        act.wait_ge(gelu_done, k - 1)
                    nc.scalar.activation(b1_now[:, par, :], b1_t[:, bass.ds(e, 1), :].rearrange("p a c -> p (a c)"),
                                         ACT.Copy).then_inc(b1_copied, 1)
                    nc.scalar.activation(w1_now[:, par, :], w1_all[:, bass.ds(e, 1), :].rearrange("p a f -> p (a f)"),
                                         ACT.Copy).then_inc(w1_copied, 1)

                def step(q, r):
                    par = r % 2
                    if isinstance(q, int) and q * NX + r == 0:
                        copy_w1(0, 0)
                        copy_turned(0, 0)
                    if block_at(q, r, -1):
                        k, _, _ = block_at(q, r, -1)
                        copy_w1(k, 1 - par)
                        copy_turned(k, 1 - par)
                    if block_at(q, r, 0):
                        k, _, _ = block_at(q, r, 0)
                        act.wait_ge(b1_copied, k + 1)
                        act.wait_ge(hidden_filled, k + 1)
                        if not (isinstance(k, int) and k < 2):
                            act.wait_ge(y_filled, k - 1)
                        for c in range(FCH):
                            done = nc.scalar.activation(
                                hidden_t[:, par, c * P:(c + 1) * P], hidden_bank[par][:, c * P:(c + 1) * P],
                                ACT.Gelu, bias=b1_now[:, par, c:c + 1])
                        done.then_inc(gelu_done, 1)

                act.wait_ge(plan_step, 1)
                act.wait_ge(tables_built, TABLES)
                for e in range(EXPERTS // 2, EXPERTS):
                    end = act.value_load(region_end[0:1, e:e + 1], min_val=0, max_val=EXPERTS * REGION)
                    act.dma_start(scratch[bass.ds(end, P), :], pad_rows[:, :]).then_inc(padded, 16)
                act.wait_ge(tables_warm, 2)
                nc.scalar.activation(warm[:, :], warm[:, :], ACT.Gelu).then_inc(tables_warm, 1)
                act.wait_ge(plan_step, PLAN_STEPS)
                act.wait_ge(experts_loaded, 4 * 16)
                run_steps(act, LAG + 2, step)

            run_batches(act, batch, tail)

        @block.vector
        def _(dve):
            def reduce(b, par, n, j, i):
                number = (b * GROUPS + n) * GR + j * TILES + i
                dve.wait_ge(s_filled, number + 1)
                if j == 0 and i == 0 and not (is_first(b) and n < 2):
                    dve.wait_ge(shift_step, (b * GROUPS + n - 1) * 4)
                nc.vector.reduce_max(maxima[:, n % 2, j * TILES + i:j * TILES + i + 1], bank_of(s_bank, j, i)[0][:, :],
                                     AXIS_X).then_inc(s_reduced, 1)

            def split_rest(b, side):
                dve.wait_ge(qk_hi, b * 2 + side + 1)
                if not is_first(b):
                    dve.wait_ge(lo_ready, b * 2)
                source = s_bank[0] if is_first(b) and side else misc
                nc.vector.scalar_tensor_tensor(
                    out=qk_rest[:, side, :], in0=source[:, 0:L], scalar=bqk[:, side:side + 1],
                    in1=qk_parts[:, 0, side, :], op0=ALU.add, op1=ALU.subtract
                    ).then_inc(k0_rest if is_first(b) and side else misc_emptied, 1)

            def split_last(side):
                dve.wait_ge(mid_ready, side + 1)
                nc.vector.tensor_tensor(qk_parts[:, 2, side, :], qk_rest[:, side, :], qk_parts[:, 1, side, :],
                                        ALU.subtract).then_inc(lo_ready, 1)

            def copy_v(b, par, index):
                dve.wait_ge(misc_filled, index + 1)
                if is_first(b):
                    dve.wait_ge(ones_col, 2)
                    dve.wait_ge(consts_loaded, 4 * 16)
                bias = bv[:, :].rearrange("p (a h c) -> p a h c", a=1, c=CH).broadcast_to([P, TILES, HEADS, CH])
                nc.vector.tensor_tensor(v_stack[:, par, :, :, 0:CH], misc_v, bias, ALU.add).then_inc(misc_emptied, 1)

            def invert(g, index):
                dve.wait_ge(misc_filled, index + 1)
                nc.vector.reciprocal(recip[:, :, :], misc_h[:, :, :, CH]).then_inc(recip_ready, 1)

            def normalise_heads(g):
                b, par, n = g
                dve.wait_ge(recip_ready, b * GROUPS + n + 1)
                over = recip[:, :, :].rearrange("p t (g a) -> p t g a", a=1).broadcast_to([P, TILES, GH, CH])
                nc.vector.tensor_tensor(
                    heads[:, :, n * GH * CH:(n + 1) * GH * CH].rearrange("p t (g c) -> p t g c", c=CH),
                    misc_h[:, :, :, 0:CH], over, ALU.mult).then_inc(misc_emptied, 1)

            def add_residual(b, par, index):
                dve.wait_ge(misc_filled, index + 1)
                dve.wait_ge(x2b_ready, b * 2)
                if not (isinstance(b, int) and b == 1):
                    dve.wait_ge(x1_ready, (b - 1) * TILES)
                nc.vector.tensor_tensor(resid[:, :, :], misc_td, x2b[:, 1 - par], ALU.add).then_inc(misc_emptied, 1)

            def statistics(b, t):
                if t == 0:
                    dve.wait_ge(misc_emptied, emptied("proj", 1, b))
                nc.vector.bn_stats(stats[:, t, :], resid[:, t, :]).then_inc(stats_ready, 1)

            def aggregate(b, t):
                if t == 0:
                    dve.wait_ge(stats_ready, b * TILES)
                    if not (isinstance(b, int) and b == 1):
                        dve.wait_ge(x1_ready, (b - 1) * TILES)
                    stand_apart(dve)
                nc.vector.bn_aggr(mean_var[:, t, :], stats[:, t, :]).then_inc(aggr_ready, 1)

            def normalise(b, par, pairs, t):
                if t == 0:
                    dve.wait_ge(rstd_ready, b)
                    dve.wait_ge(scattered[1 - par], pairs * (TILES * 16))
                nc.vector.tensor_scalar(rows[:, 1 - par, t, 0:D], resid[:, t, :], mean_var[:, t, 0:1],
                                        rstd[:, t:t + 1], ALU.subtract, ALU.mult).then_inc(x1_ready, 1)

            def spread(ap):
                return ap.rearrange("p (t a) -> p t a", a=1).broadcast_to([P, TILES, EXPERTS])

            ROUTE_STEPS = 6

            def route(b, step):
                if step == 0:
                    dve.wait_ge(misc_emptied, emptied("logits", 3, b))
                    nc.vector.reduce_max(top[:, :], logits[:, :, :], AXIS_X).then_inc(top_ready, 1)
                elif step == 1:
                    dve.wait_ge(top_ready, b)
                    nc.vector.tensor_tensor(is_top[:, :, :], logits[:, :, :], spread(top[:, :]), ALU.is_equal
                                            ).then_inc(istop_ready, 1)
                elif step == 2:
                    dve.wait_ge(istop_ready, b)
                    nc.vector.scalar_tensor_tensor(out=key[:, :, :], in0=is_top[:, :, :], scalar=-float(EXPERTS),
                                                   in1=expert_no[:, :, :], op0=ALU.mult, op1=ALU.add
                                                   ).then_inc(key_ready, 1)
                elif step == 3:
                    dve.wait_ge(key_ready, b)
                    nc.vector.tensor_reduce(first[:, :], key[:, :, :], AXIS_X, ALU.min).then_inc(first_ready, 1)
                elif step == 4:
                    dve.wait_ge(first_ready, b)
                    if not (isinstance(b, int) and b == 1):
                        dve.wait_ge(place_own, b - 1)
                    nc.vector.tensor_tensor(one_hot[:, :, :], key[:, :, :], spread(first[:, :]), ALU.is_equal
                                            ).then_inc(onehot_ready, 1)
                elif step == 5:
                    if not (isinstance(b, int) and b == 1):
                        dve.wait_ge(prob_ready, b - 1)
                    nc.vector.tensor_tensor(below[:, :, :], logits[:, :, :], spread(top[:, :]), ALU.subtract
                                            ).then_inc(below_ready, 1)

            def count_on(b, par, step):
                if step == 0:
                    dve.wait_ge(misc_filled, emptied("counts", 3, b))
                    if isinstance(b, int) and b == 1:
                        dve.wait_ge(base_ready, 2)
                    else:
                        dve.wait_ge(place_summed, b - 1)
                    before_batch = base[:, par, :].rearrange("p (a e) -> p a e", a=1)
                    nc.vector.tensor_tensor(place[:, :, :], misc_counts[:, 0:TILES, :],
                                            before_batch.broadcast_to([P, TILES, EXPERTS]), ALU.add
                                            ).then_inc(placed, 1)
                    nc.vector.tensor_tensor(base[:, 1 - par, :], misc_counts[:, TILES, :], base[:, par, :],
                                            ALU.add).then_inc(misc_emptied, 1)
                elif step == 1:
                    dve.wait_ge(placed, b)
                    nc.vector.tensor_tensor(place[:, :, :], place[:, :, :], one_hot[:, :, :], ALU.mult
                                            ).then_inc(place_own, 1)
                else:
                    dve.wait_ge(place_own, b)
                    if not (isinstance(b, int) and b == 1):
                        dve.wait_ge(slot_ready, b - 1)
                    nc.vector.tensor_reduce(own_place[:, :], place[:, :, :], AXIS_X, ALU.add
                                            ).then_inc(place_summed, 1)

            def weigh(b, par, step):
                if step == 0:
                    dve.wait_ge(prob_ready, b)
                    if not (isinstance(b, int) and b == 1):
                        dve.wait_ge(weight_ready, b - 1)
                    nc.vector.tensor_reduce(prob_sum[:, :], prob[:, :, :], AXIS_X, ALU.add).then_inc(sum_ready, 1)
                else:
                    dve.wait_ge(sum_ready, b)
                    nc.vector.reciprocal(rows[:, 1 - par, :, D], prob_sum[:, :]).then_inc(weight_ready, 1)

            def misc_use(kind, b, par, n, step):
                if kind is None:
                    return
                index = misc_before(kind, n, b)
                if kind == "U":
                    g = behind(b, par, n, 2) if not (isinstance(b, int) and b == BATCHES) else (b - 1, 1 - par, n + 2)
                    (invert(g, index) if step == 0 else normalise_heads(g))
                elif kind in ("q", "k"):
                    if step == 1:
                        split_rest(b + 1, int(kind == "k"))
                elif kind == "counts":
                    count_on(b, par, step)
                elif step == 1:
                    return
                elif kind == "v":
                    copy_v(b + 1, 1 - par, index)
                elif kind == "proj":
                    add_residual(b, par, index)

            nc.vector.memset(q32[64:128, 0], 0).then_inc(stacks_cleared, 1)
            for side in range(2):
                split_rest(0, side)
            split_last(0)
            copy_v(0, 0, 1)
            split_last(1)
            for j in range(GH):
                for i in range(TILES):
                    reduce(0, 0, 0, j, i)
            for j in range(GH):
                for i in range(TILES):
                    reduce(0, 0, 1, j, i)
            reduce(0, 0, 2, 0, 0)

            def batch(b, par, pairs):
                for n in range(GROUPS):
                    maxing = ahead(b, par, n, 2)
                    for j in range(GH):
                        following = maxing if j < GH - 1 else ahead(b, par, n, 3)
                        for i in range(TILES):
                            if i < TILES - 1 and maxing:
                                reduce(*maxing, j, i + 1)
                            if i == TILES - 1 and following:
                                reduce(*following, (j + 1) % GH, 0)
                            if i >= 2:
                                misc_use(slot_of(n, j, b), b, par, n, i - 2)
                            if not is_first(b):
                                at = (n * GH + j) * TILES + i
                                begin, combining, routing = 2 * GH * TILES - 1, (2 * GH + 1) * TILES, (3 * GH + 1) * TILES
                                if begin <= at < begin + TILES // 2:
                                    for t in range(2):
                                        statistics(b, (at - begin) * 2 + t)
                                elif at == combining:
                                    for t in range(TILES):
                                        aggregate(b, t)
                                elif routing <= at < routing + ROUTE_STEPS:
                                    route(b, at - routing)
                                elif at in (GROUPS * GR - 3, GROUPS * GR - 2):
                                    weigh(b, par, at - (GROUPS * GR - 3))
                if not is_first(b):
                    count_on(b, par, 2)

            def tail():
                b = BATCHES
                for kind, n, _ in ORDER:
                    if present(kind, n, b):
                        for step in range(2):
                            misc_use(kind, b, 0, n, step)
                        if kind == "proj":
                            for t in range(TILES):
                                statistics(b, t)
                            for t in range(TILES):
                                aggregate(b, t)
                            for t in range(TILES):
                                normalise(b, 0, (b - 1) // 2, t)
                        if kind == "logits":
                            for step in range(ROUTE_STEPS):
                                route(b, step)
                count_on(b, 0, 2)
                for step in range(2):
                    weigh(b, 0, step)
                plan_blocks()
                run_steps(dve, LAG + 2, expert_step)

            def plan_blocks():
                done = 0

                def then(instruction):
                    nonlocal done
                    done += 1
                    instruction.then_inc(plan_step, 1)
                    dve.wait_ge(plan_step, done)

                def over_blocks(ap):
                    return ap.rearrange("p (a e) -> p a e", a=1).broadcast_to([1, NBLK, EXPERTS])

                dve.wait_ge(misc_emptied, emptied("counts", 3, BATCHES))
                dve.wait_ge(tables_built, TABLES)
                ends = base[0:1, 1, :]
                then(nc.vector.tensor_copy(region_end[:, :], ends))
                then(nc.vector.scalar_tensor_tensor(out=held[:, :], in0=expert_no[0:1, 0, :], scalar=-float(REGION),
                                                    in1=ends, op0=ALU.mult, op1=ALU.add))
                then(nc.vector.tensor_tensor(
                    begun[:, :, :], held[:, :].rearrange("p (e a) -> p e a", a=1).broadcast_to(
                        [1, EXPERTS, TOKENS // P]), full_at[:, :, :], ALU.is_gt))
                then(nc.vector.tensor_reduce(blocks[:, :], begun[:, :, :], AXIS_X, ALU.add))
                then(nc.vector.tensor_tensor(
                    upto_blocks[:, :, :], up_to[:, :, :], blocks[:, :].rearrange("p (a e) -> p a e", a=1
                                                                                 ).broadcast_to([1, EXPERTS, EXPERTS]),
                    ALU.mult))
                then(nc.vector.tensor_reduce(last_block[:, :], upto_blocks[:, :, :], AXIS_X, ALU.add))
                then(nc.vector.tensor_tensor(passed[:, :, :], block_no[:, :, :], over_blocks(last_block[:, :]),
                                             ALU.is_ge))
                then(nc.vector.tensor_reduce(sums[:, 0, :], passed[:, :, :], AXIS_X, ALU.add))
                then(nc.vector.tensor_scalar(expert_of[:, :], sums[:, 0, :], float(EXPERTS - 1), None, ALU.min))
                then(nc.vector.tensor_scalar(hole[:, :], blocks[:, :], -float(P), float(REGION), ALU.mult, ALU.add))
                then(nc.vector.tensor_tensor(holes[:, :, :], passed[:, :, :], over_blocks(hole[:, :]), ALU.mult))
                then(nc.vector.tensor_reduce(sums[:, 1, :], holes[:, :, :], AXIS_X, ALU.add))
                then(nc.vector.scalar_tensor_tensor(out=row_of[:, :], in0=block_no[:, :, 0], scalar=float(P),
                                                    in1=sums[:, 1, :], op0=ALU.mult, op1=ALU.add))
                assert done == PLAN_STEPS

            def expert_step(q, r):
                par = r % 2
                two, three = block_at(q, r, 2), block_at(q, r, 3)
                if two:
                    k, buf, turn = two
                    dve.wait_ge(rows_loaded[buf], (turn + 1) * 16)
                    if not (isinstance(k, int) and k < 2):
                        dve.wait_ge(out_ready, k - 1)
                    dve.wait_ge(y_filled, k + 1)
                    nc.vector.scalar_tensor_tensor(out=z_now[:, par, :], in0=y_bank[par][:, 0:D],
                                                   scalar=block_rows[:, buf, D:D + 1],
                                                   in1=block_rows[:, buf, 0:D], op0=ALU.mult, op1=ALU.add
                                                   ).then_inc(z_ready, 1)
                if three:
                    k, buf, turn = three
                    if not (isinstance(k, int) and k < 2):
                        dve.wait_ge(out_stored[1 - par], (turn * (NX // 2) + buf // 2) * 16)
                    dve.wait_ge(z_rstd, k + 1)
                    nc.vector.tensor_scalar(out_rows[:, 1 - par, :], z_now[:, 1 - par, :],
                                            sq_mean_var[:, 1 - par, 0:1], sq_rstd[:, 1 - par:2 - par],
                                            ALU.subtract, ALU.mult).then_inc(out_ready, 1)
                if two:
                    k, buf, turn = two
                    dve.wait_ge(z_ready, k + 1)
                    nc.vector.bn_stats(sq_stats[:, par, :], z_now[:, par, :]).then_inc(z_stats, 1)
                    dve.wait_ge(z_stats, k + 1)
                    stand_apart(dve)
                    nc.vector.bn_aggr(sq_mean_var[:, par, :], sq_stats[:, par, :]).then_inc(z_aggr, 1)
                    dve.wait_ge(z_aggr, k + 1)
                    nc.vector.tensor_scalar(sq_var[:, par:par + 1], sq_mean_var[:, par, 1:2], EPS, None, ALU.add
                                            ).then_inc(z_var, 1)

            run_batches(dve, batch, tail)

        @block.gpsimd
        def _(pool):
            nc.gpsimd.memset(warm[:, :], 0.0).then_inc(tables_warm, 1)
            nc.gpsimd.memset(v_stack[:, 0], 0.0).then_inc(ones_col, 1)
            pool.wait_ge(ones_col, 1)
            nc.gpsimd.memset(v_stack[:, 0, :, :, CH:CH + 1], 1.0).then_inc(ones_col, 1)
            pool.wait_ge(ones_col, 2)
            nc.gpsimd.memset(k32[64:128, 0], MINUS_ONES_BF16).then_inc(stacks_cleared, 1)
            pool.wait_ge(stacks_cleared, 2)

            def split_last(b, side):
                pool.wait_ge(mid_ready, b * 2 + side + 1)
                nc.gpsimd.tensor_tensor(qk_parts[:, 2, side, :], qk_rest[:, side, :], qk_parts[:, 1, side, :],
                                        ALU.subtract).then_inc(lo_ready, 1)

            nc.gpsimd.memset(ones[:, :], 1.0).then_inc(base_ready, 1)
            pool.wait_ge(base_ready, 1)
            nc.gpsimd.affine_select(out=ident[:, :], in_=ones[:, :], compare_op=ALU.is_equal, fill=0.0, base=0,
                                    pattern=[[-1, P]], channel_multiplier=1).then_inc(consts_built, 1)
            nc.gpsimd.affine_select(out=ident_bf[:, :], in_=ones[:, :], compare_op=ALU.is_equal, fill=0.0, base=0,
                                    pattern=[[-1, P]], channel_multiplier=1).then_inc(consts_built, 1)
            nc.gpsimd.affine_select(out=before[:, :], in_=ones[:, :], compare_op=ALU.is_gt, fill=0.0, base=0,
                                    pattern=[[1, P]], channel_multiplier=-1).then_inc(consts_built, 1)
            nc.gpsimd.iota(expert_no[:, :, :], pattern=[[0, TILES], [1, EXPERTS]], base=0, channel_multiplier=0,
                           allow_small_or_imprecise_dtypes=True).then_inc(consts_built, 1)
            nc.gpsimd.iota(token_no[:, :], pattern=[[P, TOKENS // P]], base=0, channel_multiplier=1
                           ).then_inc(consts_built, 1)
            nc.gpsimd.memset(minus_half[:, :], -0.5).then_inc(consts_built, 1)
            nc.gpsimd.memset(ones_bf[:, :], 1.0).then_inc(consts_built, 1)
            pool.wait_ge(consts_built, CONSTS)
            nc.gpsimd.memset(q32[64:128, 1], 0).then_inc(stacks1_cleared, 1)
            nc.gpsimd.memset(k32[64:128, 1], MINUS_ONES_BF16).then_inc(stacks1_cleared, 1)
            pool.wait_ge(stacks1_cleared, 2)
            nc.gpsimd.memset(v_stack[:, 1], 0.0).then_inc(ones_col, 1)
            pool.wait_ge(ones_col, 3)
            nc.gpsimd.memset(v_stack[:, 1, :, :, CH:CH + 1], 1.0).then_inc(ones_col, 1)
            nc.gpsimd.iota(base[:, 1, :], pattern=[[REGION, EXPERTS]], base=0, channel_multiplier=0,
                           allow_small_or_imprecise_dtypes=True).then_inc(base_ready, 1)
            nc.gpsimd.iota(block_no[:, :, :], pattern=[[1, NBLK], [0, EXPERTS]], base=0, channel_multiplier=0,
                           allow_small_or_imprecise_dtypes=True).then_inc(tables_built, 1)
            nc.gpsimd.iota(full_at[:, :, :], pattern=[[0, EXPERTS], [P, TOKENS // P]], base=0, channel_multiplier=0,
                           allow_small_or_imprecise_dtypes=True).then_inc(tables_built, 1)
            nc.gpsimd.affine_select(out=up_to[:, :, :], in_=ones[0:1, 0:EXPERTS * EXPERTS].rearrange(
                "p (e f) -> p e f", e=EXPERTS), compare_op=ALU.is_ge, fill=0.0, base=0,
                pattern=[[1, EXPERTS], [-1, EXPERTS]], channel_multiplier=0).then_inc(tables_built, 1)
            nc.gpsimd.memset(pad_rows[:, 0:D + 1], 0.0).then_inc(tables_built, 1)
            nc.gpsimd.iota(pad_rows[:, D + 1:D + 2].bitcast(U32), pattern=[[0, 1]], base=TOKENS, channel_multiplier=1
                           ).then_inc(tables_built, 1)
            pool.wait_ge(consts_loaded, 4 * 16)
            pool.wait_ge(consts_built, CONSTS)

            def place_rows(b, par):
                pool.wait_ge(place_summed, b)
                stand_apart(pool)
                nc.gpsimd.tensor_copy(slot[:, 1 - par, :], own_place[:, :]).then_inc(slot_ready, 1)

            def scatter(b, par):
                pool.wait_ge(slot_ready, b)
                pool.wait_ge(weight_ready, b)
                pool.wait_ge(x1_ready, b * TILES)
                pool.wait_ge(id_ready, b)
                stand_apart(pool)
                for t in range(TILES):
                    nc.gpsimd.indirect_dma_start(
                        scratch, bass.IndirectOffsetOnAxis(ap=slot[:, 1 - par, t:t + 1], axis=0),
                        rows[:, 1 - par, t, :], None).then_inc(scattered[1 - par], 16)

            def row_work(b, par, pairs):
                pool.wait_ge(aggr_ready, b * TILES)
                if not (isinstance(b, int) and b == 1):
                    pool.wait_ge(x1_ready, (b - 1) * TILES)
                stand_apart(pool)
                nc.gpsimd.tensor_scalar_add(var_eps[:, :], mean_var[:, :, 1], EPS).then_inc(vareps_ready, 1)
                pool.wait_ge(vareps_ready, b)
                nc.gpsimd.tensor_tensor(rstd[:, :], var_eps[:, :], minus_half[:, :], ALU.pow).then_inc(rstd_ready, 1)
                pool.wait_ge(scattered[1 - par], pairs * (TILES * 16))
                stand_apart(pool)
                numbers = (token_no[:, (b - 1) * TILES:b * TILES] if isinstance(b, int)
                           else token_no[:, bass.ds((b - 1) * TILES, TILES)])
                nc.gpsimd.tensor_copy(rows[:, 1 - par, :, :].bitcast(U32)[:, :, D + 1], numbers).then_inc(id_ready, 1)

            def normalise(b, par):
                pool.wait_ge(rstd_ready, b)
                stand_apart(pool)
                for t in range(TILES):
                    nc.gpsimd.tensor_scalar(rows[:, 1 - par, t, 0:D], resid[:, t, :], mean_var[:, t, 0:1],
                                            rstd[:, t:t + 1], ALU.subtract, ALU.mult).then_inc(x1_ready, 1)

            def split_shift(g, turned=None):
                b, par, n = g
                number = b * GROUPS + n
                pool.wait_ge(s_reduced, (number + 1) * GR)
                if turned is not None:
                    pool.wait_ge(misc_filled, turned)
                stand_apart(pool)
                nc.gpsimd.tensor_copy(shift[:, 0, :], maxima[:, n % 2, :]).then_inc(shift_step, 1)
                pool.wait_ge(shift_step, number * 4 + 1)
                nc.gpsimd.tensor_tensor(shift_rest[:, :], maxima[:, n % 2, :], shift[:, 0, :], ALU.subtract
                                        ).then_inc(shift_step, 1)
                pool.wait_ge(shift_step, number * 4 + 2)
                stand_apart(pool)
                nc.gpsimd.tensor_copy(shift[:, 1, :], shift_rest[:, :]).then_inc(shift_step, 1)
                pool.wait_ge(shift_step, number * 4 + 3)
                nc.gpsimd.tensor_tensor(shift[:, 2, :], shift_rest[:, :], shift[:, 1, :], ALU.subtract
                                        ).then_inc(shift_step, 1)

            def next_shift(b, par, n):
                if ahead(b, par, n, 1):
                    turned = len(START) if is_first(b) and n == 0 else (
                        misc_before("q", 0, b) if n == 0 else emptied("sh", n - 1, b))
                    split_shift(ahead(b, par, n, 1), turned)

            def double_x(b, par):
                pool.wait_ge(x_loaded, (b + 1) * 16)
                if not is_first(b):
                    pool.wait_ge(misc_emptied, misc_before("q", 0, b))
                bias = bo[:, :].rearrange("p (a d) -> p a d", a=1).broadcast_to([P, TILES, D])
                nc.gpsimd.tensor_tensor(x2b[:, par], x_in[:, par], bias, ALU.add).then_inc(x2b_ready, 1)
                pool.wait_ge(x2b_ready, b * 2 + 1)
                nc.gpsimd.tensor_tensor(x2b[:, par], x2b[:, par], x_in[:, par], ALU.add).then_inc(x2b_ready, 1)

            split_shift((0, 0, 0))

            def batch(b, par, pairs):
                next_shift(b, par, 0)
                if not (isinstance(b, int) and b < 2):
                    place_rows(b - 1, 1 - par)
                    scatter(b - 1, 1 - par)
                if not is_last(b):
                    split_last(b + 1, 0)
                double_x(b, par)
                if not is_last(b):
                    split_last(b + 1, 1)
                next_shift(b, par, 1)
                next_shift(b, par, 2)
                if not is_first(b):
                    row_work(b, par, pairs)
                    normalise(b, par)
                next_shift(b, par, 3)

            def tail():
                place_rows(BATCHES - 1, 1)
                scatter(BATCHES - 1, 1)
                row_work(BATCHES, 0, (BATCHES - 1) // 2)
                place_rows(BATCHES, 0)
                scatter(BATCHES, 0)

                def step(q, r):
                    par = r % 2
                    if block_at(q, r, 1):
                        k, buf, _ = block_at(q, r, 1)
                        pool.wait_ge(out_ready, k + 1)
                        stand_apart(pool)
                        nc.gpsimd.indirect_dma_start(
                            out_flat, bass.IndirectOffsetOnAxis(
                                ap=block_rows[:, buf, D + 1:D + 2].bitcast(U32), axis=0),
                            out_rows[:, 1 - par, :], None, bounds_check=TOKENS - 1, oob_is_err=False
                            ).then_inc(out_stored[1 - par], 16)
                    if block_at(q, r, 0):
                        k, _, _ = block_at(q, r, 0)
                        pool.wait_ge(z_var, k + 1)

                        if not (isinstance(k, int) and k < 2):
                            pool.wait_ge(out_ready, k - 1)
                        stand_apart(pool)
                        nc.gpsimd.tensor_tensor(sq_rstd[:, par:par + 1], sq_var[:, par:par + 1], minus_half[:, 0:1],
                                                ALU.pow).then_inc(z_rstd, 1)

                run_steps(pool, LAG + 2, step)
                for par in range(2):
                    pool.wait_ge(out_stored[par], (NBLK + 1 - par) // 2 * 16)

            run_batches(pool, batch, tail)


def kernel(**inputs):
    import numpy as _np
    import concourse.bacc as _bacc
    from concourse import mybir as _mybir
    from concourse.bass_utils import run_bass_kernel_spmd as _run

    given = {name[3:].split("_", 1)[1]: _np.asarray(a) for name, a in inputs.items()}
    x, w_qkv, b_qkv = given["x"], given["w_qkv"], given["b_qkv"]
    D = x.shape[-1]
    HEADS = 16
    order = _np.arange(D).reshape(HEADS, D // HEADS).T.reshape(-1)
    order = _np.concatenate([order, D + order, _np.arange(2 * D, 3 * D)])
    arrays = {"x": x, "x_t": x.transpose(0, 2, 1), "w_qkv_t": w_qkv[order].T, "b_qkv": b_qkv[order],
              "w_o_t": given["w_o"].T, "b_o": given["b_o"], "gate_w": given["gate_w"],
              "w1": given["w1"], "b1": given["b1"], "w2": given["w2"], "b2": given["b2"]}

    nc = _bacc.Bacc("TRN2", target_bir_lowering=False, num_devices=1)
    args = []
    for name in list(arrays):
        a = _np.ascontiguousarray(arrays.pop(name))
        arrays[f"in_{name}_dram"] = a
        args.append(nc.dram_tensor(f"in_{name}_dram", a.shape, _mybir.dt.from_np(a.dtype), kind="ExternalInput").ap())
    args.append(nc.dram_tensor("out_dram", x.shape, _mybir.dt.float32, kind="ExternalOutput").ap())
    build(nc, *args)
    r = _run(nc, [arrays], core_ids=[0])
    return r.results[0]["out_dram"]
```

```python
from contextlib import ExitStack

import concourse.bass as bass
from concourse import mybir

F32 = mybir.dt.float32
BF16 = mybir.dt.bfloat16
U32 = mybir.dt.uint32
I32 = mybir.dt.int32
ALU = mybir.AluOpType
ACT = mybir.ActivationFunctionType
AXIS_X = mybir.AxisListType.X

P = 128
EPS = 1e-5
MINUS_ONES_BF16 = 0xBF80BF80


def build(nc, x, x_t, w_qkv_t, b_qkv, w_o_t, b_o, gate_w, w1, b1, w2, b2, out):
    BATCHES, L, D = x.shape
    HEADS = 16
    CH = D // HEADS
    SCALE = 1.0 / float(D) ** 0.5
    TILES = L // P
    GH = 4
    GROUPS = HEADS // GH
    EXPERTS, _, FF = w1.shape
    FCH = FF // P
    TOKENS = BATCHES * L
    PARTS = 3
    BLOCKS9 = PARTS * PARTS
    ROWS_S = 96
    SHIFT_ROW = 96
    VW = 32
    GR = GH * TILES
    REGION = TOKENS + P
    NBLK = (TOKENS + EXPERTS * (P - 1)) // P
    ROW = D + 2
    SCRATCH_ROWS = EXPERTS * REGION + P * EXPERTS

    ctx = ExitStack()
    with ctx:
        def sb(name, shape, dt=F32):
            return ctx.enter_context(nc.sbuf_tensor(name, shape, dt))

        def psum(name, shape, dt=F32):
            return ctx.enter_context(nc.psum_tensor(name, shape, dt))

        def sem(name):
            return ctx.enter_context(nc.semaphore(name))

        Q_PARTS = 2 * PARTS - 1
        parts_dram = nc.dram_tensor("split_parts", [2, Q_PARTS + PARTS, CH, HEADS * L], BF16, kind="Internal").ap()
        scratch = nc.dram_tensor("routed_rows", [SCRATCH_ROWS, ROW], F32, kind="Internal").ap()

        warm = sb("warm", [P, 1])
        wqkv = sb("wqkv", [P, 3 * D])
        bqk = sb("bqk", [P, 2])
        bv = sb("bv", [P, D])
        wo = sb("wo", [P, D])
        bo = sb("bo", [P, D])
        gate = sb("gate", [P, EXPERTS])
        ident = sb("ident", [P, P])
        ident_bf = sb("ident_bf", [P, P], BF16)
        before = sb("before", [P, P], BF16)
        ones_bf = sb("ones_bf", [P, P], BF16)
        ones = sb("ones", [P, P])
        expert_no = sb("expert_no", [P, TILES, EXPERTS])
        token_no = sb("token_no", [P, TOKENS // P], U32)
        minus_half = sb("minus_half", [P, TILES])
        xt_in = sb("xt_in", [P, 2, L])
        x_in = sb("x_in", [P, 2, TILES, D])
        x2b = sb("x2b", [P, 2, TILES, D])
        qk_rest = sb("qk_rest", [P, 2, L])
        qk_parts = sb("qk_parts", [P, PARTS, 2, L], BF16)
        q_stack = sb("q_stack", [P, 2, HEADS, L], BF16)
        k_stack = sb("k_stack", [P, 2, HEADS, L], BF16)
        v_stack = sb("v_stack", [P, 2, TILES, HEADS, VW])
        probs = sb("probs", [P, 2, GH, TILES, L])
        maxima = sb("maxima", [P, 2, GR])
        shift_rest = sb("shift_rest", [P, GR])
        shift = sb("shift", [P, PARTS, GR], BF16)
        shift_t = sb("shift_t", [PARTS * GR, 2, P], BF16)
        pv_copy = sb("pv_copy", [P, 2, L])
        recip = sb("recip", [P, TILES, GH])
        heads = sb("heads", [P, TILES, D])
        heads_t = sb("heads_t", [P, L])
        resid = sb("resid", [P, TILES, D])
        stats = sb("stats", [P, TILES, 6])
        mean_var = sb("mean_var", [P, TILES, 2])
        var_eps = sb("var_eps", [P, TILES])
        rstd = sb("rstd", [P, TILES])
        rows = sb("rows", [P, 2, TILES, ROW])
        x1_t = sb("x1_t", [P, L])
        logits = sb("logits", [P, TILES, EXPERTS])
        key = sb("key", [P, TILES, EXPERTS])
        top = sb("top", [P, TILES])
        is_top = sb("is_top", [P, TILES, EXPERTS])
        below = sb("below", [P, TILES, EXPERTS])
        prob = sb("prob", [P, TILES, EXPERTS])
        first = sb("first", [P, TILES])
        one_hot = sb("one_hot", [P, TILES, EXPERTS], BF16)
        prob_sum = sb("prob_sum", [P, TILES])
        base = sb("base", [P, 2, EXPERTS])
        place = sb("place", [P, TILES, EXPERTS])
        own_place = sb("own_place", [P, TILES])
        slot = sb("slot", [P, 2, TILES], U32)

        b2_row = sb("b2_row", [1, EXPERTS, D])
        b1_t = sb("b1_t", [P, EXPERTS, FCH])
        pad_rows = sb("pad_rows", [P, ROW])
        block_no = sb("block_no", [1, NBLK, EXPERTS])
        full_at = sb("full_at", [1, EXPERTS, TOKENS // P])
        prior = sb("prior", [1, EXPERTS + 1, EXPERTS])
        region_row = sb("region_row", [1, EXPERTS + 1])
        held = sb("held", [1, EXPERTS])
        full = sb("full", [1, EXPERTS])
        begun = sb("begun", [1, EXPERTS, TOKENS // P])
        blocks = sb("blocks", [1, EXPERTS])
        prior_blocks = sb("prior_blocks", [1, EXPERTS + 1, EXPERTS])
        block_begin = sb("block_begin", [1, EXPERTS + 1])
        cut_begin = sb("cut_begin", [1, EXPERTS + 1])
        taken = sb("taken", [1, EXPERTS + 1])
        offset = sb("offset", [1, EXPERTS + 1])
        first_row = sb("first_row", [1, EXPERTS + 1])
        jump = sb("jump", [1, EXPERTS])
        passed = sb("passed", [1, NBLK, EXPERTS])
        jumps = sb("jumps", [1, NBLK, EXPERTS])
        sums = sb("sums", [1, 2, NBLK])
        expert_of = sb("expert_of", [1, NBLK], I32)
        row_of = sb("row_of", [1, NBLK], I32)
        region_end = sb("region_end", [1, EXPERTS], I32)
        out_mean_var = sb("out_mean_var", [P, 2, 2])
        out_stats = sb("out_stats", [P, 2, 6])
        out_rstd = sb("out_rstd", [P, 2])
        out_var = sb("out_var", [P, 2])

        s_bank = [psum(f"s_bank{i}", [P, L]) for i in range(3)]
        st_bank = [psum(f"st_bank{i}", [P, L]) for i in range(3)]
        pv_bank = psum("pv_bank", [P, L])
        misc = psum("misc", [P, 512])

        qkv_loaded = sem("qkv_loaded")
        consts_loaded = sem("consts_loaded")
        consts_built = sem("consts_built")
        tables_warm = sem("tables_warm")
        register_waited = sem("register_waited")
        stacks_cleared = sem("stacks_cleared")
        stacks1_cleared = sem("stacks1_cleared")
        base_ready = sem("base_ready")
        ones_col = sem("ones_col")
        x_loaded = sem("x_loaded")
        xt_loaded = sem("xt_loaded")
        qk_hi = sem("qk_hi")
        k0_projected = sem("k0_projected")
        k0_rest = sem("k0_rest")
        mid_ready = sem("mid_ready")
        lo_ready = sem("lo_ready")
        x2b_ready = sem("x2b_ready")
        s_filled = sem("s_filled")
        s_reduced = sem("s_reduced")
        shift_step = sem("shift_step")
        shift_loaded = sem("shift_loaded")
        st_filled = sem("st_filled")
        exp_done = sem("exp_done")
        pv_done = sem("pv_done")
        pv_copied = sem("pv_copied")
        recip_ready = sem("recip_ready")
        stats_ready = sem("stats_ready")
        aggr_ready = sem("aggr_ready")
        vareps_ready = sem("vareps_ready")
        rstd_ready = sem("rstd_ready")
        x1_ready = sem("x1_ready")
        top_ready = sem("top_ready")
        below_ready = sem("below_ready")
        istop_ready = sem("istop_ready")
        key_ready = sem("key_ready")
        first_ready = sem("first_ready")
        onehot_ready = sem("onehot_ready")
        prob_ready = sem("prob_ready")
        sum_ready = sem("sum_ready")
        weight_ready = sem("weight_ready")
        placed = sem("placed")
        place_own = sem("place_own")
        place_summed = sem("place_summed")
        slot_ready = sem("slot_ready")
        id_ready = sem("id_ready")
        misc_filled = sem("misc_filled")
        misc_emptied = sem("misc_emptied")

        scattered = [sem(f"scattered{i}") for i in range(2)]
        parts_stored = [sem(f"parts_stored{i}") for i in range(PARTS)]

        group0_loaded = sem("group0_loaded")
        stack_loaded = [sem(f"stack_loaded{i}") for i in range(2)]
        STACK_LOADS = 2
        STORES = [2 if part < PARTS - 1 else 1 for part in range(PARTS)]

        w1_all = q_stack[:, 0, :, :].rearrange("p h l -> p (h l)").bitcast(F32).rearrange(
            "p (e f) -> p e f", e=EXPERTS)
        w2_all = k_stack[:, 0, :, :].rearrange("p h l -> p (h l)").bitcast(F32).rearrange(
            "p (e c d) -> p e c d", e=EXPERTS, c=FCH)
        probs_flat = probs[:, :, :, :, :].rearrange("p a g t l -> p (a g t l)")
        NX = 8
        widths = {"block_rows": NX * ROW, "block_t": 2 * P, "w1_now": 2 * FF, "hidden_t": 2 * FF,
                  "b1_now": 2 * FCH, "z_now": 2 * D, "out_rows": 2 * D}
        starts, begin = {}, 0
        for name, width in widths.items():
            starts[name] = begin
            begin += width

        def over_probs(name, count):
            return probs_flat[:, starts[name]:starts[name] + widths[name]].rearrange("p (a x) -> p a x", a=count)

        block_rows, block_t = over_probs("block_rows", NX), over_probs("block_t", 2)
        w1_now, b1_now, hidden_t = over_probs("w1_now", 2), over_probs("b1_now", 2), over_probs("hidden_t", 2)
        z_now, out_rows = over_probs("z_now", 2), over_probs("out_rows", 2)
        turn_bank, hidden_bank, y_bank = st_bank[0:2], s_bank[0:2], [s_bank[2], st_bank[2]]
        out_flat = out.rearrange("b l d -> (b l) d")

        experts_loaded = sem("experts_loaded")
        tables_built = sem("tables_built")
        plan_step = sem("plan_step")
        padded = sem("padded")
        rows_loaded = [sem(f"rows_loaded{i}") for i in range(NX)]
        turned = sem("turned")
        turn_copied = sem("turn_copied")
        w1_copied = sem("w1_copied")
        b1_copied = sem("b1_copied")
        hidden_filled = sem("hidden_filled")
        gelu_done = sem("gelu_done")
        y_filled = sem("y_filled")
        z_ready = sem("z_ready")
        z_stats = sem("z_stats")
        z_aggr = sem("z_aggr")
        z_var = sem("z_var")
        z_rstd = sem("z_rstd")
        out_ready = sem("out_ready")
        out_stored = [sem(f"out_stored{i}") for i in range(2)]

        LAG = 3
        EARLY = NX
        assert EARLY <= ((BATCHES - 1) * L - EXPERTS * (P - 1)) // P
        EARLY_STEPS = EARLY - 1
        FILLING = {"proj": (0, 1), "x1T": (2,), "logits": (3,), "counts": (4, 5, 6)}
        PADDING = [0, 0, 0, 2, 4, 5, 6, 7, EXPERTS]

        def run_steps(eng, first, step):
            turns = (NBLK - 1 - first) // NX
            with eng.Fori(0, turns) as i:
                for r in range(NX):
                    step(i, first + r)
            for k in range(first + turns * NX, NBLK + LAG):
                step(0, k)

        def block_at(i, m, lag):
            number = i * NX + m - lag
            if isinstance(number, int) and not 0 <= number < NBLK:
                return None
            return number, (m - lag) % NX, i + (m - lag) // NX

        ORDER = [("q", 0, 0), ("sh", 0, 1), ("k", 0, 2), ("U", 0, 3),
                 ("U", 1, 0), ("sh", 1, 1), ("headsT", 1, 2), ("proj", 1, 3),
                 ("U", 2, 0), ("sh", 2, 1), ("v", 2, 2), ("x1T", 2, 3),
                 ("logits", 3, 0), ("sh", 3, 1), ("U", 3, 2), ("counts", 3, 3)]
        OLD = ("headsT", "proj", "x1T", "logits", "counts")

        CONSTS = 7
        TABLES = 7
        EARLY_PLAN, PLAN_STEPS = 18, 35
        LOOPED = 3

        def present(kind, n, b):
            if isinstance(b, int):
                if b == 0:
                    return kind not in OLD and not (kind == "U" and n < 2)
                if b == BATCHES - 1:
                    return kind not in ("q", "k", "v") and not (kind == "sh" and n == GROUPS - 1)
                if b == BATCHES:
                    return kind in OLD or (kind == "U" and n < 2)
            return True

        START = ["q", "v", "sh"]
        uses0 = sum(present(k, n, 0) for k, n, _ in ORDER)
        uses7 = sum(present(k, n, BATCHES - 1) for k, n, _ in ORDER)

        def misc_before(kind, n, b):
            at = sum(present(k, m, b) for k, m, s in ORDER[:[(k, m) for k, m, _ in ORDER].index((kind, n))])
            if isinstance(b, int) and b == 0:
                return len(START) + at
            if isinstance(b, int) and b == BATCHES:
                return len(START) + uses0 + len(ORDER) * (BATCHES - 2) + uses7 + at
            return len(START) + uses0 + len(ORDER) * (b - 1) + at

        def emptied(kind, n, b):
            return misc_before(kind, n, b) + 1

        def slot_of(n, s, b):
            for kind, m, t in ORDER:
                if (m, t) == (n, s) and present(kind, m, b):
                    return kind
            return None

        def run_batches(eng, body, tail):
            for b in range(LOOPED):
                body(b, b % 2, max(b - 1, 0) // 2)
            with eng.Fori((LOOPED - 1) // 2, (BATCHES - 2) // 2) as i:
                body(i * 2 + 1, 1, i)
                body(i * 2 + 2, 0, i)
            body(BATCHES - 1, 1, (BATCHES - 2) // 2)
            tail()

        def is_last(b):
            return isinstance(b, int) and b == BATCHES - 1

        def is_first(b):
            return isinstance(b, int) and b == 0

        def ahead(b, par, n, k):
            m = n + k
            if is_last(b) and m >= GROUPS:
                return None
            return (b + 1, 1 - par, m - GROUPS) if m >= GROUPS else (b, par, m)

        def behind(b, par, n, k):
            m = n - k
            if is_first(b) and m < 0:
                return None
            return (b - 1, 1 - par, m + GROUPS) if m < 0 else (b, par, m)

        def bank_of(banks, j, i):
            at = j * TILES + i
            return banks[1 if at == GR - 1 else at % 3], {0: 4, 1: 2, 2: 4, GR - 1: 2}.get(at, 3)

        q32, k32 = q_stack[:, :, :, :].bitcast(U32), k_stack[:, :, :, :].bitcast(U32)
        misc_h = misc[:, 0:TILES * P].rearrange("p (t g w) -> p t g w", t=TILES, g=GH)
        misc_bf = misc[:, 0:P].bitcast(BF16)
        misc_v = misc[:, 0:TILES * D].rearrange("p (t h c) -> p t h c", t=TILES, c=CH)
        misc_td = misc[:, 0:TILES * D].rearrange("p (t d) -> p t d", t=TILES)
        misc_counts = misc[:, 0:(TILES + 1) * EXPERTS].rearrange("p (t e) -> p t e", e=EXPERTS)
        misc_lg = misc[:, 0:TILES * EXPERTS].rearrange("p (t e) -> p t e", t=TILES)

        def stand_apart(eng):
            eng.sem_inc(register_waited, 1)

        block = ctx.enter_context(nc.Block())

        @block.sync
        def _(sp):
            def load_x(b, par):
                sp.dma_start(xt_in[:, par, :], x_t[b]).then_inc(xt_loaded, 16)
                sp.dma_start(x_in[:, par], x[b].rearrange("(t p) d -> p t d", p=P)).then_inc(x_loaded, 16)

            def store_part(b, par, part):
                sp.wait_ge((qk_hi, mid_ready, lo_ready)[part], b * 2 + 2)
                sp.dma_start(parts_dram[par, part:part + Q_PARTS + 1:Q_PARTS].rearrange("s c (h l) -> (c h) s l", l=L),
                             qk_parts[:, part]).then_inc(parts_stored[part], 16)
                if part < PARTS - 1:
                    sp.dma_start(parts_dram[par, PARTS + part].rearrange("c (h l) -> (c h) l", l=L),
                                 qk_parts[:, part, 0]).then_inc(parts_stored[part], 16)

            def fill_stacks(b, par, read):
                for part in range(PARTS):
                    sp.wait_ge(parts_stored[part], (b + 1) * (STORES[part] * 16))
                    stand_apart(sp)
                sp.wait_ge(st_filled, read)
                stand_apart(sp)
                halves = [(0, HEADS // 2, stack_loaded[0]), (HEADS // 2, HEADS, stack_loaded[1])]
                if is_first(b):
                    halves[0:1] = [(0, GH, group0_loaded), (GH, HEADS // 2, stack_loaded[0])]
                for begin, end, loaded in halves:
                    heads_of, columns = slice(begin, end), slice(begin * L, end * L)
                    k_parts = parts_dram[par, Q_PARTS:Q_PARTS + PARTS, :, columns].rearrange(
                        "(z a) c l -> z (a c) l", z=1).broadcast_to([PARTS, PARTS * CH, (end - begin) * L])
                    q_parts = bass.AP(tensor=parts_dram.tensor, offset=parts_dram[par, 0, :, columns].offset,
                                      ap=[[CH * HEADS * L, PARTS], [HEADS * L, PARTS * CH], [1, (end - begin) * L]])
                    for stack, source in ((k_stack, k_parts), (q_stack, q_parts)):
                        sp.dma_start(stack[0:CH * BLOCKS9, par, heads_of].rearrange("c h l -> c (h l)"),
                                     source).then_inc(loaded, 16)

            def load_shift(g, index):
                b, par, n = g
                sp.wait_ge(misc_emptied, index + 1)
                for a in range(PARTS):
                    sp.dma_start(
                        q_stack[SHIFT_ROW + a:SHIFT_ROW + a + 1, par, n * GH:(n + 1) * GH, :].rearrange(
                            "a h (t l) -> a (h t) l", t=TILES),
                        shift_t[a * GR:(a + 1) * GR, n % 2, :]).then_inc(shift_loaded, 16)

            sp.dma_start(wqkv[:, :], w_qkv_t).then_inc(qkv_loaded, 16)
            sp.dma_start(xt_in[:, 0, :], x_t[0]).then_inc(xt_loaded, 16)
            sp.dma_start(bqk[:, :], b_qkv[0:2 * D].rearrange("(a p) -> p a", p=P),
                         allow_slow_non_contiguous=True).then_inc(qkv_loaded, 16)
            sp.dma_start(bv[:, :], b_qkv[2 * D:3 * D].rearrange("(a d) -> a d", a=1).broadcast_to([P, D])
                         ).then_inc(consts_loaded, 16)
            sp.dma_start(x_in[:, 0], x[0].rearrange("(t p) d -> p t d", p=P)).then_inc(x_loaded, 16)
            sp.dma_start(wo[:, :], w_o_t).then_inc(consts_loaded, 16)
            sp.dma_start(bo[:, :], b_o.rearrange("(a d) -> a d", a=1).broadcast_to([P, D])
                         ).then_inc(consts_loaded, 16)
            sp.dma_start(gate[:, :], gate_w).then_inc(consts_loaded, 16)
            sp.wait_ge(stacks_cleared, 2)
            for part in range(PARTS):
                store_part(0, 0, part)
            fill_stacks(0, 0, 0)
            load_x(1, 1)
            load_shift((0, 0, 0), 2)

            def batch(b, par, pairs):
                def turned_shift(n):
                    if ahead(b, par, n, 1):
                        load_shift(ahead(b, par, n, 1), misc_before("sh", n, b))

                if not is_last(b):
                    if not is_first(b):
                        sp.wait_ge(st_filled, b * (GROUPS * GR) - GR)
                        stand_apart(sp)
                        sp.wait_ge(x2b_ready, b * 2)
                        load_x(b + 1, 1 - par)
                    if is_first(b):
                        sp.wait_ge(stacks1_cleared, 2)
                    else:
                        for half in range(2):
                            sp.wait_ge(stack_loaded[half], b * (STACK_LOADS * 16))
                turned_shift(0)
                if not is_last(b):
                    for part in range(PARTS):
                        store_part(b + 1, 1 - par, part)
                    fill_stacks(b + 1, 1 - par, b * (GROUPS * GR))
                for n in range(1, GROUPS):
                    turned_shift(n)

            def tail():
                sp.dma_start(b2_row[:, :, :], b2.rearrange("(a e) d -> a e d", a=1)).then_inc(experts_loaded, 16)
                sp.dma_start(b1_t[:, :, :], b1.rearrange("e (c p) -> p e c", p=P), allow_slow_non_contiguous=True
                             ).then_inc(experts_loaded, 16)
                sp.wait_ge(st_filled, (BATCHES - 1) * GROUPS * GR)
                sp.dma_start(w1_all, w1.rearrange("e d f -> d e f")).then_inc(experts_loaded, 16)
                sp.dma_start(w2_all, w2.rearrange("e (c f) d -> f e c d", f=P)).then_inc(experts_loaded, 16)
                sp.wait_ge(tables_built, TABLES)
                sp.dma_start(scratch[EXPERTS * REGION:SCRATCH_ROWS].rearrange("(a p) r -> p a r", p=P),
                             pad_rows[:, :].rearrange("p (a r) -> p a r", a=1).broadcast_to([P, EXPERTS, ROW])
                             ).then_inc(padded, 16)
                for par in range(2):
                    sp.wait_ge(scattered[par], (BATCHES - 1 + 1 - par) // 2 * TILES * 16)
                sp.wait_ge(plan_step, EARLY_PLAN)
                sp.wait_ge(pv_done, BATCHES * GROUPS)

                def step(i, m):
                    if block_at(i, m, 0) is None:
                        return
                    k, buf, turn = block_at(i, m, 0)
                    if not (isinstance(k, int) and k < NX):
                        sp.wait_ge(out_stored[buf % 2], ((turn - 1) * (NX // 2) + buf // 2 + 1) * 16)
                    row = sp.value_load(row_of[0:1, k:k + 1] if isinstance(k, int) else row_of[0:1, bass.ds(k, 1)],
                                        min_val=0, max_val=SCRATCH_ROWS - P)
                    sp.dma_start(block_rows[:, buf], scratch[bass.ds(row, P), :]).then_inc(rows_loaded[buf], 16)

                for k in range(EARLY):
                    step(0, k)
                    for e in range(PADDING[k], PADDING[k + 1]):
                        end = sp.value_load(region_end[0:1, e:e + 1], min_val=0, max_val=EXPERTS * REGION)
                        sp.dma_start(scratch[bass.ds(end, L + P), :].rearrange("(a p) r -> p a r", p=P),
                                     pad_rows[:, :].rearrange("p (a r) -> p a r", a=1).broadcast_to(
                                         [P, TILES + 1, ROW])).then_inc(padded, 16)
                for par in range(2):
                    sp.wait_ge(scattered[par], BATCHES // 2 * TILES * 16)
                sp.wait_ge(plan_step, PLAN_STEPS)
                run_steps(sp, EARLY, step)

            run_batches(sp, batch, tail)

        @block.tensor
        def _(pe):
            def fill_misc(index):
                pe.wait_ge(misc_emptied, index)

            def project_qk(side, par):
                nc.tensor.matmul(misc[:, 0:L], wqkv[:, side * D:(side + 1) * D], xt_in[:, par, :],
                                 start=True, stop=True).then_inc(misc_filled, 1)

            def count():
                last = TILES * EXPERTS
                oh = one_hot[:, :, :].rearrange("p t e -> p (t e)")
                nc.tensor.matmul(misc[:, last:last + EXPERTS], ones_bf[:, :], oh[:, last - EXPERTS:last],
                                 start=True, stop=False)
                nc.tensor.matmul(misc[:, 0:last], before[:, :], oh, start=False, stop=False)
                for later in range(1, TILES + 1):
                    width = min(TILES - 1, TILES + 1 - later) * EXPERTS
                    mm = nc.tensor.matmul(misc[:, later * EXPERTS:later * EXPERTS + width], ones_bf[:, :],
                                          oh[:, 0:width], start=False, stop=(later == TILES))
                mm.then_inc(misc_filled, 1)

            def project_v(par):
                for t in range(TILES):
                    mm = nc.tensor.matmul(misc[:, t * D:(t + 1) * D], xt_in[:, par, t * P:(t + 1) * P],
                                          wqkv[:, 2 * D:3 * D], start=True, stop=True)
                mm.then_inc(misc_filled, 1)

            def turn_shift():
                nc.tensor.transpose(misc_bf[0:PARTS * GR, 0:P],
                                    shift[:, :, :].rearrange("p a g -> p (a g)"),
                                    ident_bf[:, :]).then_inc(misc_filled, 1)

            def scores(b, par, n, j, i):
                h = n * GH + j
                number = (b * GROUPS + n) * GR + j * TILES + i
                bank, last = bank_of(s_bank, j, i)
                if not (isinstance(number, int) and number < last):
                    pe.wait_ge(s_reduced, number - last + 1)
                nc.tensor.matmul(bank[:, :], q_stack[0:ROWS_S, par, h, i * P:(i + 1) * P],
                                 k_stack[0:ROWS_S, par, h, :], start=True, stop=True).then_inc(s_filled, 1)

            def scores_t(b, par, n, j, i):
                h = n * GH + j
                number = (b * GROUPS + n) * GR + j * TILES + i
                bank, last = bank_of(st_bank, j, i)
                if not (isinstance(number, int) and number < last):
                    pe.wait_ge(exp_done, number - last + 1)
                nc.tensor.matmul(bank[:, :], k_stack[:, par, h, i * P:(i + 1) * P],
                                 q_stack[:, par, h, :], start=True, stop=True).then_inc(st_filled, 1)

            def probs_v(b, par, n, i, buf):
                for j in range(GH):
                    mm = nc.tensor.matmul(pv_bank[VW * j:VW * (j + 1), :], v_stack[:, par, i, n * GH + j, :],
                                          probs[:, buf, j, i, :], start=(i == 0), stop=(i == TILES - 1))
                if i == TILES - 1:
                    mm.then_inc(pv_done, 1)

            def misc_work(kind, b, par, n):
                if kind is None:
                    return
                fill_misc(misc_before(kind, n, b))
                if kind == "U":
                    g = behind(b, par, n, 2) if not (isinstance(b, int) and b == BATCHES) else (b - 1, 1 - par, n + 2)
                    pe.wait_ge(pv_copied, g[0] * GROUPS + g[2] + 1)
                    for t in range(TILES):
                        mm = nc.tensor.transpose(misc[:, t * P:(t + 1) * P],
                                                 pv_copy[:, g[2] % 2, t * P:(t + 1) * P], ident[:, :])
                    mm.then_inc(misc_filled, 1)
                elif kind == "sh":
                    pe.wait_ge(shift_step, (b * GROUPS + n + 2) * 4)
                    stand_apart(pe)
                    turn_shift()
                elif kind in ("q", "k"):
                    if kind == "q":
                        pe.wait_ge(xt_loaded, (b + 2) * 16)
                    project_qk(int(kind == "k"), 1 - par)
                elif kind == "v":
                    project_v(1 - par)
                elif kind == "headsT":
                    for t in range(TILES):
                        mm = nc.tensor.transpose(misc[:, t * P:(t + 1) * P], heads[:, t, :], ident[:, :])
                    mm.then_inc(misc_filled, 1)
                elif kind == "proj":
                    for t in range(TILES):
                        mm = nc.tensor.matmul(misc[:, t * D:(t + 1) * D], heads_t[:, t * P:(t + 1) * P],
                                              wo[:, :], start=True, stop=True)
                    mm.then_inc(misc_filled, 1)
                elif kind == "x1T":
                    pe.wait_ge(x1_ready, b * TILES)
                    for t in range(TILES):
                        mm = nc.tensor.transpose(misc[:, t * P:(t + 1) * P], rows[:, 1 - par, t, 0:D], ident[:, :])
                    mm.then_inc(misc_filled, 1)
                elif kind == "logits":
                    for t in range(TILES):
                        mm = nc.tensor.matmul(misc[:, t * EXPERTS:(t + 1) * EXPERTS],
                                              x1_t[:, t * P:(t + 1) * P], gate[:, :], start=True, stop=True)
                    mm.then_inc(misc_filled, 1)
                elif kind == "counts":
                    pe.wait_ge(onehot_ready, b)
                    count()

            pe.wait_ge(xt_loaded, 16)
            pe.wait_ge(qkv_loaded, 2 * 16)
            project_qk(0, 0)
            nc.tensor.matmul(s_bank[0][:, :], wqkv[:, D:2 * D], xt_in[:, 0, :],
                             start=True, stop=True).then_inc(k0_projected, 1)
            fill_misc(1)
            project_v(0)
            pe.wait_ge(k0_rest, 1)
            for n in range(2):
                pe.wait_ge((group0_loaded, stack_loaded[0])[n], STACK_LOADS * 16)
                for j in range(GH):
                    for i in range(TILES):
                        scores(0, 0, n, j, i)
                if n == 0:
                    fill_misc(2)
                    pe.wait_ge(consts_built, CONSTS)
                    pe.wait_ge(shift_step, 4)
                    turn_shift()
            pe.wait_ge(stack_loaded[1], STACK_LOADS * 16)
            scores(0, 0, 2, 0, 0)
            pe.wait_ge(consts_loaded, 4 * 16)

            def batch(b, par, pairs):
                for n in range(GROUPS):
                    maxing, multiplying = ahead(b, par, n, 2), behind(b, par, n, 1)
                    pe.wait_ge(shift_loaded, (b * GROUPS + n + 1) * (PARTS * 16))
                    for j in range(GH):
                        for i in range(TILES):
                            scores_t(b, par, n, j, i)
                            if maxing and i < TILES - 1:
                                scores(*maxing, j, i + 1)
                            if i == 1:
                                misc_work(slot_of(n, j, b), b, par, n)
                        following = maxing if j < GH - 1 else ahead(b, par, n, 3)
                        if following:
                            if j == GH - 1 and n % 2 == 1:
                                half = n // 2
                                pe.wait_ge(stack_loaded[half], (b + 2) * (STACK_LOADS * 16))
                            scores(*following, (j + 1) % GH, 0)
                        if multiplying:
                            if j == 0:
                                pe.wait_ge(exp_done, (b * GROUPS + n) * GR)
                                if behind(b, par, n, 2):
                                    pe.wait_ge(pv_copied, b * GROUPS + n - 1)
                            probs_v(*multiplying, j, (n - 1) % 2)

            def tail():
                b = BATCHES
                misc_work("U", b, 0, 0)
                pe.wait_ge(exp_done, b * GROUPS * GR)
                pe.wait_ge(pv_copied, b * GROUPS - 1)
                for i in range(TILES):
                    probs_v(b - 1, 1, GROUPS - 1, i, (GROUPS - 1) % 2)

                def step(i, m):
                    if block_at(i, m, 2):
                        k, _, _ = block_at(i, m, 2)
                        par = m % 2
                        if isinstance(k, int) and k == 0:
                            pe.wait_ge(experts_loaded, 4 * 16)
                        e = pe.value_load(expert_of[0:1, k:k + 1] if isinstance(k, int)
                                          else expert_of[0:1, bass.ds(k, 1)], min_val=0, max_val=EXPERTS - 1)
                        pe.wait_ge(gelu_done, k + 1)
                        if not (isinstance(k, int) and k < 2):
                            pe.wait_ge(z_ready, k - 1)
                        nc.tensor.matmul(y_bank[par][:, 0:D], ones[0:1, :],
                                         b2_row[:, bass.ds(e, 1), :].rearrange("p a d -> p (a d)"),
                                         start=True, stop=False)
                        for c in range(FCH):
                            mm = nc.tensor.matmul(y_bank[par][:, 0:D], hidden_t[:, par, c * P:(c + 1) * P],
                                                  w2_all[:, bass.ds(e, 1), c, :].rearrange("p a d -> p (a d)"),
                                                  start=False, stop=(c == FCH - 1))
                        mm.then_inc(y_filled, 1)
                    for at in ([block_at(i, m, 0)] if isinstance(i, int) and i * NX + m == 0 else []) + [
                            block_at(i, m, -1)]:
                        if at is None:
                            continue
                        k, buf, turn = at
                        pe.wait_ge(rows_loaded[buf], (turn + 1) * 16)
                        if not (isinstance(k, int) and k < 2):
                            pe.wait_ge(turn_copied, k - 1)
                        nc.tensor.transpose(turn_bank[buf % 2][:, 0:P], block_rows[:, buf, 0:D], ident[:, :]
                                            ).then_inc(turned, 1)
                    if block_at(i, m, 0):
                        k, buf, _ = block_at(i, m, 0)
                        par = m % 2
                        pe.wait_ge(turn_copied, k + 1)
                        pe.wait_ge(w1_copied, k + 1)
                        if not (isinstance(k, int) and k < 2):
                            pe.wait_ge(gelu_done, k - 1)
                        for c in range(FCH):
                            mm = nc.tensor.matmul(hidden_bank[par][:, c * P:(c + 1) * P],
                                                  w1_now[:, par, c * P:(c + 1) * P], block_t[:, par, :],
                                                  start=True, stop=True)
                        mm.then_inc(hidden_filled, 1)

                for kind, n, _ in ORDER:
                    if present(kind, n, b) and (kind, n) != ("U", 0):
                        misc_work(kind, b, 0, n)
                        if kind == "proj":
                            pe.wait_ge(plan_step, EARLY_PLAN)
                            pe.wait_ge(exp_done, BATCHES * GROUPS * GR)
                            pe.wait_ge(s_reduced, BATCHES * GROUPS * GR)
                        for k in FILLING.get(kind, ()):
                            step(0, k)
                pe.wait_ge(plan_step, PLAN_STEPS)
                run_steps(pe, EARLY_STEPS, step)

            run_batches(pe, batch, tail)

        @block.scalar
        def _(act):
            def lead(b, side):
                if is_first(b):
                    act.wait_ge(*((misc_filled, 1), (k0_projected, 1))[side])
                else:
                    act.wait_ge(misc_filled, emptied("qk"[side], 0, b - 1))
                    for part in range(PARTS):
                        act.wait_ge(parts_stored[part], b * (STORES[part] * 16))
                source = s_bank[0] if is_first(b) and side else misc
                nc.scalar.activation(qk_parts[:, 0, side, :], source[:, 0:L], ACT.Identity,
                                     bias=bqk[:, side:side + 1]).then_inc(qk_hi, 1)

            def middle(b, side):
                if is_first(b):
                    act.wait_ge(*((misc_emptied, 1), (k0_rest, 1))[side])
                else:
                    act.wait_ge(misc_emptied, emptied("qk"[side], 0, b - 1))
                nc.scalar.activation(qk_parts[:, 1, side, :], qk_rest[:, side, :], ACT.Copy).then_inc(mid_ready, 1)

            def copy_shift(g, index):
                b, par, n = g
                number = b * GROUPS + n
                act.wait_ge(misc_filled, index + 1)
                if not (is_first(b) and n < 2):
                    act.wait_ge(shift_loaded, (number - 1) * (PARTS * 16))
                nc.scalar.activation(shift_t[:, n % 2, :], misc_bf[0:PARTS * GR, 0:P], ACT.Copy
                                     ).then_inc(misc_emptied, 1)

            def copy_pv(g):
                b, par, n = g
                act.wait_ge(pv_done, b * GROUPS + n + 1)
                nc.scalar.activation(pv_copy[:, n % 2, :], pv_bank[:, :], ACT.Copy).then_inc(pv_copied, 1)

            def exps(b, par, n, j, i):
                number = (b * GROUPS + n) * GR + j * TILES + i
                act.wait_ge(st_filled, number + 1)
                if j == 0 and i == 0 and behind(b, par, n, 2):
                    act.wait_ge(pv_done, b * GROUPS + n - 1)
                nc.scalar.activation(probs[:, n % 2, j, i, :], bank_of(st_bank, j, i)[0][:, :],
                                     ACT.Exp, scale=SCALE).then_inc(exp_done, 1)

            def misc_copy(kind, b, par, n):
                if kind not in ("sh", "headsT", "x1T", "logits"):
                    return
                index = misc_before(kind, n, b)
                if kind == "sh":
                    copy_shift(ahead(b, par, n, 1), index)
                else:
                    target, source = {
                        "headsT": (heads_t[:, :], misc[:, 0:L]),
                        "x1T": (x1_t[:, :], misc[:, 0:L]),
                        "logits": (logits[:, :, :], misc_lg)}[kind]
                    act.wait_ge(misc_filled, index + 1)
                    if kind == "logits" and not (isinstance(b, int) and b == 1):
                        act.wait_ge(below_ready, b - 1)
                    nc.scalar.activation(target, source, ACT.Copy).then_inc(misc_emptied, 1)

            def router_exp(b):
                act.wait_ge(below_ready, b)
                if not (isinstance(b, int) and b == 1):
                    act.wait_ge(sum_ready, b - 1)
                nc.scalar.activation(prob[:, :, :], below[:, :, :], ACT.Exp).then_inc(prob_ready, 1)

            act.wait_ge(tables_warm, 1)
            nc.scalar.activation(warm[:, :], warm[:, :], ACT.Exp).then_inc(tables_warm, 1)
            act.wait_ge(qkv_loaded, 2 * 16)
            for side in range(2):
                lead(0, side)
            for side in range(2):
                middle(0, side)
            copy_shift((0, 0, 0), 2)

            def batch(b, par, pairs):
                for n in range(GROUPS):
                    if behind(b, par, n, 2):
                        copy_pv(behind(b, par, n, 2))
                    for j in range(GH):
                        for i in range(TILES):
                            exps(b, par, n, j, i)
                            at = (n, j, i)
                            if not is_last(b):
                                if at in ((0, 0, 2), (0, 2, 2)):
                                    lead(b + 1, j // 2)
                                elif at in ((0, 1, 2), (0, 3, 2)):
                                    middle(b + 1, j // 2)
                            if at == (3, 2, 2) and not is_first(b):
                                router_exp(b)
                        misc_copy(slot_of(n, j, b), b, par, n)

            def tail():
                b = BATCHES
                copy_pv((b - 1, 1, GROUPS - 2))
                copy_pv((b - 1, 1, GROUPS - 1))
                def copy_turned(k, par):
                    act.wait_ge(turned, k + 1)
                    if not (isinstance(k, int) and k < 2):
                        act.wait_ge(hidden_filled, k - 1)
                    nc.scalar.activation(block_t[:, par, :], turn_bank[par][:, 0:P], ACT.Copy
                                         ).then_inc(turn_copied, 1)

                def copy_w1(k, par):
                    e = act.value_load(expert_of[0:1, k:k + 1] if isinstance(k, int)
                                       else expert_of[0:1, bass.ds(k, 1)], min_val=0, max_val=EXPERTS - 1)
                    if not (isinstance(k, int) and k < 2):
                        act.wait_ge(gelu_done, k - 1)
                    nc.scalar.activation(b1_now[:, par, :], b1_t[:, bass.ds(e, 1), :].rearrange("p a c -> p (a c)"),
                                         ACT.Copy).then_inc(b1_copied, 1)
                    nc.scalar.activation(w1_now[:, par, :], w1_all[:, bass.ds(e, 1), :].rearrange("p a f -> p (a f)"),
                                         ACT.Copy).then_inc(w1_copied, 1)

                def step(i, m):
                    par = m % 2
                    if isinstance(i, int) and i * NX + m == 0:
                        copy_w1(0, 0)
                        copy_turned(0, 0)
                    if block_at(i, m, -1):
                        k, _, _ = block_at(i, m, -1)
                        copy_w1(k, 1 - par)
                        copy_turned(k, 1 - par)
                    if block_at(i, m, 0):
                        k, _, _ = block_at(i, m, 0)
                        act.wait_ge(b1_copied, k + 1)
                        act.wait_ge(hidden_filled, k + 1)
                        if not (isinstance(k, int) and k < 2):
                            act.wait_ge(y_filled, k - 1)
                        for c in range(FCH):
                            done = nc.scalar.activation(
                                hidden_t[:, par, c * P:(c + 1) * P], hidden_bank[par][:, c * P:(c + 1) * P],
                                ACT.Gelu, bias=b1_now[:, par, c:c + 1])
                        done.then_inc(gelu_done, 1)

                for kind, n, _ in ORDER:
                    if present(kind, n, b):
                        misc_copy(kind, b, 0, n)
                        if kind == "logits":
                            router_exp(b)
                        if kind == "proj":
                            act.wait_ge(plan_step, EARLY_PLAN)
                            act.wait_ge(experts_loaded, 4 * 16)
                        for k in FILLING.get(kind, ()):
                            step(0, k)
                act.wait_ge(plan_step, PLAN_STEPS)
                run_steps(act, EARLY_STEPS, step)

            run_batches(act, batch, tail)

        @block.vector
        def _(dve):
            def reduce(b, par, n, j, i):
                number = (b * GROUPS + n) * GR + j * TILES + i
                dve.wait_ge(s_filled, number + 1)
                if j == 0 and i == 0 and not (is_first(b) and n < 2):
                    dve.wait_ge(shift_step, (b * GROUPS + n - 1) * 4)
                nc.vector.reduce_max(maxima[:, n % 2, j * TILES + i:j * TILES + i + 1], bank_of(s_bank, j, i)[0][:, :],
                                     AXIS_X).then_inc(s_reduced, 1)

            def split_rest(b, side):
                dve.wait_ge(qk_hi, b * 2 + side + 1)
                if not is_first(b):
                    dve.wait_ge(lo_ready, b * 2)
                source = s_bank[0] if is_first(b) and side else misc
                nc.vector.scalar_tensor_tensor(
                    out=qk_rest[:, side, :], in0=source[:, 0:L], scalar=bqk[:, side:side + 1],
                    in1=qk_parts[:, 0, side, :], op0=ALU.add, op1=ALU.subtract
                    ).then_inc(k0_rest if is_first(b) and side else misc_emptied, 1)

            def split_last(side):
                dve.wait_ge(mid_ready, side + 1)
                nc.vector.tensor_tensor(qk_parts[:, 2, side, :], qk_rest[:, side, :], qk_parts[:, 1, side, :],
                                        ALU.subtract).then_inc(lo_ready, 1)

            def copy_v(b, par, index):
                dve.wait_ge(misc_filled, index + 1)
                if is_first(b):
                    dve.wait_ge(ones_col, 2)
                    dve.wait_ge(consts_loaded, 4 * 16)
                bias = bv[:, :].rearrange("p (a h c) -> p a h c", a=1, c=CH).broadcast_to([P, TILES, HEADS, CH])
                nc.vector.tensor_tensor(v_stack[:, par, :, :, 0:CH], misc_v, bias, ALU.add).then_inc(misc_emptied, 1)

            def invert(g, index):
                dve.wait_ge(misc_filled, index + 1)
                nc.vector.reciprocal(recip[:, :, :], misc_h[:, :, :, CH]).then_inc(recip_ready, 1)

            def normalise_heads(g):
                b, par, n = g
                dve.wait_ge(recip_ready, b * GROUPS + n + 1)
                over = recip[:, :, :].rearrange("p t (g a) -> p t g a", a=1).broadcast_to([P, TILES, GH, CH])
                nc.vector.tensor_tensor(
                    heads[:, :, n * GH * CH:(n + 1) * GH * CH].rearrange("p t (g c) -> p t g c", c=CH),
                    misc_h[:, :, :, 0:CH], over, ALU.mult).then_inc(misc_emptied, 1)

            def add_residual(b, par, index):
                dve.wait_ge(misc_filled, index + 1)
                dve.wait_ge(x2b_ready, b * 2)
                if not (isinstance(b, int) and b == 1):
                    dve.wait_ge(x1_ready, (b - 1) * TILES)
                nc.vector.tensor_tensor(resid[:, :, :], misc_td, x2b[:, 1 - par], ALU.add).then_inc(misc_emptied, 1)

            def statistics(b, t):
                if t == 0:
                    dve.wait_ge(misc_emptied, emptied("proj", 1, b))
                nc.vector.bn_stats(stats[:, t, :], resid[:, t, :]).then_inc(stats_ready, 1)

            def aggregate(b, t):
                if t == 0:
                    dve.wait_ge(stats_ready, b * TILES)
                    if not (isinstance(b, int) and b == 1):
                        dve.wait_ge(x1_ready, (b - 1) * TILES)
                    stand_apart(dve)
                nc.vector.bn_aggr(mean_var[:, t, :], stats[:, t, :]).then_inc(aggr_ready, 1)

            def normalise(b, par, pairs, t):
                if t == 0:
                    dve.wait_ge(rstd_ready, b)
                    dve.wait_ge(scattered[1 - par], pairs * (TILES * 16))
                nc.vector.tensor_scalar(rows[:, 1 - par, t, 0:D], resid[:, t, :], mean_var[:, t, 0:1],
                                        rstd[:, t:t + 1], ALU.subtract, ALU.mult).then_inc(x1_ready, 1)

            def spread(ap):
                return ap.rearrange("p (t a) -> p t a", a=1).broadcast_to([P, TILES, EXPERTS])

            ROUTE_STEPS = 6

            def route(b, step):
                if step == 0:
                    dve.wait_ge(misc_emptied, emptied("logits", 3, b))
                    nc.vector.reduce_max(top[:, :], logits[:, :, :], AXIS_X).then_inc(top_ready, 1)
                elif step == 1:
                    dve.wait_ge(top_ready, b)
                    nc.vector.tensor_tensor(is_top[:, :, :], logits[:, :, :], spread(top[:, :]), ALU.is_equal
                                            ).then_inc(istop_ready, 1)
                elif step == 2:
                    dve.wait_ge(istop_ready, b)
                    nc.vector.scalar_tensor_tensor(out=key[:, :, :], in0=is_top[:, :, :], scalar=-float(EXPERTS),
                                                   in1=expert_no[:, :, :], op0=ALU.mult, op1=ALU.add
                                                   ).then_inc(key_ready, 1)
                elif step == 3:
                    dve.wait_ge(key_ready, b)
                    nc.vector.tensor_reduce(first[:, :], key[:, :, :], AXIS_X, ALU.min).then_inc(first_ready, 1)
                elif step == 4:
                    dve.wait_ge(first_ready, b)
                    if not (isinstance(b, int) and b == 1):
                        dve.wait_ge(place_own, b - 1)
                    nc.vector.tensor_tensor(one_hot[:, :, :], key[:, :, :], spread(first[:, :]), ALU.is_equal
                                            ).then_inc(onehot_ready, 1)
                elif step == 5:
                    if not (isinstance(b, int) and b == 1):
                        dve.wait_ge(prob_ready, b - 1)
                    nc.vector.tensor_tensor(below[:, :, :], logits[:, :, :], spread(top[:, :]), ALU.subtract
                                            ).then_inc(below_ready, 1)

            def count_on(b, par, step):
                if step == 0:
                    dve.wait_ge(misc_filled, emptied("counts", 3, b))
                    if isinstance(b, int) and b == 1:
                        dve.wait_ge(base_ready, 2)
                    else:
                        dve.wait_ge(place_summed, b - 1)
                    before_batch = base[:, par, :].rearrange("p (a e) -> p a e", a=1)
                    nc.vector.tensor_tensor(place[:, :, :], misc_counts[:, 0:TILES, :],
                                            before_batch.broadcast_to([P, TILES, EXPERTS]), ALU.add
                                            ).then_inc(placed, 1)
                    nc.vector.tensor_tensor(base[:, 1 - par, :], misc_counts[:, TILES, :], base[:, par, :],
                                            ALU.add).then_inc(misc_emptied, 1)
                elif step == 1:
                    dve.wait_ge(placed, b)
                    nc.vector.tensor_tensor(place[:, :, :], place[:, :, :], one_hot[:, :, :], ALU.mult
                                            ).then_inc(place_own, 1)
                else:
                    dve.wait_ge(place_own, b)
                    if not (isinstance(b, int) and b == 1):
                        dve.wait_ge(slot_ready, b - 1)
                    nc.vector.tensor_reduce(own_place[:, :], place[:, :, :], AXIS_X, ALU.add
                                            ).then_inc(place_summed, 1)

            def weigh(b, par, step):
                if step == 0:
                    dve.wait_ge(prob_ready, b)
                    if not (isinstance(b, int) and b == 1):
                        dve.wait_ge(weight_ready, b - 1)
                    nc.vector.tensor_reduce(prob_sum[:, :], prob[:, :, :], AXIS_X, ALU.add).then_inc(sum_ready, 1)
                else:
                    dve.wait_ge(sum_ready, b)
                    nc.vector.reciprocal(rows[:, 1 - par, :, D], prob_sum[:, :]).then_inc(weight_ready, 1)

            def misc_use(kind, b, par, n, step):
                if kind is None:
                    return
                index = misc_before(kind, n, b)
                if kind == "U":
                    g = behind(b, par, n, 2) if not (isinstance(b, int) and b == BATCHES) else (b - 1, 1 - par, n + 2)
                    (invert(g, index) if step == 0 else normalise_heads(g))
                elif kind in ("q", "k"):
                    if step == 1:
                        split_rest(b + 1, int(kind == "k"))
                elif kind == "counts":
                    count_on(b, par, step)
                elif step == 1:
                    return
                elif kind == "v":
                    copy_v(b + 1, 1 - par, index)
                elif kind == "proj":
                    add_residual(b, par, index)

            nc.vector.memset(q32[64:128, 0], 0).then_inc(stacks_cleared, 1)
            for side in range(2):
                split_rest(0, side)
            split_last(0)
            copy_v(0, 0, 1)
            split_last(1)
            for j in range(GH):
                for i in range(TILES):
                    reduce(0, 0, 0, j, i)
            for j in range(GH):
                for i in range(TILES):
                    reduce(0, 0, 1, j, i)
            reduce(0, 0, 2, 0, 0)

            def batch(b, par, pairs):
                for n in range(GROUPS):
                    maxing = ahead(b, par, n, 2)
                    for j in range(GH):
                        following = maxing if j < GH - 1 else ahead(b, par, n, 3)
                        for i in range(TILES):
                            if i < TILES - 1 and maxing:
                                reduce(*maxing, j, i + 1)
                            if i == TILES - 1 and following:
                                reduce(*following, (j + 1) % GH, 0)
                            if i >= 2:
                                misc_use(slot_of(n, j, b), b, par, n, i - 2)
                            if not is_first(b):
                                at = (n * GH + j) * TILES + i
                                begin, combining, routing = 2 * GH * TILES - 1, (2 * GH + 1) * TILES, (3 * GH + 1) * TILES
                                if begin <= at < begin + TILES // 2:
                                    for t in range(2):
                                        statistics(b, (at - begin) * 2 + t)
                                elif at == combining:
                                    for t in range(TILES):
                                        aggregate(b, t)
                                elif routing <= at < routing + ROUTE_STEPS:
                                    route(b, at - routing)
                                elif at in (GROUPS * GR - 3, GROUPS * GR - 2):
                                    weigh(b, par, at - (GROUPS * GR - 3))
                if not is_first(b):
                    count_on(b, par, 2)

            def tail():
                b = BATCHES
                plan_early()
                for kind, n, _ in ORDER:
                    if present(kind, n, b):
                        for step in range(2):
                            misc_use(kind, b, 0, n, step)
                        if kind == "proj":
                            for t in range(TILES):
                                statistics(b, t)
                            for t in range(TILES):
                                aggregate(b, t)
                            for t in range(TILES):
                                normalise(b, 0, (b - 1) // 2, t)
                        if kind == "logits":
                            for step in range(ROUTE_STEPS):
                                route(b, step)
                        if kind == "counts":
                            count_on(b, 0, 2)
                            for step in range(2):
                                weigh(b, 0, step)
                            plan_rest()
                        for k in FILLING.get(kind, ()):
                            expert_step(0, k)
                run_steps(dve, EARLY_STEPS, expert_step)

            planned = [0]

            def plan(instruction):
                planned[0] += 1
                instruction.then_inc(plan_step, 1)
                dve.wait_ge(plan_step, planned[0])

            def count_held(ends):
                plan(nc.vector.scalar_tensor_tensor(out=held[:, :], in0=expert_no[0:1, 0, :], scalar=-float(REGION),
                                                    in1=ends, op0=ALU.mult, op1=ALU.add))

            def count_blocks(tokens):
                plan(nc.vector.tensor_tensor(
                    begun[:, :, :], tokens.rearrange("p (e a) -> p e a", a=1).broadcast_to(
                        [1, EXPERTS, TOKENS // P]), full_at[:, :, :], ALU.is_gt))
                plan(nc.vector.tensor_reduce(blocks[:, :], begun[:, :, :], AXIS_X, ALU.add))

            def lay_out(first, count):
                def over_blocks(ap):
                    return ap.rearrange("p (a e) -> p a e", a=1).broadcast_to([1, count, EXPERTS])

                plan(nc.vector.tensor_tensor(
                    prior_blocks[:, :, :], prior[:, :, :], blocks[:, :].rearrange("p (a e) -> p a e", a=1
                                                                                  ).broadcast_to(
                        [1, EXPERTS + 1, EXPERTS]), ALU.mult))
                plan(nc.vector.tensor_reduce(block_begin[:, :], prior_blocks[:, :, :], AXIS_X, ALU.add))
                plan(nc.vector.tensor_tensor(offset[:, :], taken[:, :], block_begin[:, :], ALU.subtract))
                plan(nc.vector.scalar_tensor_tensor(out=first_row[:, :], in0=offset[:, :], scalar=float(P),
                                                    in1=region_row[:, :], op0=ALU.mult, op1=ALU.add))
                plan(nc.vector.tensor_tensor(jump[:, :], first_row[:, 1:], first_row[:, 0:EXPERTS], ALU.subtract))
                plan(nc.vector.tensor_tensor(passed[:, 0:count, :], block_no[:, 0:count, :],
                                             over_blocks(block_begin[:, 1:]), ALU.is_ge))
                plan(nc.vector.tensor_reduce(sums[:, 0, 0:count], passed[:, 0:count, :], AXIS_X, ALU.add))
                plan(nc.vector.tensor_scalar(expert_of[:, first:first + count], sums[:, 0, 0:count],
                                             float(EXPERTS - 1), None, ALU.min))
                plan(nc.vector.tensor_tensor(jumps[:, 0:count, :], passed[:, 0:count, :], over_blocks(jump[:, :]),
                                             ALU.mult))
                plan(nc.vector.tensor_reduce(sums[:, 1, 0:count], jumps[:, 0:count, :], AXIS_X, ALU.add))
                plan(nc.vector.scalar_tensor_tensor(out=sums[:, 1, 0:count], in0=block_no[:, 0:count, 0],
                                                    scalar=float(P), in1=sums[:, 1, 0:count], op0=ALU.mult,
                                                    op1=ALU.add))
                plan(nc.vector.tensor_scalar(row_of[:, first:first + count], sums[:, 1, 0:count],
                                             first_row[:, 0:1], None, ALU.add))

            def plan_early():
                dve.wait_ge(misc_emptied, emptied("counts", 3, BATCHES - 1))
                dve.wait_ge(tables_built, TABLES)
                ends = base[0:1, 0, :]
                plan(nc.vector.tensor_copy(region_end[:, :], ends))
                count_held(ends)
                plan(nc.vector.tensor_scalar(full[:, :], held[:, :], -float(P - 1), None, ALU.add))
                count_blocks(full[:, :])
                lay_out(0, EARLY)
                plan(nc.vector.tensor_scalar(cut_begin[:, :], block_begin[:, :], float(EARLY), None, ALU.min))
                assert planned[0] == EARLY_PLAN

            def plan_rest():
                plan(nc.vector.tensor_tensor(taken[:, 0:EXPERTS], cut_begin[:, 1:], cut_begin[:, 0:EXPERTS],
                                             ALU.subtract))
                dve.wait_ge(misc_emptied, emptied("counts", 3, BATCHES))
                count_held(base[0:1, 1, :])
                count_blocks(held[:, :])
                plan(nc.vector.tensor_tensor(blocks[:, :], blocks[:, :], taken[:, 0:EXPERTS], ALU.subtract))
                lay_out(EARLY, NBLK - EARLY)
                assert planned[0] == PLAN_STEPS, planned

            def expert_step(i, m):
                par = m % 2
                two, three = block_at(i, m, 2), block_at(i, m, 3)
                if two:
                    k, buf, turn = two
                    dve.wait_ge(rows_loaded[buf], (turn + 1) * 16)
                    if not (isinstance(k, int) and k < 2):
                        dve.wait_ge(out_ready, k - 1)
                    dve.wait_ge(y_filled, k + 1)
                    nc.vector.scalar_tensor_tensor(out=z_now[:, par, :], in0=y_bank[par][:, 0:D],
                                                   scalar=block_rows[:, buf, D:D + 1],
                                                   in1=block_rows[:, buf, 0:D], op0=ALU.mult, op1=ALU.add
                                                   ).then_inc(z_ready, 1)
                if three:
                    k, buf, turn = three
                    if not (isinstance(k, int) and k < 2):
                        dve.wait_ge(out_stored[1 - par], (turn * (NX // 2) + buf // 2) * 16)
                    dve.wait_ge(z_rstd, k + 1)
                    nc.vector.tensor_scalar(out_rows[:, 1 - par, :], z_now[:, 1 - par, :],
                                            out_mean_var[:, 1 - par, 0:1], out_rstd[:, 1 - par:2 - par],
                                            ALU.subtract, ALU.mult).then_inc(out_ready, 1)
                if two:
                    k, buf, turn = two
                    dve.wait_ge(z_ready, k + 1)
                    nc.vector.bn_stats(out_stats[:, par, :], z_now[:, par, :]).then_inc(z_stats, 1)
                    dve.wait_ge(z_stats, k + 1)
                    stand_apart(dve)
                    nc.vector.bn_aggr(out_mean_var[:, par, :], out_stats[:, par, :]).then_inc(z_aggr, 1)
                    dve.wait_ge(z_aggr, k + 1)
                    nc.vector.tensor_scalar(out_var[:, par:par + 1], out_mean_var[:, par, 1:2], EPS, None, ALU.add
                                            ).then_inc(z_var, 1)

            run_batches(dve, batch, tail)

        @block.gpsimd
        def _(pool):
            nc.gpsimd.memset(warm[:, :], 0.0).then_inc(tables_warm, 1)
            nc.gpsimd.memset(v_stack[:, 0], 0.0).then_inc(ones_col, 1)
            pool.wait_ge(ones_col, 1)
            nc.gpsimd.memset(v_stack[:, 0, :, :, CH:CH + 1], 1.0).then_inc(ones_col, 1)
            pool.wait_ge(ones_col, 2)
            nc.gpsimd.memset(k32[64:128, 0], MINUS_ONES_BF16).then_inc(stacks_cleared, 1)
            pool.wait_ge(stacks_cleared, 2)

            def split_last(b, side):
                pool.wait_ge(mid_ready, b * 2 + side + 1)
                nc.gpsimd.tensor_tensor(qk_parts[:, 2, side, :], qk_rest[:, side, :], qk_parts[:, 1, side, :],
                                        ALU.subtract).then_inc(lo_ready, 1)

            nc.gpsimd.memset(ones[:, :], 1.0).then_inc(base_ready, 1)
            pool.wait_ge(base_ready, 1)
            nc.gpsimd.affine_select(out=ident[:, :], in_=ones[:, :], compare_op=ALU.is_equal, fill=0.0, base=0,
                                    pattern=[[-1, P]], channel_multiplier=1).then_inc(consts_built, 1)
            nc.gpsimd.affine_select(out=ident_bf[:, :], in_=ones[:, :], compare_op=ALU.is_equal, fill=0.0, base=0,
                                    pattern=[[-1, P]], channel_multiplier=1).then_inc(consts_built, 1)
            nc.gpsimd.affine_select(out=before[:, :], in_=ones[:, :], compare_op=ALU.is_gt, fill=0.0, base=0,
                                    pattern=[[1, P]], channel_multiplier=-1).then_inc(consts_built, 1)
            nc.gpsimd.iota(expert_no[:, :, :], pattern=[[0, TILES], [1, EXPERTS]], base=0, channel_multiplier=0,
                           allow_small_or_imprecise_dtypes=True).then_inc(consts_built, 1)
            nc.gpsimd.iota(token_no[:, :], pattern=[[P, TOKENS // P]], base=0, channel_multiplier=1
                           ).then_inc(consts_built, 1)
            nc.gpsimd.memset(minus_half[:, :], -0.5).then_inc(consts_built, 1)
            nc.gpsimd.memset(ones_bf[:, :], 1.0).then_inc(consts_built, 1)
            pool.wait_ge(consts_built, CONSTS)
            nc.gpsimd.memset(q32[64:128, 1], 0).then_inc(stacks1_cleared, 1)
            nc.gpsimd.memset(k32[64:128, 1], MINUS_ONES_BF16).then_inc(stacks1_cleared, 1)
            pool.wait_ge(stacks1_cleared, 2)
            nc.gpsimd.memset(v_stack[:, 1], 0.0).then_inc(ones_col, 1)
            pool.wait_ge(ones_col, 3)
            nc.gpsimd.memset(v_stack[:, 1, :, :, CH:CH + 1], 1.0).then_inc(ones_col, 1)
            nc.gpsimd.iota(base[:, 1, :], pattern=[[REGION, EXPERTS]], base=0, channel_multiplier=0,
                           allow_small_or_imprecise_dtypes=True).then_inc(base_ready, 1)
            nc.gpsimd.iota(block_no[:, :, :], pattern=[[1, NBLK], [0, EXPERTS]], base=0, channel_multiplier=0,
                           allow_small_or_imprecise_dtypes=True).then_inc(tables_built, 1)
            nc.gpsimd.iota(full_at[:, :, :], pattern=[[0, EXPERTS], [P, TOKENS // P]], base=0, channel_multiplier=0,
                           allow_small_or_imprecise_dtypes=True).then_inc(tables_built, 1)
            nc.gpsimd.affine_select(out=prior[:, :, :], in_=ones[0:1, 0:(EXPERTS + 1) * EXPERTS].rearrange(
                "p (e f) -> p e f", f=EXPERTS), compare_op=ALU.is_gt, fill=0.0, base=0,
                pattern=[[1, EXPERTS + 1], [-1, EXPERTS]], channel_multiplier=0).then_inc(tables_built, 1)
            nc.gpsimd.iota(region_row[:, :], pattern=[[REGION, EXPERTS + 1]], base=0, channel_multiplier=0,
                           allow_small_or_imprecise_dtypes=True).then_inc(tables_built, 1)
            nc.gpsimd.memset(taken[:, :], 0.0).then_inc(tables_built, 1)
            nc.gpsimd.memset(pad_rows[:, 0:D + 1], 0.0).then_inc(tables_built, 1)
            nc.gpsimd.iota(pad_rows[:, D + 1:D + 2].bitcast(U32), pattern=[[0, 1]], base=TOKENS, channel_multiplier=1
                           ).then_inc(tables_built, 1)
            pool.wait_ge(consts_loaded, 4 * 16)
            pool.wait_ge(consts_built, CONSTS)

            def place_rows(b, par):
                pool.wait_ge(place_summed, b)
                stand_apart(pool)
                nc.gpsimd.tensor_copy(slot[:, 1 - par, :], own_place[:, :]).then_inc(slot_ready, 1)

            def scatter(b, par):
                pool.wait_ge(slot_ready, b)
                pool.wait_ge(weight_ready, b)
                pool.wait_ge(x1_ready, b * TILES)
                pool.wait_ge(id_ready, b)
                stand_apart(pool)
                for t in range(TILES):
                    nc.gpsimd.indirect_dma_start(
                        scratch, bass.IndirectOffsetOnAxis(ap=slot[:, 1 - par, t:t + 1], axis=0),
                        rows[:, 1 - par, t, :], None).then_inc(scattered[1 - par], 16)

            def row_work(b, par, pairs):
                pool.wait_ge(aggr_ready, b * TILES)
                if not (isinstance(b, int) and b == 1):
                    pool.wait_ge(x1_ready, (b - 1) * TILES)
                stand_apart(pool)
                nc.gpsimd.tensor_scalar_add(var_eps[:, :], mean_var[:, :, 1], EPS).then_inc(vareps_ready, 1)
                pool.wait_ge(vareps_ready, b)
                nc.gpsimd.tensor_tensor(rstd[:, :], var_eps[:, :], minus_half[:, :], ALU.pow).then_inc(rstd_ready, 1)
                pool.wait_ge(scattered[1 - par], pairs * (TILES * 16))
                stand_apart(pool)
                numbers = (token_no[:, (b - 1) * TILES:b * TILES] if isinstance(b, int)
                           else token_no[:, bass.ds((b - 1) * TILES, TILES)])
                nc.gpsimd.tensor_copy(rows[:, 1 - par, :, :].bitcast(U32)[:, :, D + 1], numbers).then_inc(id_ready, 1)

            def normalise(b, par):
                pool.wait_ge(rstd_ready, b)
                stand_apart(pool)
                for t in range(TILES):
                    nc.gpsimd.tensor_scalar(rows[:, 1 - par, t, 0:D], resid[:, t, :], mean_var[:, t, 0:1],
                                            rstd[:, t:t + 1], ALU.subtract, ALU.mult).then_inc(x1_ready, 1)

            def split_shift(g, turned=None):
                b, par, n = g
                number = b * GROUPS + n
                pool.wait_ge(s_reduced, (number + 1) * GR)
                if turned is not None:
                    pool.wait_ge(misc_filled, turned)
                stand_apart(pool)
                nc.gpsimd.tensor_copy(shift[:, 0, :], maxima[:, n % 2, :]).then_inc(shift_step, 1)
                pool.wait_ge(shift_step, number * 4 + 1)
                nc.gpsimd.tensor_tensor(shift_rest[:, :], maxima[:, n % 2, :], shift[:, 0, :], ALU.subtract
                                        ).then_inc(shift_step, 1)
                pool.wait_ge(shift_step, number * 4 + 2)
                stand_apart(pool)
                nc.gpsimd.tensor_copy(shift[:, 1, :], shift_rest[:, :]).then_inc(shift_step, 1)
                pool.wait_ge(shift_step, number * 4 + 3)
                nc.gpsimd.tensor_tensor(shift[:, 2, :], shift_rest[:, :], shift[:, 1, :], ALU.subtract
                                        ).then_inc(shift_step, 1)

            def next_shift(b, par, n):
                if ahead(b, par, n, 1):
                    turned = len(START) if is_first(b) and n == 0 else (
                        misc_before("q", 0, b) if n == 0 else emptied("sh", n - 1, b))
                    split_shift(ahead(b, par, n, 1), turned)

            def double_x(b, par):
                pool.wait_ge(x_loaded, (b + 1) * 16)
                if not is_first(b):
                    pool.wait_ge(misc_emptied, misc_before("q", 0, b))
                bias = bo[:, :].rearrange("p (a d) -> p a d", a=1).broadcast_to([P, TILES, D])
                nc.gpsimd.tensor_tensor(x2b[:, par], x_in[:, par], bias, ALU.add).then_inc(x2b_ready, 1)
                pool.wait_ge(x2b_ready, b * 2 + 1)
                nc.gpsimd.tensor_tensor(x2b[:, par], x2b[:, par], x_in[:, par], ALU.add).then_inc(x2b_ready, 1)

            split_shift((0, 0, 0))

            def batch(b, par, pairs):
                next_shift(b, par, 0)
                if not (isinstance(b, int) and b < 2):
                    place_rows(b - 1, 1 - par)
                    scatter(b - 1, 1 - par)
                if not is_last(b):
                    split_last(b + 1, 0)
                double_x(b, par)
                if not is_last(b):
                    split_last(b + 1, 1)
                next_shift(b, par, 1)
                next_shift(b, par, 2)
                if not is_first(b):
                    row_work(b, par, pairs)
                    normalise(b, par)
                next_shift(b, par, 3)

            def tail():
                place_rows(BATCHES - 1, 1)
                scatter(BATCHES - 1, 1)
                row_work(BATCHES, 0, (BATCHES - 1) // 2)

                def step(i, m):
                    par = m % 2
                    if block_at(i, m, 1):
                        k, buf, _ = block_at(i, m, 1)
                        pool.wait_ge(out_ready, k + 1)
                        stand_apart(pool)
                        nc.gpsimd.indirect_dma_start(
                            out_flat, bass.IndirectOffsetOnAxis(
                                ap=block_rows[:, buf, D + 1:D + 2].bitcast(U32), axis=0),
                            out_rows[:, 1 - par, :], None, bounds_check=TOKENS - 1, oob_is_err=False
                            ).then_inc(out_stored[1 - par], 16)
                    if block_at(i, m, 0):
                        k, _, _ = block_at(i, m, 0)
                        pool.wait_ge(z_var, k + 1)
                        if not (isinstance(k, int) and k < 2):
                            pool.wait_ge(out_ready, k - 1)
                        stand_apart(pool)
                        nc.gpsimd.tensor_tensor(out_rstd[:, par:par + 1], out_var[:, par:par + 1], minus_half[:, 0:1],
                                                ALU.pow).then_inc(z_rstd, 1)

                for kind in FILLING:
                    if kind == "counts":
                        place_rows(BATCHES, 0)
                        pool.wait_ge(padded, (EXPERTS + 1) * 16)
                        scatter(BATCHES, 0)
                    for k in FILLING[kind]:
                        if k >= 2:
                            step(0, k - 2)
                run_steps(pool, EARLY_STEPS - 2, step)
                for par in range(2):
                    pool.wait_ge(out_stored[par], (NBLK + 1 - par) // 2 * 16)

            run_batches(pool, batch, tail)


def kernel(**inputs):
    import numpy as _np
    import concourse.bacc as _bacc
    from concourse import mybir as _mybir
    from concourse.bass_utils import run_bass_kernel_spmd as _run

    given = {name[3:].split("_", 1)[1]: _np.asarray(a) for name, a in inputs.items()}
    x, w_qkv, b_qkv = given["x"], given["w_qkv"], given["b_qkv"]
    D = x.shape[-1]
    HEADS = 16
    order = _np.arange(D).reshape(HEADS, D // HEADS).T.reshape(-1)
    order = _np.concatenate([order, D + order, _np.arange(2 * D, 3 * D)])
    arrays = {"x": x, "x_t": x.transpose(0, 2, 1), "w_qkv_t": w_qkv[order].T, "b_qkv": b_qkv[order],
              "w_o_t": given["w_o"].T, "b_o": given["b_o"], "gate_w": given["gate_w"],
              "w1": given["w1"], "b1": given["b1"], "w2": given["w2"], "b2": given["b2"]}

    nc = _bacc.Bacc("TRN2", target_bir_lowering=False, num_devices=1)
    args = []
    for name in list(arrays):
        a = _np.ascontiguousarray(arrays.pop(name))
        arrays[f"in_{name}_dram"] = a
        args.append(nc.dram_tensor(f"in_{name}_dram", a.shape, _mybir.dt.from_np(a.dtype), kind="ExternalInput").ap())
    args.append(nc.dram_tensor("out_dram", x.shape, _mybir.dt.float32, kind="ExternalOutput").ap())
    build(nc, *args)
    r = _run(nc, [arrays], core_ids=[0])
    return r.results[0]["out_dram"]
```
